# Optimizing a Trainium2 kernel written in Bass

```python
import numpy as np
import jax
import jax.numpy as jnp

def _softmax(x, axis=-1):
    return jax.nn.softmax(x, axis=axis)

def _gelu(x):
    return jax.nn.gelu(x, approximate=True)

def _silu(x):
    return jax.nn.silu(x)

def _sigmoid(x):
    return jax.nn.sigmoid(x)

def _layernorm(x, axis=-1, eps=1e-05):
    m = jnp.mean(x, axis=axis, keepdims=True)
    v = jnp.var(x, axis=axis, keepdims=True)
    return (x - m) / jnp.sqrt(v + eps)

def _scatter_add(tgt, idx, src, axis=0):
    return tgt.at[idx].add(src)

def _segment_sum(src, seg, n):
    return jax.ops.segment_sum(src, seg, n)
kernel_name = 'mk_hybrid_d1_jaxref_r4_fc103e'

def setup_inputs(seed: int=0):
    np.random.seed(seed)
    _w = jnp.asarray

    def _L0_attn_a_setup():
        import math
        import jax, jax.numpy as jnp
        import numpy as np
        N_HEAD = 16
        N_CLUSTER = 64
        GROUP_SIZE = 64

        def _sinusoidal(n, d):
            pos = jnp.arange(n, dtype=jnp.float32)[:, None]
            div = jnp.exp(jnp.arange(0, d, 2, dtype=jnp.float32) * (-math.log(10000.0) / d))
            ang = pos * div
            return jnp.stack([jnp.sin(ang), jnp.cos(ang)], axis=-1).reshape(n, d)

        def _rotary(pe, x):
            d = x.shape[-1]
            sin, cos = (pe[..., :d // 2], pe[..., d // 2:])
            x_even, x_odd = (x[..., ::2], x[..., 1::2])
            out = jnp.stack([-x_odd * cos, x_even * sin], axis=-1)
            return out.reshape(jnp.broadcast_shapes(x.shape[:-1] + (d // 2,), out.shape[:-1]) + (2,)).reshape(x.shape) if False else jnp.broadcast_to(out, x.shape[:-1] + (d // 2, 2)).reshape(x.shape)

        def _forward(x, w_attn, b_attn, w_proj, b_proj, w_assign):
            B, T, C = x.shape
            H, nc, gs = (N_HEAD, N_CLUSTER, GROUP_SIZE)
            hd = C // H
            ntpc = T // nc
            G = T // gs
            ncpg = gs // ntpc
            c_max = (G - 1) * ncpg
            qkv = x @ w_attn.T + b_attn
            q, k, v = jnp.split(qkv, 3, axis=-1)
            x_r = x.reshape(B, nc, ntpc, C)
            logits = jnp.einsum('bctd,cd->bct', x_r, w_assign)
            w = jax.nn.softmax(logits, axis=-1)
            ck = jnp.einsum('bct,bctd->bcd', w, k.reshape(B, nc, ntpc, C))
            cv = jnp.einsum('bct,bctd->bcd', w, v.reshape(B, nc, ntpc, C))
            qg = q.reshape(B, G, gs, H, hd).transpose(0, 1, 3, 2, 4)
            kl = k.reshape(B, G, gs, H, hd).transpose(0, 1, 3, 2, 4)
            vl = v.reshape(B, G, gs, H, hd).transpose(0, 1, 3, 2, 4)
            kc = ck[:, :c_max].reshape(B, c_max, H, hd)
            vc = cv[:, :c_max].reshape(B, c_max, H, hd)
            S = _sinusoidal(c_max + gs, hd)
            qr = _rotary(S[:gs], qg)
            kcr = _rotary(S[:c_max, None, :], kc)
            pos_local = jnp.arange(G)[:, None] * ncpg + jnp.arange(gs)[None, :]
            klr = _rotary(S[pos_local][None, :, None], kl)
            scale = 1.0 / math.sqrt(hd)
            sc = jnp.einsum('bghqd,bchd->bghqc', qr, kcr) * scale
            sl = jnp.einsum('bghqd,bghkd->bghqk', qr, klr) * scale
            cmask = jnp.arange(c_max)[None, :] < (jnp.arange(G) * ncpg)[:, None]
            sc = jnp.where(cmask[None, :, None, None, :], sc, -jnp.inf)
            lmask = jnp.tril(jnp.ones((gs, gs), dtype=bool))
            sl = jnp.where(lmask, sl, -jnp.inf)
            p = jax.nn.softmax(jnp.concatenate([sc, sl], axis=-1), axis=-1)
            pc, pl = (p[..., :c_max], p[..., c_max:])
            y = jnp.einsum('bghqc,bchd->bghqd', pc, vc) + jnp.einsum('bghqk,bghkd->bghqd', pl, vl)
            y = y.transpose(0, 1, 3, 2, 4).reshape(B, T, C)
            return y @ w_proj.T + b_proj
        key = jax.random.key(seed)
        ks = jax.random.split(key, 4)
        B, T, C, NC = (4, 1024, 256, N_CLUSTER)
        x = jax.random.normal(ks[0], (B, T, C), jnp.float32)
        w_attn = jax.random.normal(ks[1], (3 * C, C), jnp.float32) * 0.02
        b_attn = jnp.zeros((3 * C,), jnp.float32)
        w_proj = jax.random.normal(ks[2], (C, C), jnp.float32) * 0.02
        b_proj = jnp.zeros((C,), jnp.float32)
        w_assign = jax.random.normal(ks[3], (NC, C), jnp.float32) * 0.02
        return {'x': x, 'w_attn': w_attn, 'b_attn': b_attn, 'w_proj': w_proj, 'b_proj': b_proj, 'w_assign': w_assign}
    _L0_attn_a_in = _L0_attn_a_setup()

    def _L0_attn_b_setup():
        import jax, jax.numpy as jnp
        import numpy as np
        NUM_HEADS = 16
        NUM_LANDMARKS = 64
        DIM = 256
        B, N = (2, 2048)

        def iterative_inv(K, n_iter=6):
            m = K.shape[-1]
            I = jnp.eye(m, dtype=K.dtype)
            denom = jnp.max(jnp.sum(K, axis=-2), axis=-1)[..., None, None]
            V = jnp.swapaxes(K, -1, -2) / denom
            for _ in range(n_iter):
                KV = K @ V
                V = 0.25 * V @ (13.0 * I - KV @ (15.0 * I - KV @ (7.0 * I - KV)))
            return V

        def _reference_tuple_inner(x, w_qkv, w_proj):
            Bb, Nn, C = x.shape
            H = NUM_HEADS
            hd = C // H
            m = NUM_LANDMARKS
            scale = hd ** 0.5
            qkv = (x @ w_qkv).reshape(Bb, Nn, 3, H, hd).transpose(2, 0, 3, 1, 4)
            q, k, v = (qkv[0], qkv[1], qkv[2])
            q = q / scale
            k_lm = k.reshape(Bb, H, m, Nn // m, hd).mean(axis=-2)
            q_lm = q.reshape(Bb, H, m, Nn // m, hd).mean(axis=-2)
            kernel1 = jax.nn.softmax(jnp.einsum('bhnd,bhmd->bhnm', q, k_lm), axis=-1)
            kernel2 = jax.nn.softmax(jnp.einsum('bhld,bhmd->bhlm', q_lm, k_lm), axis=-1)
            kernel3 = jax.nn.softmax(jnp.einsum('bhmd,bhnd->bhmn', q_lm, k), axis=-1)
            SV = kernel1 @ iterative_inv(kernel2) @ (kernel3 @ v)
            SV = SV.transpose(0, 2, 1, 3).reshape(Bb, Nn, C)
            out = SV @ w_proj
            return (out, SV)
        key = jax.random.key(seed)
        k1, k2, k3 = jax.random.split(key, 3)
        x = jax.random.normal(k1, (B, N, DIM), dtype=jnp.float32)
        w_qkv = jax.random.normal(k2, (DIM, 3 * DIM), dtype=jnp.float32) * DIM ** (-0.5)
        w_proj = jax.random.normal(k3, (DIM, DIM), dtype=jnp.float32) * DIM ** (-0.5)
        return {'x': x, 'w_qkv': w_qkv, 'w_proj': w_proj}
    _L0_attn_b_in = _L0_attn_b_setup()

    def _L0_ffn_setup():
        import jax, jax.numpy as jnp
        import numpy as np
        B, S, D, E = (2, 512, 256, 8)
        key = jax.random.key(seed)
        ks = jax.random.split(key, 5)
        x = jax.random.normal(ks[0], (B, S, D), dtype=jnp.float32)
        router_w = jax.random.normal(ks[1], (E, D), dtype=jnp.float32) * 0.02
        router_b = jnp.zeros((E,), dtype=jnp.float32)
        expert_w = jax.random.normal(ks[2], (E, D, D), dtype=jnp.float32) * 0.02
        expert_b = jnp.zeros((E, D), dtype=jnp.float32)
        return {'x': x, 'router_w': router_w, 'router_b': router_b, 'expert_w': expert_w, 'expert_b': expert_b}
    _L0_ffn_in = _L0_ffn_setup()
    _d = {'L0_attn_a_x': _L0_attn_a_in['x'], 'L0_attn_a_w_attn': _L0_attn_a_in['w_attn'], 'L0_attn_a_b_attn': _L0_attn_a_in['b_attn'], 'L0_attn_a_w_proj': _L0_attn_a_in['w_proj'], 'L0_attn_a_b_proj': _L0_attn_a_in['b_proj'], 'L0_attn_a_w_assign': _L0_attn_a_in['w_assign'], 'L0_attn_b_w_qkv': _L0_attn_b_in['w_qkv'], 'L0_attn_b_w_proj': _L0_attn_b_in['w_proj'], 'L0_ffn_router_w': _L0_ffn_in['router_w'], 'L0_ffn_router_b': _L0_ffn_in['router_b'], 'L0_ffn_expert_w': _L0_ffn_in['expert_w'], 'L0_ffn_expert_b': _L0_ffn_in['expert_b']}
    _x0 = _d['L0_attn_a_x']
    _d['L0_attn_a_x'] = jax.random.normal(jax.random.fold_in(jax.random.key(seed), 1), (8, 512, 256), dtype=_x0.dtype)
    del _x0
    return _d

def reference(L0_attn_a_x, L0_attn_a_w_attn, L0_attn_a_b_attn, L0_attn_a_w_proj, L0_attn_a_b_proj, L0_attn_a_w_assign, L0_attn_b_w_qkv, L0_attn_b_w_proj, L0_ffn_router_w, L0_ffn_router_b, L0_ffn_expert_w, L0_ffn_expert_b):

    def _L0_attn_a_ref(x, w_attn, b_attn, w_proj, b_proj, w_assign):
        import math
        import jax, jax.numpy as jnp
        import numpy as np
        N_HEAD = 16
        N_CLUSTER = 64
        GROUP_SIZE = 64

        def _sinusoidal(n, d):
            pos = jnp.arange(n, dtype=jnp.float32)[:, None]
            div = jnp.exp(jnp.arange(0, d, 2, dtype=jnp.float32) * (-math.log(10000.0) / d))
            ang = pos * div
            return jnp.stack([jnp.sin(ang), jnp.cos(ang)], axis=-1).reshape(n, d)

        def _rotary(pe, x):
            d = x.shape[-1]
            sin, cos = (pe[..., :d // 2], pe[..., d // 2:])
            x_even, x_odd = (x[..., ::2], x[..., 1::2])
            out = jnp.stack([-x_odd * cos, x_even * sin], axis=-1)
            return out.reshape(jnp.broadcast_shapes(x.shape[:-1] + (d // 2,), out.shape[:-1]) + (2,)).reshape(x.shape) if False else jnp.broadcast_to(out, x.shape[:-1] + (d // 2, 2)).reshape(x.shape)

        def _forward(x, w_attn, b_attn, w_proj, b_proj, w_assign):
            B, T, C = x.shape
            H, nc, gs = (N_HEAD, N_CLUSTER, GROUP_SIZE)
            hd = C // H
            ntpc = T // nc
            G = T // gs
            ncpg = gs // ntpc
            c_max = (G - 1) * ncpg
            qkv = x @ w_attn.T + b_attn
            q, k, v = jnp.split(qkv, 3, axis=-1)
            x_r = x.reshape(B, nc, ntpc, C)
            logits = jnp.einsum('bctd,cd->bct', x_r, w_assign)
            w = jax.nn.softmax(logits, axis=-1)
            ck = jnp.einsum('bct,bctd->bcd', w, k.reshape(B, nc, ntpc, C))
            cv = jnp.einsum('bct,bctd->bcd', w, v.reshape(B, nc, ntpc, C))
            qg = q.reshape(B, G, gs, H, hd).transpose(0, 1, 3, 2, 4)
            kl = k.reshape(B, G, gs, H, hd).transpose(0, 1, 3, 2, 4)
            vl = v.reshape(B, G, gs, H, hd).transpose(0, 1, 3, 2, 4)
            kc = ck[:, :c_max].reshape(B, c_max, H, hd)
            vc = cv[:, :c_max].reshape(B, c_max, H, hd)
            S = _sinusoidal(c_max + gs, hd)
            qr = _rotary(S[:gs], qg)
            kcr = _rotary(S[:c_max, None, :], kc)
            pos_local = jnp.arange(G)[:, None] * ncpg + jnp.arange(gs)[None, :]
            klr = _rotary(S[pos_local][None, :, None], kl)
            scale = 1.0 / math.sqrt(hd)
            sc = jnp.einsum('bghqd,bchd->bghqc', qr, kcr) * scale
            sl = jnp.einsum('bghqd,bghkd->bghqk', qr, klr) * scale
            cmask = jnp.arange(c_max)[None, :] < (jnp.arange(G) * ncpg)[:, None]
            sc = jnp.where(cmask[None, :, None, None, :], sc, -jnp.inf)
            lmask = jnp.tril(jnp.ones((gs, gs), dtype=bool))
            sl = jnp.where(lmask, sl, -jnp.inf)
            p = jax.nn.softmax(jnp.concatenate([sc, sl], axis=-1), axis=-1)
            pc, pl = (p[..., :c_max], p[..., c_max:])
            y = jnp.einsum('bghqc,bchd->bghqd', pc, vc) + jnp.einsum('bghqk,bghkd->bghqd', pl, vl)
            y = y.transpose(0, 1, 3, 2, 4).reshape(B, T, C)
            return y @ w_proj.T + b_proj
        return _forward(x, w_attn, b_attn, w_proj, b_proj, w_assign)

    def _L0_attn_b_ref(x, w_qkv, w_proj):
        import jax, jax.numpy as jnp
        import numpy as np
        NUM_HEADS = 16
        NUM_LANDMARKS = 64
        DIM = 256
        B, N = (2, 2048)

        def iterative_inv(K, n_iter=6):
            m = K.shape[-1]
            I = jnp.eye(m, dtype=K.dtype)
            denom = jnp.max(jnp.sum(K, axis=-2), axis=-1)[..., None, None]
            V = jnp.swapaxes(K, -1, -2) / denom
            for _ in range(n_iter):
                KV = K @ V
                V = 0.25 * V @ (13.0 * I - KV @ (15.0 * I - KV @ (7.0 * I - KV)))
            return V

        def _reference_tuple_inner(x, w_qkv, w_proj):
            Bb, Nn, C = x.shape
            H = NUM_HEADS
            hd = C // H
            m = NUM_LANDMARKS
            scale = hd ** 0.5
            qkv = (x @ w_qkv).reshape(Bb, Nn, 3, H, hd).transpose(2, 0, 3, 1, 4)
            q, k, v = (qkv[0], qkv[1], qkv[2])
            q = q / scale
            k_lm = k.reshape(Bb, H, m, Nn // m, hd).mean(axis=-2)
            q_lm = q.reshape(Bb, H, m, Nn // m, hd).mean(axis=-2)
            kernel1 = jax.nn.softmax(jnp.einsum('bhnd,bhmd->bhnm', q, k_lm), axis=-1)
            kernel2 = jax.nn.softmax(jnp.einsum('bhld,bhmd->bhlm', q_lm, k_lm), axis=-1)
            kernel3 = jax.nn.softmax(jnp.einsum('bhmd,bhnd->bhmn', q_lm, k), axis=-1)
            SV = kernel1 @ iterative_inv(kernel2) @ (kernel3 @ v)
            SV = SV.transpose(0, 2, 1, 3).reshape(Bb, Nn, C)
            out = SV @ w_proj
            return (out, SV)
        return _reference_tuple_inner(x, w_qkv, w_proj)[0]

    def _L0_ffn_ref(x, router_w, router_b, expert_w, expert_b):
        import jax, jax.numpy as jnp
        import numpy as np
        B, S, D, E = (2, 512, 256, 8)
        logits = jnp.einsum('bsd,ed->bse', x, router_w) + router_b
        probs = jax.nn.softmax(logits, axis=-1)
        weights = jnp.max(probs, axis=-1)
        top1 = jnp.argmax(probs, axis=-1)
        y_all = jnp.einsum('bsd,eod->bseo', x, expert_w) + expert_b
        y = jnp.take_along_axis(y_all, top1[:, :, None, None], axis=2)[:, :, 0, :]
        out = y * weights[:, :, None]
        return out
    x = L0_attn_a_x
    x = x + _L0_attn_a_ref(_layernorm(x, axis=-1), L0_attn_a_w_attn, L0_attn_a_b_attn, L0_attn_a_w_proj, L0_attn_a_b_proj, L0_attn_a_w_assign)
    x = x + _L0_ffn_ref(_layernorm(x, axis=-1), L0_ffn_router_w, L0_ffn_router_b, L0_ffn_expert_w, L0_ffn_expert_b)
    x = x + _L0_attn_b_ref(_layernorm(x, axis=-1), L0_attn_b_w_qkv, L0_attn_b_w_proj)
    x = x + _L0_ffn_ref(_layernorm(x, axis=-1), L0_ffn_router_w, L0_ffn_router_b, L0_ffn_expert_w, L0_ffn_expert_b)
    return x

_drawn_inputs = setup_inputs


def setup_inputs(seed=0):
    import zlib

    import numpy as np

    out = dict(_drawn_inputs(seed))
    spreads = {'L0_attn_a_b_attn': (0.0, 0.1),
     'L0_attn_a_b_proj': (0.0, 0.1),
     'L0_ffn_router_b': (0.0, 0.1),
     'L0_ffn_expert_b': (0.0, 0.1)}
    factors = {'L0_attn_a_w_attn': 3.148, 'L0_attn_a_w_assign': 8.0}
    for name, (base, spread) in spreads.items():
        noise = np.random.default_rng([zlib.crc32(name.encode()), seed]).standard_normal(out[name].shape)
        drawn = base * np.exp(spread * noise) if base else spread * noise
        out[name] = jnp.asarray(drawn.astype(out[name].dtype))
    for name, factor in factors.items():
        out[name] = (out[name] * factor).astype(out[name].dtype)
    return out
```

```python
import concourse.bass as bass
from concourse import mybir
from contextlib import ExitStack

fp32 = mybir.dt.float32
bf16 = mybir.dt.bfloat16
ALU = mybir.AluOpType
ACT = mybir.ActivationFunctionType
AX = mybir.AxisListType

P = 128
B, T, C = 8, 512, 256
H, HD = 16, 16
NT = T // P
E = 8
EPS = 1e-5


def ln_rstd(nc, dve, stats, mean, rstd, scr, s_var, s_sqrt):
    me, mo = stats[:, :, 1], stats[:, :, 4]
    half, dif, var, std = (scr[:, i, :] for i in range(4))
    tt = nc.vector.tensor_tensor
    tt(out=half, in0=me, in1=mo, op=ALU.add).then_inc(s_var, 1)
    tt(out=dif, in0=me, in1=mo, op=ALU.subtract).then_inc(s_var, 1)
    tt(out=var, in0=stats[:, :, 2], in1=stats[:, :, 5], op=ALU.add).then_inc(s_var, 1)
    dve.wait_ge(s_var, 3)
    nc.vector.tensor_scalar(mean[:], half, 0.5, None, ALU.mult).then_inc(s_var, 1)
    nc.vector.tensor_scalar(var, var, 1.0 / C, EPS, ALU.mult, ALU.add).then_inc(s_var, 1)
    nc.vector.tensor_scalar(dif, dif, 0.5, None, ALU.mult).then_inc(s_var, 1)
    dve.wait_ge(s_var, 6)
    tt(out=half, in0=dif, in1=dif, op=ALU.mult).then_inc(s_var, 1)
    dve.wait_ge(s_var, 7)
    tt(out=var, in0=var, in1=half, op=ALU.add).then_inc(s_var, 1)
    dve.wait_ge(s_sqrt, 1)
    nc.vector.reciprocal(rstd[:], std).then_inc(s_var, 1)
    dve.wait_ge(s_var, 9)
    tt(out=half, in0=rstd[:], in1=rstd[:], op=ALU.mult).then_inc(s_var, 1)
    dve.wait_ge(s_var, 10)
    tt(out=half, in0=half, in1=var, op=ALU.mult).then_inc(s_var, 1)
    dve.wait_ge(s_var, 11)
    nc.vector.tensor_scalar(half, half, -0.5, 1.5, ALU.mult, ALU.add).then_inc(s_var, 1)
    dve.wait_ge(s_var, 12)
    tt(out=rstd[:], in0=rstd[:], in1=half, op=ALU.mult).then_inc(s_var, 1)
    dve.wait_ge(s_var, 13)


def ln_sqrt(nc, act, scr, s_var, s_sqrt):
    act.wait_ge(s_var, 8)
    nc.scalar.activation(scr[:, 3, :], scr[:, 2, :], ACT.Sqrt).then_inc(s_sqrt, 1)


def cluster_attention(nc, X, stats, ident, identb, w):
    with ExitStack() as ctx:
        sb = lambda name, shape, dt=fp32: ctx.enter_context(nc.sbuf_tensor("a_" + name, shape, dt))
        sem = lambda name: ctx.enter_context(nc.semaphore("a_" + name))

        GS = 64
        NCL = 64
        KEYS = GS + NCL
        HQ = 4
        UNITS = NT * (H // HQ)
        DV = HD + 1
        HH = 2
        H8 = H // HH

        wqkT = sb("wqkT", [P, 2, 2 * C])
        wvT = sb("wvT", [P, 2, C])
        wpT = sb("wpT", [P, 2, C])
        bqk = sb("bqk", [P, 4])
        bv = sb("bv", [P, C])
        bp = sb("bp", [P, C])
        wassign = sb("wassign", [P, NT, C])
        tabq = sb("tabq", [P, GS])
        tabk = sb("tabk", [P, T])
        tabc = sb("tabc", [P, H8, NCL])
        own16 = sb("own16", [P, 32])
        maskf = sb("maskf", [P, NT, KEYS])
        maskb = sb("maskb", [P, NT, KEYS], bf16)
        rstd = sb("rstd", [P, B * NT])
        mean = sb("mean", [P, B * NT])
        scr = sb("scr", [P, 4, B * NT])

        xn = sb("xn", [P, NT, C])
        xT = sb("xT", [P, 2, T])
        dump = sb("dump", [P, C])
        logit = sb("logit", [P, NT])
        lrow = sb("lrow", [NT, T // NT])
        lmax = sb("lmax", [NT, 16])
        lexp = sb("lexp", [NT, T // NT])
        lsum = sb("lsum", [NT, 16])
        lw = sb("lw", [NT, T // NT])
        wsel = sb("wsel", [P, NT, 32])
        xbar = sb("xbar", [P, C])
        xbT = sb("xbT", [P, 2, 2, NCL])
        qT = sb("qT", [P, HH, T])
        kT = sb("kT", [P, HH, T])
        bdK = sb("bdK", [P, HH, H8, T])
        bdC = sb("bdC", [P, HH, H8, NCL])
        cvb = sb("cvb", [P, C])
        V = [sb(f"V{e}", [P, NT, H, DV]) for e in range(2)]
        smax = sb("smax", [P, 2, HQ])
        sh = sb("sh", [P, 2, HQ, KEYS])
        pr = sb("pr", [P, 2, HQ, KEYS])
        pT = sb("pT", [P, 2, HQ, P])
        rsum = sb("rsum", [P, 2, H])
        y = sb("y", [P, 2, C])
        yT = sb("yT", [P, 2, 2, P])

        bank = [ctx.enter_context(nc.psum_tensor(f"a_bank{i}", [P, 512], fp32)) for i in range(8)]
        S, TB, O, G = bank[0:3], bank[3:5], bank[5], bank[6:8]

        USES = ["xT0", "xT1", "lgT", "q0", "q1", "wT", "k0", "k1", "xb", "xbT", "ckv", "v0", "v1"]
        for t in range(NT):
            USES += [f"yT{t}", f"pj{t}"]
        PER = [(len(USES) + 1) // 2, len(USES) // 2]

        s_const = sem("const_loaded")
        s_prep = sem("constants_ready")
        s_zero = sem("zeroed")
        s_var = sem("variance")
        s_sqrt = sem("sqrt_done")
        s_batch = sem("batch_done")
        s_xn = sem("xn_ready")
        s_logit = sem("logit_ready")
        s_lexp = sem("logit_exp")
        s_lsum = sem("cluster_softmax_steps")
        s_lw = sem("cluster_weights")
        s_bdk = sem("bdk_ready")
        s_vc = sem("cluster_v_placed")
        s_bias = sem("x_biased")
        s_full = [sem("g_full0"), sem("g_full1")]
        s_empty = [sem("g_empty0"), sem("g_empty1")]
        s_scores = sem("scores_ready")
        s_max = sem("row_max")
        s_sh = sem("scores_shifted")
        s_exp = sem("exp_done")
        s_tp = sem("probs_transposed")
        s_pT = sem("pT_ready")
        s_pv = sem("pv_done")
        s_rsum = sem("rsum_ready")
        s_y = sem("y_ready")

        def g(name):
            i = USES.index(name)
            return i % 2, i // 2

        def full(eng, n, name):
            b, k = g(name)
            eng.wait_ge(s_full[b], n * PER[b] + k + 1)
            return G[b]

        def filled(ins, name):
            ins.then_inc(s_full[g(name)[0]], 1)

        def emptied(ins, name):
            ins.then_inc(s_empty[g(name)[0]], 1)

        def out_of(eng, n, name):
            b, k = g(name)
            eng.wait_ge(s_empty[b], n * PER[b] + k + 2)

        def claim(pe, n, name):
            b, k = g(name)
            pe.wait_ge(s_empty[b], n * PER[b] + k + 1)
            return G[b]

        LOADS = 16 * (11 + NT * 8)
        block = ctx.enter_context(nc.Block())

        @block.sync
        def _(sp):
            cw = w["a_w_attnT"]
            loads = [(wqkT[:], cw[:, 0:2 * C].rearrange("(k p) n -> p k n", p=P)),
                     (wvT[:], cw[:, 2 * C:3 * C].rearrange("(k p) n -> p k n", p=P)),
                     (wpT[:], w["a_w_projT"].rearrange("(k p) n -> p k n", p=P)),
                     (bqk[:], w["a_bqk"]),
                     (bv[:], w["a_b_attn"][2 * C:3 * C].partition_broadcast(P)),
                     (bp[:], w["a_b_proj"].partition_broadcast(P)),
                     (tabq[:], w["tabq"]), (tabk[:], w["tabk"]),
                     (tabc[:], w["tabc"]), (own16[:], w["own16"]), (maskf[:], w["maska"])]
            for dst, src in loads:
                sp.dma_start(dst, src).then_inc(s_const, 16)
            per = P // 8
            for t in range(NT):
                for j in range(8):
                    sp.dma_start(wassign[j:P:8, t, :], w["a_w_assign"][t * per:(t + 1) * per, :])\
                      .then_inc(s_const, 16)
            sp.wait_ge(s_zero, 2)
            with sp.Fori(0, B) as n:
                for hh in range(HH):
                    out_of(sp, n, f"k{hh}")
                    sp.nop(nofuse=True)
                    for h in range(H8):
                        sp.dma_start(bdK[h * HD:(h + 1) * HD, hh, h, :], kT[h * HD:(h + 1) * HD, hh, :])\
                          .then_inc(s_bdk, 16)
                sp.wait_ge(s_bdk, (n + 1) * H * 16)
                sp.nop(nofuse=True)

        @block.gpsimd
        def _(pool):
            nc.gpsimd.memset(bdK[:], 0.0).then_inc(s_zero, 1)
            for e in range(2):
                last = nc.gpsimd.memset(V[e][:], 1.0)
            last.then_inc(s_zero, 1)
            pool.wait_ge(s_const, LOADS)
            with pool.Fori(0, B) as n:
                pool.wait_ge(s_xn, (n + 1) * NT)
                xb = X[:, bass.ds(n * NT, NT), :]
                nc.gpsimd.tensor_tensor(out=xb, in0=xb, in1=bp[:].unsqueeze(1).broadcast_to([P, NT, C]),
                                        op=ALU.add).then_inc(s_bias, 1)
                out_of(pool, n, "ckv")
                for e, r in ((0, 64), (1, 0)):
                    pool.wait_ge(s_bias, n + 1)
                    if e == 1:
                        pool.wait_ge(s_vc, n * 2 + 1)
                    pool.nop(nofuse=True)
                    for t in range(NT):
                        last = nc.gpsimd.tensor_copy(
                            V[e][r:r + 64, t, :, 0:HD],
                            cvb[r:r + 64, :].rearrange("p (h d) -> p h d", h=H))
                    last.then_inc(s_vc, 1)
                pool.wait_ge(s_vc, n * 2 + 2)
                pool.nop(nofuse=True)

        @block.vector
        def _(dve):
            ln_rstd(nc, dve, stats, mean, rstd, scr, s_var, s_sqrt)
            dve.wait_ge(s_const, LOADS)
            nc.vector.tensor_copy(maskb[:], maskf[:]).then_inc(s_prep, 1)
            dve.wait_ge(s_zero, 2)
            with dve.Fori(0, B) as n:
                dve.wait_ge(s_batch, n + 1)
                for t in range(NT):
                    tt = n * NT + t
                    nc.vector.tensor_scalar(xn[:, t, :], X[:, bass.ds(tt, 1), :], mean[:, bass.ds(tt, 1)],
                                            rstd[:, bass.ds(tt, 1)], ALU.subtract, ALU.mult).then_inc(s_xn, 1)
                for t in range(NT):
                    dve.wait_ge(s_xn, n * NT + t + 1)
                    last = nc.vector.tensor_tensor_reduce(
                        out=dump[:], in0=xn[:, t, :], in1=wassign[:, t, :], scale=1.0, scalar=0.0,
                        op0=ALU.mult, op1=ALU.add, accum_out=logit[:, t:t + 1])
                    last.then_inc(s_logit, 1)
                    dve.wait_ge(s_logit, n * NT + t + 1)
                gb = full(dve, n, "lgT")
                row = gb[0:NT, 0:P].rearrange("t (c j) -> t c j", j=8)
                nc.vector.tensor_reduce(out=lmax[:], in_=row, axis=AX.X, op=ALU.max).then_inc(s_lsum, 1)
                dve.wait_ge(s_lsum, n * 3 + 1)
                last = nc.vector.tensor_tensor(
                    out=lrow[:].rearrange("t (c j) -> t c j", j=8), in0=row,
                    in1=lmax[:].unsqueeze(2).broadcast_to([NT, 16, 8]), op=ALU.subtract)
                emptied(last, "lgT")
                for hh in range(HH):
                    gb = full(dve, n, f"q{hh}")
                    last = nc.vector.scalar_tensor_tensor(
                        out=qT[:, hh, :].rearrange("p (g j) -> p g j", j=GS),
                        in0=gb[:].rearrange("p (g j) -> p g j", j=GS), scalar=bqk[:, hh:hh + 1],
                        in1=tabq[:].unsqueeze(1).broadcast_to([P, T // GS, GS]), op0=ALU.add, op1=ALU.mult)
                    emptied(last, f"q{hh}")
                dve.wait_ge(s_lexp, n + 1)
                nc.vector.tensor_reduce(out=lsum[:], in_=lexp[:].rearrange("t (c j) -> t c j", j=8),
                                        axis=AX.X, op=ALU.add).then_inc(s_lsum, 1)
                dve.wait_ge(s_lsum, n * 3 + 2)
                nc.vector.reciprocal(lmax[:], lsum[:]).then_inc(s_lsum, 1)
                dve.wait_ge(s_lsum, n * 3 + 3)
                nc.vector.tensor_tensor(
                    out=lw[:].rearrange("t (c j) -> t c j", j=8), in0=lexp[:].rearrange("t (c j) -> t c j", j=8),
                    in1=lmax[:].unsqueeze(2).broadcast_to([NT, 16, 8]), op=ALU.mult).then_inc(s_lw, 1)
                gb = full(dve, n, "wT")
                last = nc.vector.tensor_tensor(
                    out=wsel[:], in0=gb[:, 0:NT].unsqueeze(2).broadcast_to([P, NT, 32]),
                    in1=own16[:].unsqueeze(1).broadcast_to([P, NT, 32]), op=ALU.mult)
                emptied(last, "wT")
                for hh in range(HH):
                    gb = full(dve, n, f"k{hh}")
                    last = nc.vector.scalar_tensor_tensor(out=kT[:, hh, :], in0=gb[:], scalar=bqk[:, 2 + hh:3 + hh],
                                                   in1=tabk[:], op0=ALU.add, op1=ALU.mult)
                    emptied(last, f"k{hh}")
                gb = full(dve, n, "ckv")
                for hh in range(HH):
                    nc.vector.scalar_tensor_tensor(
                        out=bdC[:, hh], in0=gb[:, hh * P:hh * P + NCL].unsqueeze(1).broadcast_to([P, H8, NCL]),
                        scalar=bqk[:, 2 + hh:3 + hh], in1=tabc[:], op0=ALU.add, op1=ALU.mult)
                last = nc.vector.tensor_tensor(out=cvb[:], in0=gb[:, 256:512], in1=bv[:], op=ALU.add)
                emptied(last, "ckv")
                for i in range(2):
                    gb = full(dve, n, f"v{i}")
                    for e in range(2):
                        r = slice(64 * e, 64 * e + 64)
                        last = nc.vector.tensor_tensor(
                            out=V[e][r, 2 * i:2 * i + 2, :, 0:HD],
                            in0=gb[r, :].rearrange("p (t h d) -> p t h d", t=2, h=H),
                            in1=bv[r, :].rearrange("p (h d) -> p h d", h=H).unsqueeze(1)
                            .broadcast_to([64, 2, H, HD]), op=ALU.add)
                    emptied(last, f"v{i}")

                def normalise(t):
                    dve.wait_ge(s_pv, n * UNITS + 4 * t + 4)
                    if t >= 2:
                        dve.wait_ge(s_y, n * NT + t - 1)
                    o = O[:, 0:H * DV].rearrange("p (h d) -> p h d", d=DV)
                    nc.vector.reciprocal(rsum[:, t % 2, :], o[:, :, HD:DV]).then_inc(s_rsum, 1)
                    dve.wait_ge(s_rsum, n * NT + t + 1)
                    nc.vector.tensor_tensor(
                        out=y[:, t % 2, :].rearrange("p (h d) -> p h d", h=H), in0=o[:, :, 0:HD],
                        in1=rsum[:, t % 2, :].unsqueeze(2).broadcast_to([P, H, HD]), op=ALU.mult).then_inc(s_y, 1)

                def residual(t):
                    gb = full(dve, n, f"pj{t}")
                    tt = n * NT + t
                    if t == 0:
                        dve.wait_ge(s_bias, n + 1)
                    x = X[:, bass.ds(tt, 1), :]
                    last = nc.vector.tensor_tensor(out=x, in0=x, in1=gb[:, 0:C].unsqueeze(1), op=ALU.add)
                    emptied(last, f"pj{t}")
                    out_of(dve, n, f"pj{t}")
                    dve.nop(nofuse=True)
                    last = nc.vector.bn_stats(stats[:, bass.ds(tt, 1), :], x)
                    if t == NT - 1:
                        last.then_inc(s_batch, 1)

                for u in range(UNITS + 4):
                    if u < UNITS:
                        sc = S[u % 3][:].rearrange("p (h k) -> p h k", h=HQ)
                        dve.wait_ge(s_scores, n * UNITS + u + 1)
                        nc.vector.tensor_reduce(out=smax[:, u % 2, :], in_=sc, axis=AX.X, op=ALU.max)\
                          .then_inc(s_max, 1)
                        dve.wait_ge(s_max, n * UNITS + u + 1)
                        if u >= 2:
                            dve.wait_ge(s_exp, n * UNITS + u - 1)
                        nc.vector.tensor_tensor(
                            out=sh[:, u % 2], in0=sc,
                            in1=smax[:, u % 2, :].unsqueeze(2).broadcast_to([P, HQ, KEYS]),
                            op=ALU.subtract).then_inc(s_sh, 1)
                    if u >= 7 and (u - 7) % 4 == 0 and (u - 7) // 4 < NT - 1:
                        normalise((u - 7) // 4)
                    if u >= 10 and (u - 10) % 4 == 0 and (u - 10) // 4 < NT - 2:
                        residual((u - 10) // 4)
                normalise(NT - 1)
                residual(NT - 2)
                residual(NT - 1)

        @block.scalar
        def _(act):
            ln_sqrt(nc, act, scr, s_var, s_sqrt)
            with act.Fori(0, B) as n:
                for kc in range(2):
                    gb = full(act, n, f"xT{kc}")
                    emptied(nc.scalar.activation(xT[:, kc, :], gb[:], ACT.Copy), f"xT{kc}")
                out_of(act, n, "lgT")
                nc.scalar.activation(lexp[:], lrow[:], ACT.Exp).then_inc(s_lexp, 1)
                gb = full(act, n, "xb")
                emptied(nc.scalar.activation(xbar[:], gb[:, 0:C], ACT.Copy), "xb")
                gb = full(act, n, "xbT")
                for kc in range(2):
                    for dup in range(2):
                        last = nc.scalar.activation(
                            xbT[:, kc, dup, :].rearrange("p (t c) -> p t c", t=NT),
                            gb[:, kc * P:(kc + 1) * P].rearrange("p (t c) -> p t c", t=NT)[:, :, 0:16], ACT.Copy)
                emptied(last, "xbT")

                def copy_yT(t):
                    gb = full(act, n, f"yT{t}")
                    emptied(nc.scalar.activation(yT[:, t % 2], gb[:, 0:C].rearrange("p (k q) -> p k q", k=2),
                                                 ACT.Copy), f"yT{t}")

                for u in range(UNITS + 3):
                    if u < UNITS:
                        act.wait_ge(s_sh, n * UNITS + u + 1)
                        if u >= 2:
                            act.wait_ge(s_tp, n * UNITS + u - 1)
                        nc.scalar.activation(pr[:, u % 2], sh[:, u % 2], ACT.Exp, scale=float(HD) ** -0.5)\
                          .then_inc(s_exp, 1)
                    if u >= 2 and u - 2 < UNITS:
                        v = u - 2
                        act.wait_ge(s_tp, n * UNITS + v + 1)
                        if v >= 2:
                            act.wait_ge(s_pv, n * UNITS + v - 1)
                        nc.scalar.activation(pT[:, v % 2], TB[v % 2][:].rearrange("p (h q) -> p h q", h=HQ),
                                             ACT.Copy).then_inc(s_pT, 1)
                    if u >= 9 and (u - 9) % 4 == 0 and (u - 9) // 4 < NT - 1:
                        copy_yT((u - 9) // 4)
                copy_yT(NT - 1)

        @block.tensor
        def _(pe):
            mm = nc.tensor.matmul
            pe.sem_inc(s_empty[0], 1)
            pe.sem_inc(s_empty[1], 1)
            pe.sem_inc(s_batch, 1)
            pe.wait_ge(s_const, LOADS)
            pe.wait_ge(s_prep, 1)
            pe.wait_ge(s_zero, 2)
            with pe.Fori(0, B) as n:
                for kc in range(2):
                    gb = claim(pe, n, f"xT{kc}")
                    for t in range(NT):
                        if kc == 0:
                            pe.wait_ge(s_xn, n * NT + t + 1)
                        last = nc.tensor.transpose(gb[:, t * P:(t + 1) * P], xn[:, t, kc * P:(kc + 1) * P], ident[:])
                    filled(last, f"xT{kc}")
                gb = claim(pe, n, "lgT")
                pe.wait_ge(s_logit, (n + 1) * NT)
                filled(nc.tensor.transpose(gb[0:NT, 0:P], logit[:], ident[:]), "lgT")

                def project(name, blk, last=None):
                    gb = claim(pe, n, name)
                    for kc in range(2):
                        out_of(pe, n, f"xT{kc}")
                    for kc in range(2):
                        last = mm(gb[:], wqkT[:, kc, blk * P:(blk + 1) * P], xT[:, kc, :],
                                  start=(kc == 0), stop=(kc == 1))
                    filled(last, name)

                project("q0", 0)
                project("q1", 1)
                gb = claim(pe, n, "wT")
                pe.wait_ge(s_lw, n + 1)
                pe.nop(nofuse=True)
                filled(nc.tensor.transpose(gb[:, 0:NT], lw[:], ident[0:NT, 0:NT]), "wT")
                project("k0", 2)
                project("k1", 3)
                gb = claim(pe, n, "xb")
                out_of(pe, n, "wT")
                for t in range(NT):
                    last = mm(gb[32 * t:32 * t + 32, 0:C], wsel[:, t, :], xn[:, t, :], start=True, stop=True)
                filled(last, "xb")
                gb = claim(pe, n, "xbT")
                out_of(pe, n, "xb")
                for kc in range(2):
                    last = nc.tensor.transpose(gb[:, kc * P:(kc + 1) * P], xbar[:, kc * P:(kc + 1) * P], ident[:])
                filled(last, "xbT")
                gb = claim(pe, n, "ckv")
                out_of(pe, n, "xbT")
                for hh in range(HH):
                    for kc in range(2):
                        mm(gb[:, hh * P:(hh + 1) * P], wqkT[:, kc, (2 + hh) * P:(3 + hh) * P],
                           xbT[:, kc, :, :], start=(kc == 0), stop=(kc == 1))
                for kc in range(2):
                    last = mm(gb[:, 256:512], xbT[:, kc, :, :], wvT[:, kc, :], start=(kc == 0), stop=(kc == 1))
                filled(last, "ckv")
                for i in range(2):
                    gb = claim(pe, n, f"v{i}")
                    for t in (2 * i, 2 * i + 1):
                        for kc in range(2):
                            last = mm(gb[:, (t % 2) * C:(t % 2 + 1) * C], xT[:, kc, t * P:(t + 1) * P],
                                      wvT[:, kc, :], start=(kc == 0), stop=(kc == 1))
                    filled(last, f"v{i}")

                def scores(u):
                    t, hq = u // 4, u % 4
                    hh, h0 = hq // 2, (hq % 2) * HQ
                    if u == 0:
                        out_of(pe, n, "q0")
                        out_of(pe, n, "q1")
                        pe.wait_ge(s_bdk, (n + 1) * H * 16)
                        out_of(pe, n, "ckv")
                    if u >= 3:
                        pe.wait_ge(s_sh, n * UNITS + u - 2)
                    s4 = S[u % 3][:].rearrange("p (h k) -> p h k", h=HQ)
                    q0 = t * P
                    hs = slice(h0, h0 + HQ)
                    for e in range(2):
                        r = slice(64 * e, 64 * e + 64)
                        mm(s4[r], identb[:, r], maskb[:, t, :].unsqueeze(1).broadcast_to([P, HQ, KEYS]),
                           start=True, stop=False)
                    for part in range(2):
                        for e in range(2):
                            r = slice(64 * e, 64 * e + 64)
                            cols = slice(64 * ((part + e) % 2), 64 * ((part + e) % 2) + 64)
                            lhs = qT[:, hh, q0 + 64 * e:q0 + 64 * e + 64]
                            rhs = (bdK[:, hh, hs, q0 + 64 * e:q0 + 64 * e + 64] if part == 0 else bdC[:, hh, hs, :])
                            last = mm(s4[r, :, cols], lhs, rhs, start=False, stop=(part == 1))
                    last.then_inc(s_scores, 1)

                def turn(u):
                    pe.wait_ge(s_exp, n * UNITS + u + 1)
                    if u >= 2:
                        pe.wait_ge(s_pT, n * UNITS + u - 1)
                    for h in range(HQ):
                        last = nc.tensor.transpose(TB[u % 2][:, h * P:(h + 1) * P], pr[:, u % 2, h, :], ident[:])
                    last.then_inc(s_tp, 1)

                def weigh(u):
                    t, hq = u // 4, u % 4
                    pe.wait_ge(s_pT, n * UNITS + u + 1)
                    if u == 0:
                        out_of(pe, n, "v0")
                        out_of(pe, n, "v1")
                        pe.wait_ge(s_vc, n * 2 + 2)
                    if hq == 0 and t >= 1:
                        pe.wait_ge(s_y, n * NT + t)
                    for h in range(HQ):
                        for j in range(4):
                            hd = hq * HQ + h
                            last = mm(O[32 * j:32 * j + 32, hd * DV:(hd + 1) * DV],
                                      pT[:, u % 2, h, 32 * j:32 * j + 32], V[j // 2][:, t, hd, :],
                                      start=True, stop=True)
                    last.then_inc(s_pv, 1)

                def out_t(t):
                    gb = claim(pe, n, f"yT{t}")
                    pe.wait_ge(s_y, n * NT + t + 1)
                    for kc in range(2):
                        last = nc.tensor.transpose(gb[:, kc * P:(kc + 1) * P], y[:, t % 2, kc * P:(kc + 1) * P],
                                                   ident[:])
                    filled(last, f"yT{t}")

                def out_p(t):
                    gb = claim(pe, n, f"pj{t}")
                    out_of(pe, n, f"yT{t}")
                    for kc in range(2):
                        last = mm(gb[:, 0:C], yT[:, t % 2, kc, :], wpT[:, kc, :], start=(kc == 0), stop=(kc == 1))
                    filled(last, f"pj{t}")

                for u in range(UNITS + 3):
                    if u < UNITS:
                        scores(u)
                    if 2 <= u < UNITS + 2:
                        turn(u - 2)
                    if u >= 3:
                        weigh(u - 3)
                    if u >= 8 and (u - 8) % 4 == 0 and (u - 8) // 4 < NT - 1:
                        out_t((u - 8) // 4)
                    if u >= 9 and (u - 9) % 4 == 0 and (u - 9) // 4 < NT - 1:
                        out_p((u - 9) // 4)
                out_t(NT - 1)
                out_p(NT - 1)
def moe_ffn(nc, X, stats, ident, w, phase):
    with ExitStack() as ctx:
        sb = lambda name, shape, dt=fp32: ctx.enter_context(nc.sbuf_tensor(f"f{phase}_" + name, shape, dt))
        sem = lambda name: ctx.enter_context(nc.semaphore(f"f{phase}_" + name))

        rw = sb("rw", [P, 2, E])
        rb = sb("rb", [P, E])
        ew = sb("ew", [P, 2, E, C])
        eb = sb("eb", [E, C])
        rank = sb("rank", [P, E])
        rstd = sb("rstd", [P, B * NT])
        mean = sb("mean", [P, B * NT])
        scr = sb("scr", [P, 4, B * NT])
        xn = sb("xn", [P, NT, C])
        xT = sb("xT", [P, 2, T])
        lg = sb("lg", [P, NT, E])
        lmax = sb("lmax", [P, NT])
        sh = sb("sh", [P, NT, E])
        ex = sb("ex", [P, NT, E])
        first = sb("first", [P, NT, E])
        wt = sb("wt", [P, NT])
        best = sb("best", [P, NT])
        coef = sb("coef", [P, NT, E])
        coefT = sb("coefT", [E, NT, P])
        acc = sb("acc", [P, 2, C])

        bank = [ctx.enter_context(nc.psum_tensor(f"f{phase}_bank{i}", [P, 512], fp32)) for i in range(8)]
        XB, LG, BI, Y = bank[0:2], bank[2], bank[3], bank[4:8]

        s_const, s_var, s_sqrt = sem("const_loaded"), sem("variance"), sem("sqrt_done")
        s_batch = sem("batch_done")
        s_xn = sem("xn_ready")
        s_tx = sem("x_transposed")
        s_xT = sem("xT_ready")
        s_lg = sem("logits_done")
        s_route = sem("route_steps")
        s_ex = sem("exp_done")
        s_tc = sem("coef_transposed")
        s_bi = sem("bias_done")
        s_acc = sem("acc_steps")
        s_y = [sem(f"expert_pair{j}") for j in range(4)]
        LOADS = 16 * 6
        ROUTE, ACCS = 11, E + 1
        block = ctx.enter_context(nc.Block())

        @block.sync
        def _(sp):
            for dst, src in [(rw[:], w["r_wT"].rearrange("(k p) e -> p k e", p=P)),
                             (rb[:], w["r_b"].partition_broadcast(P)),
                             (eb[:], w["e_b"]), (rank[:], w["rank"])]:
                sp.dma_start(dst, src).then_inc(s_const, 16)
            for kc in range(2):
                sp.dma_start(ew[:, kc], w["e_wT"][:, kc * P:(kc + 1) * P, :].rearrange("e p o -> p e o"))\
                  .then_inc(s_const, 16)

        @block.vector
        def _(dve):
            ln_rstd(nc, dve, stats, mean, rstd, scr, s_var, s_sqrt)
            dve.wait_ge(s_const, LOADS)
            V = nc.vector
            TTE = [P, NT, E]
            with dve.Fori(0, B) as n:
                dve.wait_ge(s_batch, n + 1)
                for t in range(NT):
                    tt = n * NT + t
                    V.tensor_scalar(xn[:, t, :], X[:, bass.ds(tt, 1), :], mean[:, bass.ds(tt, 1)],
                                    rstd[:, bass.ds(tt, 1)], ALU.subtract, ALU.mult).then_inc(s_xn, 1)
                count = 0

                def step(ins):
                    nonlocal count
                    ins.then_inc(s_route, 1)
                    count += 1
                    dve.wait_ge(s_route, n * ROUTE + count)

                dve.wait_ge(s_lg, n + 1)
                step(V.tensor_tensor(out=lg[:], in0=LG[:, 0:NT * E].rearrange("p (t e) -> p t e", e=E),
                                     in1=rb[:].unsqueeze(1).broadcast_to(TTE), op=ALU.add))
                step(V.tensor_reduce(out=lmax[:], in_=lg[:], axis=AX.X, op=ALU.max))
                step(V.tensor_tensor(out=sh[:], in0=lg[:], in1=lmax[:].unsqueeze(2).broadcast_to(TTE),
                                     op=ALU.subtract))
                step(V.tensor_scalar(first[:], sh[:], 0.0, None, ALU.is_ge))
                step(V.tensor_tensor(out=first[:], in0=first[:], in1=rank[:].unsqueeze(1).broadcast_to(TTE),
                                     op=ALU.mult))
                step(V.tensor_reduce(out=best[:], in_=first[:], axis=AX.X, op=ALU.max))
                step(V.tensor_tensor(out=first[:], in0=first[:], in1=best[:].unsqueeze(2).broadcast_to(TTE),
                                     op=ALU.is_equal))
                dve.wait_ge(s_ex, n + 1)
                step(V.tensor_reduce(out=wt[:], in_=ex[:], axis=AX.X, op=ALU.add))
                step(V.reciprocal(best[:], wt[:]))
                step(V.tensor_tensor(out=coef[:], in0=first[:], in1=best[:].unsqueeze(2).broadcast_to(TTE),
                                     op=ALU.mult))
                dve.wait_ge(s_tc, n + 1)
                step(V.tensor_copy(coefT[:], LG[0:E, 0:NT * P].rearrange("e (t p) -> e t p", t=NT)))
                for t in range(NT):
                    a = acc[:, t % 2, :]
                    base = n * NT * ACCS + t * ACCS
                    dve.wait_ge(s_bi, n * NT + t + 1)
                    x = X[:, bass.ds(n * NT + t, 1), :]
                    V.tensor_tensor(out=a.unsqueeze(1), in0=x, in1=BI[:, 0:C].unsqueeze(1), op=ALU.add)\
                     .then_inc(s_acc, 1)
                    for e in range(E):
                        if e % 2 == 0:
                            dve.wait_ge(s_y[e // 2], n * NT + t + 1)
                        dve.wait_ge(s_acc, base + e + 1)
                        y = Y[e // 2][:, (e % 2) * C:(e % 2 + 1) * C]
                        if e == E - 1:
                            dve.nop(nofuse=True)
                        V.scalar_tensor_tensor(out=(x.squeeze(1) if e == E - 1 else a), in0=y,
                                               scalar=coef[:, t, e:e + 1], in1=a, op0=ALU.mult, op1=ALU.add)\
                         .then_inc(s_acc, 1)
                    dve.wait_ge(s_acc, base + ACCS)
                    dve.nop(nofuse=True)
                    last = V.bn_stats(stats[:, bass.ds(n * NT + t, 1), :], x)
                last.then_inc(s_batch, 1)

        @block.scalar
        def _(act):
            ln_sqrt(nc, act, scr, s_var, s_sqrt)
            with act.Fori(0, B) as n:
                for kc in range(2):
                    act.wait_ge(s_tx, n * 2 + kc + 1)
                    nc.scalar.activation(xT[:, kc, :], XB[kc][:], ACT.Copy).then_inc(s_xT, 1)
                act.wait_ge(s_route, n * ROUTE + 3)
                nc.scalar.activation(ex[:], sh[:], ACT.Exp).then_inc(s_ex, 1)

        @block.tensor
        def _(pe):
            mm = nc.tensor.matmul
            pe.sem_inc(s_batch, 1)
            pe.wait_ge(s_const, LOADS)
            with pe.Fori(0, B) as n:
                for kc in range(2):
                    for t in range(NT):
                        if kc == 0:
                            pe.wait_ge(s_xn, n * NT + t + 1)
                        last = nc.tensor.transpose(XB[kc][:, t * P:(t + 1) * P], xn[:, t, kc * P:(kc + 1) * P],
                                                   ident[:])
                    last.then_inc(s_tx, 1)
                pe.wait_ge(s_xT, n * 2 + 2)
                for t in range(NT):
                    for kc in range(2):
                        last = mm(LG[:, t * E:(t + 1) * E], xT[:, kc, t * P:(t + 1) * P], rw[:, kc, :],
                                  start=(kc == 0), stop=(kc == 1))
                last.then_inc(s_lg, 1)

                def experts(t):
                    for j in range(4):
                        if t >= 1:
                            pe.wait_ge(s_acc, n * NT * ACCS + (t - 1) * ACCS + 2 * j + 3)
                        for kc in range(2):
                            last = mm(Y[j][:], xT[:, kc, t * P:(t + 1) * P], ew[:, kc, 2 * j:2 * j + 2, :],
                                      start=(kc == 0), stop=(kc == 1))
                        last.then_inc(s_y[j], 1)

                def bias(t):
                    if t >= 1:
                        pe.wait_ge(s_acc, n * NT * ACCS + (t - 1) * ACCS + 1)
                    mm(BI[:, 0:C], coefT[:, t, :], eb[:], start=True, stop=True).then_inc(s_bi, 1)

                experts(0)
                pe.wait_ge(s_route, n * ROUTE + 10)
                for t in range(NT):
                    last = nc.tensor.transpose(LG[0:E, t * P:(t + 1) * P], coef[:, t, :], ident[:])
                last.then_inc(s_tc, 1)
                pe.wait_ge(s_route, (n + 1) * ROUTE)
                bias(0)
                for t in range(1, NT):
                    experts(t)
                    bias(t)
def landmark_attention(nc, X, stats, ident, w):
    with ExitStack() as ctx:
        sb = lambda name, shape, dt=fp32: ctx.enter_context(nc.sbuf_tensor("b_" + name, shape, dt))
        sem = lambda name: ctx.enter_context(nc.semaphore("b_" + name))

        M = 64
        HH, H8 = 2, 8
        NS = H // 2
        AW = P + HD
        ITERS = 6
        GROUPS = [(0, 3), (3, 6), (6, 8)]
        NU = 2 * NS

        wq = sb("wq", [P, 2, 3 * C])
        wp = sb("wp", [P, 2, C])
        hmask = sb("hmask", [P, H8])
        bones = sb("bones", [P, P])
        rstd = sb("rstd", [P, B * NT])
        mean = sb("mean", [P, B * NT])
        scr = sb("scr", [P, 4, B * NT])

        xn = sb("xn", [P, NT, C])
        xT = sb("xT", [P, 2, T])
        qT = sb("qT", [P, HH, T])
        kT = sb("kT", [P, HH, T])
        vv = sb("vv", [P, NT, C])
        lsum = sb("lsum", [P, 4, M])
        klm = sb("klm", [P, HH, M])
        bdQ = sb("bdQ", [P, HH, H8, M])
        bdKl = sb("bdKl", [P, HH, H8, M])
        k2 = sb("k2", [P, NS, M])
        k2max = sb("k2max", [P, NS])
        k2sum = sb("k2sum", [P, NS])
        bdK2 = sb("bdK2", [P, NS, P])
        k2T = sb("k2T", [P, NS, P])
        dmax = sb("dmax", [P, NS])
        dinv = sb("dinv", [P, NS])
        aw = sb("aw", [P, NS, AW])
        aw3 = sb("aw3", [P, NS, AW])
        rq = sb("rq", [P, NS, AW])
        uq = sb("uq", [P, NS, AW])
        tm = sb("tm", [P, NS, AW])
        zbd = sb("zbd", [P, NS, 2 * HD])
        smax = sb("smax", [P, 2, H8])
        sh = sb("sh", [P, 2, T])
        pr = sb("pr", [P, 2, T])
        esum = sb("esum", [P, NU, H8])
        p3T = sb("p3T", [P, 2, NT, P])
        p1T = sb("p1T", [P, NS, T])
        svT = sb("svT", [P, HH, T])

        bank = [ctx.enter_context(nc.psum_tensor(f"b_bank{i}", [P, 512], fp32)) for i in range(8)]
        S, TB, I, G = bank[0:2], bank[2], bank[3:6], bank[6:8]

        ORDER = ["xT0", "xT1", "q0", "k0", "q1", "k1", "S2", "v0", "v1", "score0", "score1", "turn0"]
        mid = {2: ["d0", "d1"], 3: ["kT0", "kT1"], 4: ["A0", "A1"]}
        for u in range(2, NS):
            ORDER += [f"score{u}"] + mid.get(u, []) + [f"turn{u - 1}", f"w{u - 2}"]
        ORDER += [f"turn{NS - 1}", f"w{NS - 2}", f"w{NS - 1}"]
        u = NS
        for i in range(ITERS):
            for half in ("R", "N"):
                ORDER += [f"{half}{i}.{g}" for g in range(len(GROUPS))]
                if u < NU:
                    ORDER += [f"score{u}"]
                if NS + 1 < u <= NU + 1:
                    ORDER += [f"turn{u - 2}"]
                u += 1
        ORDER += ["Z", "sv0", "sv1"] + [f"pj{t}" for t in range(NT)]
        USES = [o for o in ORDER if not o.startswith(("score", "turn", "R", "N"))]
        PER = [(len(USES) + 1) // 2, len(USES) // 2]

        s_const = sem("const_loaded")
        s_zero = sem("zeroed")
        s_var = sem("variance")
        s_sqrt = sem("sqrt_done")
        s_batch = sem("batch_done")
        s_xn = sem("xn_ready")
        s_lm = sem("landmark_steps")
        s_k2e = sem("kernel2_exp")
        s_k2 = sem("kernel2_steps")
        s_dinv = sem("dinv_steps")
        s_full = [sem("g_full0"), sem("g_full1")]
        s_empty = [sem("g_empty0"), sem("g_empty1")]
        s_scores = sem("scores_ready")
        s_max = sem("row_max")
        s_sh = sem("scores_shifted")
        s_exp = sem("exp_done")
        s_es = sem("exp_sum_steps")
        s_norm = sem("probs_normalised")
        s_tp = sem("probs_transposed")
        s_pT = sem("pT_ready")
        s_rinv = sem("kernel3_sum_inverse")
        s_sq = sem("square_done")
        s_rq = sem("square_copied")
        s_uq = sem("uq_ready")
        s_pd = sem("product_done")
        s_aw3 = sem("aw3_ready")
        s_tm = sem("tm_ready")
        s_aw = sem("aw_ready")

        def g(name):
            i = USES.index(name)
            return i % 2, i // 2

        def full(eng, n, name):
            b, k = g(name)
            eng.wait_ge(s_full[b], n * PER[b] + k + 1)
            return G[b]

        def filled(ins, name):
            ins.then_inc(s_full[g(name)[0]], 1)

        def emptied(ins, name):
            ins.then_inc(s_empty[g(name)[0]], 1)

        def out_of(eng, n, name):
            b, k = g(name)
            eng.wait_ge(s_empty[b], n * PER[b] + k + 2)

        def out_of_all(eng, n, names, claimed=None):
            for b in range(2):
                ks = [g(x)[1] for x in names if g(x)[0] == b]
                if ks and (claimed is None or g(claimed)[0] != b):
                    eng.wait_ge(s_empty[b], n * PER[b] + max(ks) + 2)

        def claim(pe, n, name):
            b, k = g(name)
            pe.wait_ge(s_empty[b], n * PER[b] + k + 1)
            return G[b]

        def step(n, i, gr):
            return n * ITERS * 3 + i * 3 + gr + 1

        LOADS = 16 * 4
        block = ctx.enter_context(nc.Block())

        @block.sync
        def _(sp):
            for dst, src in [(wq[:], w["b_w_qkv"].rearrange("(k p) n -> p k n", p=P)),
                             (wp[:], w["b_w_proj"].rearrange("(k p) n -> p k n", p=P)),
                             (hmask[:], w["headmask"]), (bones[:], w["blockones"])]:
                sp.dma_start(dst, src).then_inc(s_const, 16)

        @block.gpsimd
        def _(pool):
            nc.gpsimd.memset(bdK2[:], 0.0).then_inc(s_zero, 1)
            nc.gpsimd.memset(zbd[:], 0.0).then_inc(s_zero, 1)
            with pool.Fori(0, B) as n:
                for u in range(NS, NU):
                    pool.wait_ge(s_es, n * 2 * NS + 2 * (u - NS) + 2)
                    p = pr[:, u % 2].rearrange("p (h m) -> p h m", m=M)
                    nc.gpsimd.tensor_tensor(out=p, in0=p, in1=esum[:, u, :].unsqueeze(2).broadcast_to([P, H8, M]),
                                            op=ALU.mult).then_inc(s_norm, 1)
                pool.wait_ge(s_norm, (n + 1) * NS)
                pool.nop(nofuse=True)

        def rinv(dve, n, s):
            dve.wait_ge(s_exp, n * NU + s + 1)
            nc.vector.reciprocal(esum[:, s, 1:2], esum[:, s, 0:1]).then_inc(s_rinv, 1)

        def sums(dve, n, u):
            v = u - NS
            dve.wait_ge(s_exp, n * NU + u + 1)
            nc.vector.tensor_reduce(out=smax[:, u % 2, :], in_=pr[:, u % 2].rearrange("p (h m) -> p h m", m=M),
                                    axis=AX.X, op=ALU.add).then_inc(s_es, 1)
            dve.wait_ge(s_es, n * 2 * NS + 2 * v + 1)
            nc.vector.reciprocal(esum[:, u, :], smax[:, u % 2, :]).then_inc(s_es, 1)
            dve.wait_ge(s_es, n * 2 * NS + 2 * v + 2)

        @block.vector
        def _(dve):
            ln_rstd(nc, dve, stats, mean, rstd, scr, s_var, s_sqrt)
            dve.wait_ge(s_const, LOADS)
            dve.wait_ge(s_zero, 2)
            V = nc.vector
            with dve.Fori(0, B) as n:
                dve.wait_ge(s_batch, n + 1)
                for t in range(NT):
                    tt = n * NT + t
                    V.tensor_scalar(xn[:, t, :], X[:, bass.ds(tt, 1), :], mean[:, bass.ds(tt, 1)],
                                    rstd[:, bass.ds(tt, 1)], ALU.subtract, ALU.mult).then_inc(s_xn, 1)
                lm = 0
                for item in ORDER:
                    if item[0] in "qk" and item[1].isdigit():
                        isk, hh = item[0] == "k", int(item[1])
                        src, dst = (kT, bdKl) if isk else (qT, bdQ)
                        ls = lsum[:, 2 * isk + hh, :]
                        out_of(dve, n, item)
                        V.tensor_reduce(out=ls, in_=src[:, hh, :].rearrange("p (m j) -> p m j", j=T // M),
                                        axis=AX.X, op=ALU.add).then_inc(s_lm, 1)
                        lm += 1
                        dve.wait_ge(s_lm, n * 10 + lm)
                        if isk:
                            V.tensor_scalar(klm[:, hh, :], ls, M / T, None, ALU.mult).then_inc(s_lm, 1)
                            lm += 1
                        V.scalar_tensor_tensor(
                            out=dst[:, hh], in0=ls.unsqueeze(1).broadcast_to([P, H8, M]), scalar=M / T,
                            in1=hmask[:].unsqueeze(2).broadcast_to([P, H8, M]),
                            op0=ALU.mult, op1=ALU.mult).then_inc(s_lm, 1)
                        lm += 1
                    elif item == "S2":
                        gb = full(dve, n, item)
                        s2 = gb[:].rearrange("p (s m) -> p s m", m=M)
                        V.tensor_reduce(out=k2max[:], in_=s2, axis=AX.X, op=ALU.max).then_inc(s_k2, 1)
                        dve.wait_ge(s_k2, n * 5 + 1)
                        emptied(V.tensor_tensor(out=k2[:], in0=s2,
                                                in1=k2max[:].unsqueeze(2).broadcast_to([P, NS, M]),
                                                op=ALU.subtract), item)
                    elif item == "v1":
                        dve.wait_ge(s_k2e, n + 1)
                        V.tensor_reduce(out=k2sum[:], in_=k2[:], axis=AX.X, op=ALU.add).then_inc(s_k2, 1)
                        dve.wait_ge(s_k2, n * 5 + 2)
                        V.reciprocal(k2max[:], k2sum[:]).then_inc(s_k2, 1)
                        dve.wait_ge(s_k2, n * 5 + 3)
                        for e in range(2):
                            r = slice(64 * e, 64 * e + 64)
                            V.tensor_tensor(out=bdK2[r, :, 64 * e:64 * e + 64], in0=k2[r],
                                            in1=k2max[r, :].unsqueeze(2).broadcast_to([64, NS, M]),
                                            op=ALU.mult).then_inc(s_k2, 1)
                    elif item in ("d0", "d1"):
                        j = int(item[1])
                        gb = full(dve, n, item)
                        emptied(V.tensor_reduce(out=dmax[:, 4 * j:4 * j + 4],
                                                in_=gb[:].rearrange("p (s m) -> p s m", m=P),
                                                axis=AX.X, op=ALU.max), item)
                        if j == 1:
                            out_of_all(dve, n, ["d0", "d1"])
                            V.reciprocal(dinv[:], dmax[:]).then_inc(s_dinv, 1)
                    elif item in ("A0", "A1"):
                        j = int(item[1])
                        gb = full(dve, n, item)
                        dve.wait_ge(s_dinv, n + 1)
                        emptied(V.tensor_tensor(
                            out=aw[:, 4 * j:4 * j + 4, 0:P], in0=gb[:].rearrange("p (s m) -> p s m", m=P),
                            in1=dinv[:, 4 * j:4 * j + 4].unsqueeze(2).broadcast_to([P, 4, P]), op=ALU.mult), item)
                    elif item.startswith("score"):
                        u = int(item[5:])
                        dve.wait_ge(s_scores, n * NU + u + 1)
                        if u < NS:
                            V.tensor_reduce(out=smax[:, u % 2, 0:1], in_=S[u % 2][:], axis=AX.X, op=ALU.max,
                                            negate=True).then_inc(s_max, 1)
                        else:
                            sc = S[u % 2][:].rearrange("p (h m) -> p h m", m=M)
                            V.tensor_reduce(out=smax[:, u % 2, :], in_=sc, axis=AX.X, op=ALU.max)\
                             .then_inc(s_max, 1)
                            dve.wait_ge(s_max, n * NU + u + 1)
                            if u >= NS + 2:
                                dve.wait_ge(s_exp, n * NU + u - 1)
                            V.tensor_tensor(out=sh[:, u % 2].rearrange("p (h m) -> p h m", m=M), in0=sc,
                                            in1=smax[:, u % 2, :].unsqueeze(2).broadcast_to([P, H8, M]),
                                            op=ALU.subtract).then_inc(s_sh, 1)
                            if u > NS:
                                sums(dve, n, u - 1)
                    elif item[0] == "w":
                        s = int(item[1:])
                        rinv(dve, n, s)
                        gb = full(dve, n, item)
                        dve.wait_ge(s_rinv, n * NS + s + 1)
                        emptied(V.tensor_scalar(aw[:, s, P:AW], gb[:, 0:HD], esum[:, s, 1:2], None, ALU.mult), item)
                    elif item[0] == "R":
                        i, gr = int(item[1]), int(item[3])
                        a, b = GROUPS[gr]
                        k = slice(0, AW) if i < ITERS - 1 else slice(P, AW)
                        dve.wait_ge(s_rq, step(n, i, gr))
                        V.scalar_tensor_tensor(out=uq[:, a:b, k], in0=aw[:, a:b, k], scalar=1.75,
                                               in1=rq[:, a:b, k], op0=ALU.mult, op1=ALU.subtract)\
                         .then_inc(s_uq, 1)
                        dve.wait_ge(s_aw3, step(n, i, gr))
                        V.scalar_tensor_tensor(out=tm[:, a:b, k], in0=rq[:, a:b, k], scalar=-15.0,
                                               in1=aw3[:, a:b, k], op0=ALU.mult, op1=ALU.add).then_inc(s_tm, 1)
                    elif item[0] == "N":
                        i, gr = int(item[1]), int(item[3])
                        a, b = GROUPS[gr]
                        k = slice(0, AW) if i < ITERS - 1 else slice(P, AW)
                        dve.wait_ge(s_tm, step(n, i, gr))
                        dve.wait_ge(s_pd, step(n, i, gr))
                        V.scalar_tensor_tensor(
                            out=aw[:, a:b, k],
                            in0=I[gr][:, 0:(b - a) * AW].rearrange("p (s m) -> p s m", m=AW)[:, :, k],
                            scalar=4.0, in1=tm[:, a:b, k], op0=ALU.mult, op1=ALU.add).then_inc(s_aw, 1)
                    elif item == "Z":
                        gb = full(dve, n, item)
                        for e in range(2):
                            r = slice(64 * e, 64 * e + 64)
                            last = V.tensor_tensor(
                                out=zbd[r, :, HD * e:HD * e + HD],
                                in0=gb[r, 0:NS * HD].rearrange("p (s d) -> p s d", d=HD),
                                in1=dinv[r, :].unsqueeze(2).broadcast_to([64, NS, HD]), op=ALU.mult)
                        emptied(last, item)
                    elif item.startswith("pj"):
                        t = int(item[2])
                        gb = full(dve, n, item)
                        x = X[:, bass.ds(n * NT + t, 1), :]
                        emptied(V.tensor_tensor(out=x, in0=x, in1=gb[:, 0:C].unsqueeze(1), op=ALU.add), item)
                        out_of(dve, n, item)
                        dve.nop(nofuse=True)
                        last = V.bn_stats(stats[:, bass.ds(n * NT + t, 1), :], x)
                        if t == NT - 1:
                            last.then_inc(s_batch, 1)
                    if item == f"score{NU - 1}":
                        sums(dve, n, NU - 1)

        @block.scalar
        def _(act):
            ln_sqrt(nc, act, scr, s_var, s_sqrt)
            A = nc.scalar.activation
            with act.Fori(0, B) as n:
                for item in ORDER:
                    if item[:2] == "xT":
                        emptied(A(xT[:, int(item[2]), :], full(act, n, item)[:], ACT.Copy), item)
                    elif item[0] == "q":
                        emptied(A(qT[:, int(item[1]), :], full(act, n, item)[:], ACT.Copy,
                                  scale=float(HD) ** -0.5), item)
                    elif item in ("k0", "k1"):
                        emptied(A(kT[:, int(item[1]), :], full(act, n, item)[:], ACT.Copy), item)
                    elif item in ("v0", "v1"):
                        if item == "v0":
                            out_of(act, n, "S2")
                            A(k2[:], k2[:], ACT.Exp).then_inc(s_k2e, 1)
                        j = 2 * int(item[1])
                        emptied(A(vv[:, j:j + 2, :], full(act, n, item)[:].rearrange("p (t c) -> p t c", t=2),
                                  ACT.Copy), item)
                    elif item in ("kT0", "kT1"):
                        j = 4 * int(item[2])
                        emptied(A(k2T[:, j:j + 4, :], full(act, n, item)[:].rearrange("p (s m) -> p s m", m=P),
                                  ACT.Copy), item)
                    elif item.startswith("score"):
                        u = int(item[5:])
                        if u >= 2:
                            act.wait_ge(s_tp, n * NU + u - 1)
                        if u < NS:
                            act.wait_ge(s_max, n * NU + u + 1)
                            A(pr[:, u % 2], S[u % 2][:], ACT.Exp, bias=smax[:, u % 2, 0:1],
                              accum_out=esum[:, u, 0:1]).then_inc(s_exp, 1)
                        else:
                            act.wait_ge(s_sh, n * NS + u - NS + 1)
                            A(pr[:, u % 2], sh[:, u % 2], ACT.Exp).then_inc(s_exp, 1)
                    elif item.startswith("turn"):
                        u = int(item[4:])
                        act.wait_ge(s_tp, n * NU + u + 1)
                        tb = TB[:].rearrange("p (j q) -> p j q", j=4)
                        if u < NS:
                            if u >= 2:
                                b, k = g(f"w{u - 2}")
                                act.wait_ge(s_full[b], n * PER[b] + k + 1)
                            A(p3T[:, u % 2], tb, ACT.Copy).then_inc(s_pT, 1)
                        else:
                            t, hh = (u - NS) // 2, (u - NS) % 2
                            A(p1T[:, 4 * hh:4 * hh + 4, t * P:(t + 1) * P], tb, ACT.Copy).then_inc(s_pT, 1)
                    elif item[0] == "R":
                        i, gr = int(item[1]), int(item[3])
                        a, b = GROUPS[gr]
                        if i == 0 and gr == 0:
                            out_of_all(act, n, ["A0", "A1"] + [f"w{s}" for s in range(NS)])
                        k = slice(0, AW) if i < ITERS - 1 else slice(P, AW)
                        if i > 0:
                            act.wait_ge(s_aw, step(n, i - 1, gr))
                        A(aw3[:, a:b, k], aw[:, a:b, k], ACT.Copy, scale=3.25).then_inc(s_aw3, 1)
                        act.wait_ge(s_sq, step(n, i, gr))
                        A(rq[:, a:b, :], I[gr][:, 0:(b - a) * AW].rearrange("p (s m) -> p s m", m=AW), ACT.Copy,
                          scale=0.25).then_inc(s_rq, 1)
                    elif item[:2] == "sv":
                        emptied(A(svT[:, int(item[2]), :], full(act, n, item)[:], ACT.Copy), item)

        @block.tensor
        def _(pe):
            mm = nc.tensor.matmul
            for sm in (s_empty[0], s_empty[1], s_batch):
                pe.sem_inc(sm, 1)
            pe.wait_ge(s_const, LOADS)
            pe.wait_ge(s_zero, 2)
            with pe.Fori(0, B) as n:
                for item in ORDER:
                    gb = claim(pe, n, item) if item in USES else None
                    if item[:2] == "xT":
                        kc = int(item[2])
                        for t in range(NT):
                            if kc == 0:
                                pe.wait_ge(s_xn, n * NT + t + 1)
                            last = nc.tensor.transpose(gb[:, t * P:(t + 1) * P], xn[:, t, kc * P:(kc + 1) * P],
                                                       ident[:])
                    elif item in ("q0", "q1", "k0", "k1"):
                        blk = 2 * (item[0] == "k") + int(item[1])
                        if item == "q0":
                            out_of_all(pe, n, ["xT0", "xT1"], item)
                        for kc in range(2):
                            last = mm(gb[:], wq[:, kc, blk * P:(blk + 1) * P], xT[:, kc, :],
                                      start=(kc == 0), stop=(kc == 1))
                    elif item in ("v0", "v1"):
                        for j in range(2):
                            t = 2 * int(item[1]) + j
                            for kc in range(2):
                                last = mm(gb[:, j * C:(j + 1) * C], xT[:, kc, t * P:(t + 1) * P],
                                          wq[:, kc, 2 * C:3 * C], start=(kc == 0), stop=(kc == 1))
                    elif item == "S2":
                        pe.wait_ge(s_lm, (n + 1) * 10)
                        for s in range(NS):
                            hh, h0 = s // 4, 2 * (s % 4)
                            last = mm(gb[:, s * M:(s + 1) * M], bdQ[:, hh, h0:h0 + 2, :], klm[:, hh, :],
                                      start=True, stop=True)
                    elif item in ("d0", "d1"):
                        j = int(item[1])
                        pe.wait_ge(s_k2, n * 5 + 5)
                        last = mm(gb[:], bones[:], bdK2[:, 4 * j:4 * j + 4, :], start=True, stop=True)
                    elif item in ("kT0", "kT1"):
                        for j in range(4):
                            s = 4 * int(item[2]) + j
                            last = nc.tensor.transpose(gb[:, j * P:(j + 1) * P], bdK2[:, s, :], ident[:])
                    elif item in ("A0", "A1"):
                        out_of_all(pe, n, [f"kT{item[1]}"], item)
                        for j in range(4):
                            s = 4 * int(item[1]) + j
                            last = mm(gb[:, j * P:(j + 1) * P], k2T[:, s, :], k2T[:, s, :], start=True, stop=True)
                    elif item.startswith("score"):
                        u = int(item[5:])
                        if 2 <= u < NS + 2:
                            pe.wait_ge(s_exp, n * NU + u - 1)
                        elif u >= NS + 2:
                            pe.wait_ge(s_sh, n * NS + u - NS - 1)
                        if u < NS:
                            hh, h0 = u // 4, 2 * (u % 4)
                            last = mm(S[u % 2][:], bdQ[:, hh, h0:h0 + 2, :], kT[:, hh, :], start=True, stop=True)
                        else:
                            t, hh = (u - NS) // 2, (u - NS) % 2
                            last = mm(S[u % 2][:], qT[:, hh, t * P:(t + 1) * P], bdKl[:, hh], start=True, stop=True)
                        last.then_inc(s_scores, 1)
                    elif item.startswith("turn"):
                        u = int(item[4:])
                        if u < NS:
                            pe.wait_ge(s_exp, n * NU + u + 1)
                        else:
                            pe.wait_ge(s_norm, n * NS + u - NS + 1)
                        if u >= 1:
                            pe.wait_ge(s_pT, n * NU + u)
                        for j in range(4):
                            last = nc.tensor.transpose(TB[:, j * P:(j + 1) * P], pr[:, u % 2, j * P:(j + 1) * P],
                                                       ident[:])
                        last.then_inc(s_tp, 1)
                    elif item[0] == "w":
                        s = int(item[1:])
                        pe.wait_ge(s_pT, n * NU + s + 1)
                        if s == 0:
                            out_of_all(pe, n, ["v0", "v1"], item)
                        for t in range(NT):
                            for j in range(4):
                                hd = 2 * s + j // 2
                                last = mm(gb[32 * j:32 * j + 32, 0:HD], p3T[:, s % 2, t, 32 * j:32 * j + 32],
                                          vv[:, t, hd * HD:(hd + 1) * HD], start=(t == 0), stop=(t == NT - 1))
                    elif item[0] == "R":
                        i, gr = int(item[1]), int(item[3])
                        if i == 0 and gr == 0:
                            out_of_all(pe, n, ["A0", "A1"] + [f"w{s}" for s in range(NS)])
                        if i > 0:
                            pe.wait_ge(s_aw, step(n, i - 1, gr))
                        a, b = GROUPS[gr]
                        for s in range(a, b):
                            last = mm(I[gr][:, (s - a) * AW:(s - a + 1) * AW], aw[:, s, 0:P], aw[:, s, :],
                                      start=True, stop=True)
                        last.then_inc(s_sq, 1)
                    elif item[0] == "N":
                        i, gr = int(item[1]), int(item[3])
                        a, b = GROUPS[gr]
                        k = 0 if i < ITERS - 1 else P
                        pe.wait_ge(s_uq, step(n, i, gr))
                        for s in range(a, b):
                            last = mm(I[gr][:, (s - a) * AW + k:(s - a + 1) * AW], rq[:, s, 0:P], uq[:, s, k:AW],
                                      start=True, stop=True)
                        last.then_inc(s_pd, 1)
                    elif item == "Z":
                        pe.wait_ge(s_aw, step(n, ITERS - 1, 2))
                        for s in range(NS):
                            last = mm(gb[:, s * HD:(s + 1) * HD], bdK2[:, s, :], aw[:, s, P:AW],
                                      start=True, stop=True)
                    elif item[:2] == "sv":
                        hh = int(item[2])
                        out_of_all(pe, n, ["Z"], item)
                        pe.wait_ge(s_pT, (n + 1) * NU)
                        for j in range(4):
                            last = mm(gb[32 * j:32 * j + 32, :], zbd[:, 4 * hh + j, :], p1T[:, 4 * hh + j, :],
                                      start=True, stop=True)
                    elif item[:2] == "pj":
                        t = int(item[2])
                        if t == 0:
                            out_of_all(pe, n, ["sv0", "sv1"], item)
                        for hh in range(HH):
                            last = mm(gb[:, 0:C], svT[:, hh, t * P:(t + 1) * P], wp[:, hh, :],
                                      start=(hh == 0), stop=(hh == 1))
                    if gb is not None:
                        filled(last, item)


def load_x(nc, x, X, stats, ident, identb):
    with ExitStack() as ctx:
        s_x = [ctx.enter_context(nc.semaphore(f"x_loaded{b}")) for b in range(B)]
        s_id = ctx.enter_context(nc.semaphore("identity"))
        block = ctx.enter_context(nc.Block())

        @block.sync
        def _(sp):
            xv = x.rearrange("b (t p) c -> b p t c", p=P)
            for b in range(B):
                sp.dma_start(X[:, b * NT:(b + 1) * NT, :], xv[b]).then_inc(s_x[b], 16)

        @block.gpsimd
        def _(pool):
            nc.gpsimd.memset(ident[:], 0.0).then_inc(s_id, 1)
            pool.wait_ge(s_id, 1)
            nc.gpsimd.affine_select(out=ident[:], in_=ident[:], compare_op=ALU.not_equal, fill=1.0, base=0,
                                    pattern=[[-1, P]], channel_multiplier=1).then_inc(s_id, 1)

        @block.vector
        def _(dve):
            dve.wait_ge(s_id, 2)
            nc.vector.tensor_copy(identb[:], ident[:])
            for b in range(B):
                dve.wait_ge(s_x[b], 16)
                for t in range(b * NT, (b + 1) * NT):
                    nc.vector.bn_stats(stats[:, t, :], X[:, t, :])


def store_x(nc, X, out):
    with ExitStack() as ctx:
        s_out = ctx.enter_context(nc.semaphore("x_stored"))
        block = ctx.enter_context(nc.Block())

        @block.sync
        def _(sp):
            ov = out.rearrange("b (t p) c -> b p t c", p=P)
            for b in range(B):
                sp.dma_start(ov[b], X[:, b * NT:(b + 1) * NT, :]).then_inc(s_out, 16)
            sp.wait_ge(s_out, 16 * B)


def build(nc, w, out, phases="AFBF"):
    with ExitStack() as ctx:
        X = ctx.enter_context(nc.sbuf_tensor("X", [P, B * NT, C], fp32))
        stats = ctx.enter_context(nc.sbuf_tensor("stats", [P, B * NT, 6], fp32))
        ident = ctx.enter_context(nc.sbuf_tensor("ident", [P, P], fp32))
        identb = ctx.enter_context(nc.sbuf_tensor("identb", [P, P], bf16))
        load_x(nc, w["x"], X, stats, ident, identb)
        for i, ph in enumerate(phases):
            if ph == "A":
                cluster_attention(nc, X, stats, ident, identb, w)
            elif ph == "F":
                moe_ffn(nc, X, stats, ident, w, i)
            elif ph == "B":
                landmark_attention(nc, X, stats, ident, w)
        store_x(nc, X, out)


def _tables():
    import math
    import numpy as np
    gs, ncl, per = 64, 64, 8
    pos = np.arange(ncl + gs, dtype=np.float32)[:, None]
    div = np.exp(np.arange(0, HD, 2, dtype=np.float32) * np.float32(-math.log(10000.0) / HD))
    ang = (pos * div).astype(np.float32)
    S = np.stack([np.sin(ang), np.cos(ang)], axis=-1).reshape(ncl + gs, HD).astype(np.float32)
    order = np.array([d // 2 + (HD // 2) * (d % 2) for d in range(HD)])
    R = S[:, order]
    dims = np.arange(P) % HD
    tabq = R[:gs][:, dims].T
    posk = (np.arange(T) // gs) * per + np.arange(T) % gs
    tabk = R[posk][:, dims].T
    tabc = R[:ncl][:, dims].T[:, None, :] * (np.arange(P)[:, None] // HD == np.arange(8)[None])[:, :, None]
    own16 = (np.arange(P)[:, None] // per == np.arange(32)[None]).astype(np.float32)
    row = np.arange(P)
    g = 2 * np.arange(NT)[None, :] + (row // gs)[:, None]
    col = np.arange(2 * gs)
    local = (col // gs)[None, :] == (row // gs)[:, None]
    seen = np.where(local[:, None, :], (col % gs)[None, None, :] <= (row % gs)[:, None, None],
                    (col % gs)[None, None, :] < (g * per)[:, :, None])
    maska = np.where(seen, 0.0, -1e30)
    f = lambda a: np.ascontiguousarray(a, dtype=np.float32)
    rank = np.broadcast_to(E - np.arange(E), (P, E))
    return {"rank": f(rank), "tabq": f(tabq), "tabk": f(tabk), "tabc": f(tabc), "own16": f(own16), "maska": f(maska),
            "headmask": f(np.arange(P)[:, None] // HD == np.arange(8)[None]),
            "blockones": f(np.arange(P)[:, None] // 64 == (np.arange(P)[None] // 64))}


def _layout(i):
    import numpy as np
    c = np.ascontiguousarray
    i = {k: np.asarray(v) for k, v in i.items()}
    return {"x": c(i["L0_attn_a_x"]),
            "a_w_attnT": c(i["L0_attn_a_w_attn"].T), "a_w_projT": c(i["L0_attn_a_w_proj"].T),
            "a_b_attn": c(i["L0_attn_a_b_attn"]), "a_bqk": c(i["L0_attn_a_b_attn"][:2 * C].reshape(4, P).T),
            "a_b_proj": c(i["L0_attn_a_b_proj"]), "a_w_assign": c(i["L0_attn_a_w_assign"]),
            "b_w_qkv": c(i["L0_attn_b_w_qkv"]), "b_w_proj": c(i["L0_attn_b_w_proj"]),
            "r_wT": c(i["L0_ffn_router_w"].T), "r_b": c(i["L0_ffn_router_b"]),
            "e_wT": c(i["L0_ffn_expert_w"].transpose(0, 2, 1)), "e_b": c(i["L0_ffn_expert_b"])}


def kernel(**inputs):
    import concourse.bacc as bacc
    from concourse.bass_utils import run_bass_kernel_spmd as run
    nc = bacc.Bacc("TRN2", target_bir_lowering=False, num_devices=1)
    arrays = {**_layout(inputs), **_tables()}
    w = {n: nc.dram_tensor(f"in_{n}", a.shape, mybir.dt.from_np(a.dtype), kind="ExternalInput").ap()
         for n, a in arrays.items()}
    out = nc.dram_tensor("out", (B, T, C), fp32, kind="ExternalOutput").ap()
    build(nc, w, out)
    r = run(nc, [{f"in_{n}": a for n, a in arrays.items()}], core_ids=[0])
    return r.results[0]["out"]
```

```python
import concourse.bass as bass
from concourse import mybir
from contextlib import ExitStack

fp32 = mybir.dt.float32
bf16 = mybir.dt.bfloat16
ALU = mybir.AluOpType
ACT = mybir.ActivationFunctionType
AX = mybir.AxisListType

P = 128
B, T, C = 8, 512, 256
H, HD = 16, 16
NT = T // P
E = 8
EPS = 1e-5


def steps(eng, step, body):
    def partial(n):
        for ahead, item in step:
            if 0 <= n + ahead < B:
                body(item, n + ahead, (n + ahead) % 2)

    partial(-2)
    partial(-1)
    with eng.Fori(0, B // 2 - 1) as j:
        for par in range(2):
            for ahead, item in step:
                body(item, j * 2 + (par + ahead), (par + ahead) % 2)
    partial(B - 2)
    partial(B - 1)


def wait_later(eng, sem, value):
    if not isinstance(value, int) or value >= 1:
        eng.wait_ge(sem, value)


class Uses:

    def __init__(self, banks, full, empty, names):
        self.banks, self.full, self.empty, self.names = banks, full, empty, names
        self.per = [len(names[i::len(banks)]) for i in range(len(banks))]

    def at(self, name):
        i = self.names.index(name)
        return i % len(self.banks), i // len(self.banks)

    def claim(self, pe, n, name):
        b, k = self.at(name)
        pe.wait_ge(self.empty[b], n * self.per[b] + (k + 1))
        return self.banks[b]

    def filled(self, ins, name):
        ins.then_inc(self.full[self.at(name)[0]], 1)

    def filled_bank(self, eng, n, name):
        b, k = self.at(name)
        eng.wait_ge(self.full[b], n * self.per[b] + (k + 1))
        return self.banks[b]

    def emptied(self, ins, name):
        ins.then_inc(self.empty[self.at(name)[0]], 1)

    def brought_out(self, eng, n, names, claimed=None):
        for b in range(len(self.banks)):
            ks = [self.at(x)[1] for x in names if self.at(x)[0] == b]
            if ks and (claimed is None or self.at(claimed)[0] != b):
                eng.wait_ge(self.empty[b], n * self.per[b] + (max(ks) + 2))


def ln_rstd(nc, dve, stats, mean, rstd, scr, s_var, s_sqrt):
    me, mo = stats[:, :, 1], stats[:, :, 4]
    half, dif, var, std = (scr[:, i, :] for i in range(4))
    tt = nc.vector.tensor_tensor
    tt(out=half, in0=me, in1=mo, op=ALU.add).then_inc(s_var, 1)
    tt(out=dif, in0=me, in1=mo, op=ALU.subtract).then_inc(s_var, 1)
    tt(out=var, in0=stats[:, :, 2], in1=stats[:, :, 5], op=ALU.add).then_inc(s_var, 1)
    dve.wait_ge(s_var, 3)
    nc.vector.tensor_scalar(mean[:], half, 0.5, None, ALU.mult).then_inc(s_var, 1)
    nc.vector.tensor_scalar(var, var, 1.0 / C, EPS, ALU.mult, ALU.add).then_inc(s_var, 1)
    nc.vector.tensor_scalar(dif, dif, 0.5, None, ALU.mult).then_inc(s_var, 1)
    dve.wait_ge(s_var, 6)
    tt(out=half, in0=dif, in1=dif, op=ALU.mult).then_inc(s_var, 1)
    dve.wait_ge(s_var, 7)
    tt(out=var, in0=var, in1=half, op=ALU.add).then_inc(s_var, 1)
    dve.wait_ge(s_sqrt, 1)
    nc.vector.reciprocal(rstd[:], std).then_inc(s_var, 1)
    dve.wait_ge(s_var, 9)
    tt(out=half, in0=rstd[:], in1=rstd[:], op=ALU.mult).then_inc(s_var, 1)
    dve.wait_ge(s_var, 10)
    tt(out=half, in0=half, in1=var, op=ALU.mult).then_inc(s_var, 1)
    dve.wait_ge(s_var, 11)
    nc.vector.tensor_scalar(half, half, -0.5, 1.5, ALU.mult, ALU.add).then_inc(s_var, 1)
    dve.wait_ge(s_var, 12)
    tt(out=rstd[:], in0=rstd[:], in1=half, op=ALU.mult).then_inc(s_var, 1)
    dve.wait_ge(s_var, 13)


def ln_sqrt(nc, act, scr, s_var, s_sqrt):
    act.wait_ge(s_var, 8)
    nc.scalar.activation(scr[:, 3, :], scr[:, 2, :], ACT.Sqrt).then_inc(s_sqrt, 1)


def cluster_attention(nc, X, stats, ident, w):
    with ExitStack() as ctx:
        sb = lambda name, shape, dt=fp32: ctx.enter_context(nc.sbuf_tensor("a_" + name, shape, dt))
        sem = lambda name: ctx.enter_context(nc.semaphore("a_" + name))

        GS = 64
        NCL = 64
        KEYS = GS + NCL
        HQ = 4
        UNITS = NT * (H // HQ)
        DV = HD + 1
        HH = 2
        H8 = H // HH
        RING = 4

        wqkT = sb("wqkT", [P, 2, 2 * C])
        wvT = sb("wvT", [P, 2, C])
        wpT = sb("wpT", [P, 2, C])
        bqk = sb("bqk", [P, 4])
        bv = sb("bv", [P, C])
        bp = sb("bp", [P, C])
        wassign = sb("wassign", [P, NT, C])
        tabq = sb("tabq", [P, GS])
        tabk = sb("tabk", [P, T])
        tabc = sb("tabc", [P, H8, NCL])
        own16 = sb("own16", [P, 32])
        mask = sb("mask", [P, NT, KEYS])
        rstd = sb("rstd", [P, B * NT])
        mean = sb("mean", [P, B * NT])
        scr = sb("scr", [P, 4, B * NT])

        xn = sb("xn", [P, NT, C])
        xT = sb("xT", [P, 2, T])
        dump = sb("dump", [P, C])
        logit = sb("logit", [P, NT])
        lrow = sb("lrow", [NT, T // NT])
        lmax = sb("lmax", [NT, 16])
        lexp = sb("lexp", [NT, T // NT])
        lsum = sb("lsum", [NT, 16])
        lw = sb("lw", [NT, T // NT])
        wsel = sb("wsel", [P, NT, 32])
        xbar = sb("xbar", [P, C])
        xbT = sb("xbT", [P, 2, 2, NCL])
        qT = sb("qT", [P, 2, HH, T])
        kT = sb("kT", [P, HH, T])
        bdK = sb("bdK", [P, 2, HH, H8, T])
        bdC = sb("bdC", [P, 2, HH, H8, NCL])
        cvb = sb("cvb", [P, C])
        V = [sb(f"V{e}", [P, 2, NT, H, DV]) for e in range(2)]
        smax = sb("smax", [P, RING, HQ])
        pr = sb("pr", [P, RING, HQ, KEYS])
        pT = sb("pT", [P, 2, HQ, P])
        rsum = sb("rsum", [P, 2, H])
        y = sb("y", [P, 2, C])
        yT = sb("yT", [P, 2, 2, P])

        bank = [ctx.enter_context(nc.psum_tensor(f"a_bank{i}", [P, 512], fp32)) for i in range(8)]
        S, TB, O, PB, MB = bank[0:2], bank[2:4], bank[4], bank[5:7], bank[7]

        PREP = ["xn", "lg", "xT0", "xT1", "lgT", "q0", "lexp", "k0", "k1", "lsum", "wT", "q1", "xb", "v0", "xbT",
                "ckv", "v1", "vcl"]
        LAG = 3

        def unit(kind, u):
            return (1 + u // UNITS, f"{kind}{u % UNITS}")

        STEP, prep = [], list(PREP)
        for u in range(UNITS):
            t = u // 4
            STEP += [unit("score", u + LAG + 1), unit("turn", u + 1), unit("exp", u + LAG), unit("weigh", u)]
            STEP += [(2, x) for x in prep[:1 + (u % 2)]]
            prep = prep[1 + (u % 2):]
            if u % 4 == 0:
                STEP += [(t > 0, f"yT{(t - 1) % NT}")]
            if u % 4 == 1:
                STEP += [(t > 0, f"pj{(t - 1) % NT}")]
            if u % 4 == 3:
                STEP += [(1, f"norm{t}")]
            if u + LAG + 1 == UNITS - 1:
                assert not prep

        s_const = sem("const_loaded")
        s_zero = sem("zeroed")
        s_var = sem("variance")
        s_sqrt = sem("sqrt_done")
        s_xn = sem("xn_ready")
        s_logit = sem("logit_ready")
        s_lexp = sem("logit_exp")
        s_lsum = sem("cluster_softmax_steps")
        s_lw = sem("cluster_weights")
        s_bdk = sem("bdk_ready")
        s_vc = sem("cluster_v_placed")
        s_bias = sem("x_biased")
        s_scores = sem("scores_ready")
        s_masked = sem("scores_masked")
        s_max = sem("row_max")
        s_sh = sem("scores_shifted")
        s_exp = sem("exp_done")
        s_tp = sem("probs_transposed")
        s_pT = sem("pT_ready")
        s_pv = sem("pv_done")
        s_rsum = sem("rsum_ready")
        s_y = sem("y_ready")

        used = [x for x in PREP if x not in ("xn", "lg", "lexp", "lsum", "vcl")]
        pre = Uses(PB, [sem("prep_full0"), sem("prep_full1")], [sem("prep_empty0"), sem("prep_empty1")], used)
        out = Uses([MB], [sem("main_full")], [sem("main_empty")], [f"{x}{t}" for t in range(NT) for x in ("yT", "pj")])

        LOADS = 16 * (11 + NT * 8)
        block = ctx.enter_context(nc.Block())

        @block.sync
        def _(sp):
            cw = w["a_w_attnT"]
            loads = [(wqkT[:], cw[:, 0:2 * C].rearrange("(k p) n -> p k n", p=P)),
                     (wvT[:], cw[:, 2 * C:3 * C].rearrange("(k p) n -> p k n", p=P)),
                     (wpT[:], w["a_w_projT"].rearrange("(k p) n -> p k n", p=P)),
                     (bqk[:], w["a_bqk"]),
                     (bv[:], w["a_b_attn"][2 * C:3 * C].partition_broadcast(P)),
                     (bp[:], w["a_b_proj"].partition_broadcast(P)),
                     (tabq[:], w["tabq"]), (tabk[:], w["tabk"]),
                     (tabc[:], w["tabc"]), (own16[:], w["own16"]), (mask[:], w["maska"])]
            for dst, src in loads:
                sp.dma_start(dst, src).then_inc(s_const, 16)
            per = P // 8
            for t in range(NT):
                for j in range(8):
                    sp.dma_start(wassign[j:P:8, t, :], w["a_w_assign"][t * per:(t + 1) * per, :])\
                      .then_inc(s_const, 16)
            sp.wait_ge(s_zero, 2)
            with sp.Fori(0, B // 2) as j:
                for par in range(2):
                    n = j * 2 + par
                    for hh in range(HH):
                        pre.brought_out(sp, n, [f"k{hh}"])
                        sp.nop(nofuse=True)
                        for h in range(H8):
                            sp.dma_start(bdK[h * HD:(h + 1) * HD, par, hh, h, :], kT[h * HD:(h + 1) * HD, hh, :])\
                              .then_inc(s_bdk, 16)
                    sp.wait_ge(s_bdk, (n + 1) * (H * 16))
                    sp.nop(nofuse=True)

        @block.gpsimd
        def _(pool):
            nc.gpsimd.memset(bdK[:], 0.0).then_inc(s_zero, 1)
            for e in range(2):
                last = nc.gpsimd.memset(V[e][:], 1.0)
            last.then_inc(s_zero, 1)
            pool.wait_ge(s_zero, 2)
            pool.wait_ge(s_const, LOADS)

            def body(item, n, par):
                if item == "xn":
                    pool.wait_ge(s_xn, (n + 1) * NT)
                    xb = X[:, bass.ds(n * NT, NT), :]
                    nc.gpsimd.tensor_tensor(out=xb, in0=xb, in1=bp[:].unsqueeze(1).broadcast_to([P, NT, C]),
                                            op=ALU.add).then_inc(s_bias, 1)
                    pool.wait_ge(s_bias, n + 1)
                    pool.nop(nofuse=True)
                elif item.startswith("score"):
                    u = int(item[5:])
                    pool.wait_ge(s_max, n * UNITS + (u + 1))
                    nc.gpsimd.tensor_tensor(
                        out=pr[:, u % RING], in0=pr[:, u % RING],
                        in1=smax[:, u % RING, :].unsqueeze(2).broadcast_to([P, HQ, KEYS]),
                        op=ALU.subtract).then_inc(s_sh, 1)
                    pool.wait_ge(s_sh, n * UNITS + (u + 1))
                    pool.nop(nofuse=True)

            steps(pool, STEP, body)

        @block.vector
        def _(dve):
            V_ = nc.vector
            ln_rstd(nc, dve, stats, mean, rstd, scr, s_var, s_sqrt)
            dve.wait_ge(s_const, LOADS)
            dve.wait_ge(s_zero, 2)

            def body(item, n, par):
                if item == "xn":
                    for t in range(NT):
                        tt = n * NT + t
                        V_.tensor_scalar(xn[:, t, :], X[:, bass.ds(tt, 1), :], mean[:, bass.ds(tt, 1)],
                                         rstd[:, bass.ds(tt, 1)], ALU.subtract, ALU.mult).then_inc(s_xn, 1)
                elif item == "lg":
                    for t in range(NT):
                        dve.wait_ge(s_xn, n * NT + (t + 1))
                        V_.tensor_tensor_reduce(
                            out=dump[:], in0=xn[:, t, :], in1=wassign[:, t, :], scale=1.0, scalar=0.0,
                            op0=ALU.mult, op1=ALU.add, accum_out=logit[:, t:t + 1]).then_inc(s_logit, 1)
                        dve.wait_ge(s_logit, n * NT + (t + 1))
                elif item == "lgT":
                    row = pre.filled_bank(dve, n, item)[0:NT, 0:P].rearrange("t (c j) -> t c j", j=8)
                    V_.tensor_reduce(out=lmax[:], in_=row, axis=AX.X, op=ALU.max).then_inc(s_lsum, 1)
                    dve.wait_ge(s_lsum, n * 3 + 1)
                    pre.emptied(V_.tensor_tensor(
                        out=lrow[:].rearrange("t (c j) -> t c j", j=8), in0=row,
                        in1=lmax[:].unsqueeze(2).broadcast_to([NT, 16, 8]), op=ALU.subtract), item)
                elif item == "lsum":
                    ex = lexp[:].rearrange("t (c j) -> t c j", j=8)
                    dve.wait_ge(s_lexp, n + 1)
                    V_.tensor_reduce(out=lsum[:], in_=ex, axis=AX.X, op=ALU.add).then_inc(s_lsum, 1)
                    dve.wait_ge(s_lsum, n * 3 + 2)
                    V_.reciprocal(lmax[:], lsum[:]).then_inc(s_lsum, 1)
                    dve.wait_ge(s_lsum, n * 3 + 3)
                    V_.tensor_tensor(out=lw[:].rearrange("t (c j) -> t c j", j=8), in0=ex,
                                     in1=lmax[:].unsqueeze(2).broadcast_to([NT, 16, 8]), op=ALU.mult)\
                      .then_inc(s_lw, 1)
                elif item == "wT":
                    gb = pre.filled_bank(dve, n, item)
                    pre.emptied(V_.tensor_tensor(
                        out=wsel[:], in0=gb[:, 0:NT].unsqueeze(2).broadcast_to([P, NT, 32]),
                        in1=own16[:].unsqueeze(1).broadcast_to([P, NT, 32]), op=ALU.mult), item)
                elif item in ("q0", "q1"):
                    hh = int(item[1])
                    gb = pre.filled_bank(dve, n, item)
                    pre.emptied(V_.scalar_tensor_tensor(
                        out=qT[:, par, hh, :].rearrange("p (g j) -> p g j", j=GS),
                        in0=gb[:].rearrange("p (g j) -> p g j", j=GS), scalar=bqk[:, hh:hh + 1],
                        in1=tabq[:].unsqueeze(1).broadcast_to([P, T // GS, GS]), op0=ALU.add, op1=ALU.mult), item)
                elif item in ("k0", "k1"):
                    hh = int(item[1])
                    gb = pre.filled_bank(dve, n, item)
                    pre.emptied(V_.scalar_tensor_tensor(
                        out=kT[:, hh, :], in0=gb[:], scalar=bqk[:, 2 + hh:3 + hh], in1=tabk[:],
                        op0=ALU.add, op1=ALU.mult), item)
                elif item == "ckv":
                    gb = pre.filled_bank(dve, n, item)
                    for hh in range(HH):
                        V_.scalar_tensor_tensor(
                            out=bdC[:, par, hh],
                            in0=gb[:, hh * P:hh * P + NCL].unsqueeze(1).broadcast_to([P, H8, NCL]),
                            scalar=bqk[:, 2 + hh:3 + hh], in1=tabc[:], op0=ALU.add, op1=ALU.mult)
                    pre.emptied(V_.tensor_tensor(out=cvb[:], in0=gb[:, 256:512], in1=bv[:], op=ALU.add), item)
                elif item in ("v0", "v1"):
                    i = int(item[1])
                    gb = pre.filled_bank(dve, n, item)
                    for e in range(2):
                        r = slice(64 * e, 64 * e + 64)
                        last = V_.tensor_tensor(
                            out=V[e][r, par, 2 * i:2 * i + 2, :, 0:HD],
                            in0=gb[r, :].rearrange("p (t h d) -> p t h d", t=2, h=H),
                            in1=bv[r, :].rearrange("p (h d) -> p h d", h=H).unsqueeze(1)
                            .broadcast_to([64, 2, H, HD]), op=ALU.add)
                    pre.emptied(last, item)
                elif item.startswith("score"):
                    u = int(item[5:])
                    t = u // 4
                    dve.wait_ge(s_scores, n * UNITS + (u + 1))
                    wait_later(dve, s_tp, n * UNITS + (u - RING + 1))
                    V_.tensor_tensor(out=pr[:, u % RING], in0=S[u % 2][:].rearrange("p (h k) -> p h k", h=HQ),
                                     in1=mask[:, t, :].unsqueeze(1).broadcast_to([P, HQ, KEYS]), op=ALU.add)\
                      .then_inc(s_masked, 1)
                    dve.wait_ge(s_masked, n * UNITS + (u + 1))
                    V_.tensor_reduce(out=smax[:, u % RING, :], in_=pr[:, u % RING], axis=AX.X, op=ALU.max)\
                      .then_inc(s_max, 1)
                elif item.startswith("norm"):
                    t = int(item[4:])
                    dve.wait_ge(s_pv, n * UNITS + (4 * t + 4))
                    wait_later(dve, s_y, n * NT + (t - 1))
                    o = O[:, 0:H * DV].rearrange("p (h d) -> p h d", d=DV)
                    V_.reciprocal(rsum[:, t % 2, :], o[:, :, HD:DV]).then_inc(s_rsum, 1)
                    dve.wait_ge(s_rsum, n * NT + (t + 1))
                    V_.tensor_tensor(
                        out=y[:, t % 2, :].rearrange("p (h d) -> p h d", h=H), in0=o[:, :, 0:HD],
                        in1=rsum[:, t % 2, :].unsqueeze(2).broadcast_to([P, H, HD]), op=ALU.mult).then_inc(s_y, 1)
                elif item.startswith("pj"):
                    t = int(item[2:])
                    gb = out.filled_bank(dve, n, item)
                    if t == 0:
                        dve.wait_ge(s_bias, n + 1)
                    x = X[:, bass.ds(n * NT + t, 1), :]
                    out.emptied(V_.tensor_tensor(out=x, in0=x, in1=gb[:, 0:C].unsqueeze(1), op=ALU.add), item)
                    out.brought_out(dve, n, [item])
                    dve.nop(nofuse=True)
                    V_.bn_stats(stats[:, bass.ds(n * NT + t, 1), :], x)

            steps(dve, STEP, body)

        @block.scalar
        def _(act):
            ln_sqrt(nc, act, scr, s_var, s_sqrt)

            def body(item, n, par):
                if item in ("xT0", "xT1"):
                    gb = pre.filled_bank(act, n, item)
                    pre.emptied(nc.scalar.activation(xT[:, int(item[2]), :], gb[:], ACT.Copy), item)
                elif item == "lexp":
                    pre.brought_out(act, n, ["lgT"])
                    nc.scalar.activation(lexp[:], lrow[:], ACT.Exp).then_inc(s_lexp, 1)
                elif item == "xb":
                    gb = pre.filled_bank(act, n, item)
                    pre.emptied(nc.scalar.activation(xbar[:], gb[:, 0:C], ACT.Copy), item)
                elif item == "xbT":
                    gb = pre.filled_bank(act, n, item)
                    for kc in range(2):
                        for dup in range(2):
                            last = nc.scalar.activation(
                                xbT[:, kc, dup, :].rearrange("p (t c) -> p t c", t=NT),
                                gb[:, kc * P:(kc + 1) * P].rearrange("p (t c) -> p t c", t=NT)[:, :, 0:16],
                                ACT.Copy)
                    pre.emptied(last, item)
                elif item == "vcl":
                    pre.brought_out(act, n, ["ckv"])
                    for e, r in ((0, 64), (1, 0)):
                        nc.scalar.activation(
                            V[e][r:r + 64, par, :, :, 0:HD],
                            cvb[r:r + 64, :].rearrange("p (h d) -> p h d", h=H).unsqueeze(1)
                            .broadcast_to([64, NT, H, HD]), ACT.Copy).then_inc(s_vc, 1)
                elif item.startswith("exp"):
                    u = int(item[3:])
                    act.wait_ge(s_sh, n * UNITS + (u + 1))
                    nc.scalar.activation(pr[:, u % RING], pr[:, u % RING], ACT.Exp, scale=float(HD) ** -0.5)\
                      .then_inc(s_exp, 1)
                elif item.startswith("turn"):
                    u = int(item[4:])
                    act.wait_ge(s_tp, n * UNITS + (u + 1))
                    wait_later(act, s_pv, n * UNITS + (u - 1))
                    nc.scalar.activation(pT[:, u % 2], TB[u % 2][:].rearrange("p (h q) -> p h q", h=HQ),
                                         ACT.Copy).then_inc(s_pT, 1)
                elif item.startswith("yT"):
                    gb = out.filled_bank(act, n, item)
                    out.emptied(nc.scalar.activation(yT[:, int(item[2:]) % 2],
                                                     gb[:, 0:C].rearrange("p (k q) -> p k q", k=2), ACT.Copy), item)

            steps(act, STEP, body)

        @block.tensor
        def _(pe):
            mm = nc.tensor.matmul
            for sm in (*pre.empty, *out.empty):
                pe.sem_inc(sm, 1)
            pe.wait_ge(s_const, LOADS)
            pe.wait_ge(s_zero, 2)

            def body(item, n, par):
                gb = last = None
                if item in pre.names:
                    gb = pre.claim(pe, n, item)
                elif item in out.names:
                    gb = out.claim(pe, n, item)
                if item in ("xT0", "xT1"):
                    kc = int(item[2])
                    for t in range(NT):
                        if kc == 0:
                            pe.wait_ge(s_xn, n * NT + (t + 1))
                        last = nc.tensor.transpose(gb[:, t * P:(t + 1) * P], xn[:, t, kc * P:(kc + 1) * P], ident[:])
                elif item == "lgT":
                    pe.wait_ge(s_logit, (n + 1) * NT)
                    last = nc.tensor.transpose(gb[0:NT, 0:P], logit[:], ident[:])
                elif item in ("q0", "q1", "k0", "k1"):
                    blk = 2 * (item[0] == "k") + int(item[1])
                    pre.brought_out(pe, n, ["xT0", "xT1"], item)
                    for kc in range(2):
                        last = mm(gb[:], wqkT[:, kc, blk * P:(blk + 1) * P], xT[:, kc, :],
                                  start=(kc == 0), stop=(kc == 1))
                elif item == "wT":
                    pe.wait_ge(s_lw, n + 1)
                    pe.nop(nofuse=True)
                    last = nc.tensor.transpose(gb[:, 0:NT], lw[:], ident[0:NT, 0:NT])
                elif item == "xb":
                    pre.brought_out(pe, n, ["wT"], item)
                    for t in range(NT):
                        last = mm(gb[32 * t:32 * t + 32, 0:C], wsel[:, t, :], xn[:, t, :], start=True, stop=True)
                elif item == "xbT":
                    pre.brought_out(pe, n, ["xb"], item)
                    for kc in range(2):
                        last = nc.tensor.transpose(gb[:, kc * P:(kc + 1) * P], xbar[:, kc * P:(kc + 1) * P], ident[:])
                elif item == "ckv":
                    pre.brought_out(pe, n, ["xbT"], item)
                    for hh in range(HH):
                        for kc in range(2):
                            mm(gb[:, hh * P:(hh + 1) * P], wqkT[:, kc, (2 + hh) * P:(3 + hh) * P],
                               xbT[:, kc, :, :], start=(kc == 0), stop=(kc == 1))
                    for kc in range(2):
                        last = mm(gb[:, 256:512], xbT[:, kc, :, :], wvT[:, kc, :], start=(kc == 0), stop=(kc == 1))
                elif item in ("v0", "v1"):
                    for t in (2 * int(item[1]), 2 * int(item[1]) + 1):
                        for kc in range(2):
                            last = mm(gb[:, (t % 2) * C:(t % 2 + 1) * C], xT[:, kc, t * P:(t + 1) * P],
                                      wvT[:, kc, :], start=(kc == 0), stop=(kc == 1))
                elif item.startswith("score"):
                    u = int(item[5:])
                    t, hq = u // 4, u % 4
                    hh, h0 = hq // 2, (hq % 2) * HQ
                    if u == 0:
                        pre.brought_out(pe, n, ["q0", "q1", "ckv"])
                        pe.wait_ge(s_bdk, (n + 1) * (H * 16))
                    wait_later(pe, s_masked, n * UNITS + (u - 1))
                    s4 = S[u % 2][:].rearrange("p (h k) -> p h k", h=HQ)
                    hs = slice(h0, h0 + HQ)
                    for part in range(2):
                        for e in range(2):
                            r = slice(64 * e, 64 * e + 64)
                            q = slice(t * P + 64 * e, t * P + 64 * e + 64)
                            cols = slice(64 * ((part + e) % 2), 64 * ((part + e) % 2) + 64)
                            rhs = bdK[:, par, hh, hs, q] if part == 0 else bdC[:, par, hh, hs, :]
                            last = mm(s4[r, :, cols], qT[:, par, hh, q], rhs, start=True, stop=True)
                    last.then_inc(s_scores, 1)
                elif item.startswith("turn"):
                    u = int(item[4:])
                    pe.wait_ge(s_exp, n * UNITS + (u + 1))
                    wait_later(pe, s_pT, n * UNITS + (u - 1))
                    for h in range(HQ):
                        last = nc.tensor.transpose(TB[u % 2][:, h * P:(h + 1) * P], pr[:, u % RING, h, :], ident[:])
                    last.then_inc(s_tp, 1)
                elif item.startswith("weigh"):
                    u = int(item[5:])
                    t, hq = u // 4, u % 4
                    pe.wait_ge(s_pT, n * UNITS + (u + 1))
                    if u == 0:
                        pre.brought_out(pe, n, ["v0", "v1"])
                        pe.wait_ge(s_vc, n * 2 + 2)
                    if hq == 0:
                        wait_later(pe, s_y, n * NT + t)
                    for h in range(HQ):
                        for j in range(4):
                            hd = hq * HQ + h
                            last = mm(O[32 * j:32 * j + 32, hd * DV:(hd + 1) * DV],
                                      pT[:, u % 2, h, 32 * j:32 * j + 32], V[j // 2][:, par, t, hd, :],
                                      start=True, stop=True)
                    last.then_inc(s_pv, 1)
                elif item.startswith("yT"):
                    t = int(item[2:])
                    pe.wait_ge(s_y, n * NT + (t + 1))
                    for kc in range(2):
                        last = nc.tensor.transpose(gb[:, kc * P:(kc + 1) * P], y[:, t % 2, kc * P:(kc + 1) * P],
                                                   ident[:])
                elif item.startswith("pj"):
                    t = int(item[2:])
                    for kc in range(2):
                        last = mm(gb[:, 0:C], yT[:, t % 2, kc, :], wpT[:, kc, :], start=(kc == 0), stop=(kc == 1))
                if item in pre.names:
                    pre.filled(last, item)
                elif item in out.names:
                    out.filled(last, item)

            steps(pe, STEP, body)
def moe_ffn(nc, X, stats, ident, w, phase):
    with ExitStack() as ctx:
        sb = lambda name, shape, dt=fp32: ctx.enter_context(nc.sbuf_tensor(f"f{phase}_" + name, shape, dt))
        sem = lambda name: ctx.enter_context(nc.semaphore(f"f{phase}_" + name))

        rw = sb("rw", [P, 2, E])
        rb = sb("rb", [P, E])
        ew = sb("ew", [P, 2, E, C])
        eb = sb("eb", [E, C])
        rank = sb("rank", [P, E])
        rstd = sb("rstd", [P, B * NT])
        mean = sb("mean", [P, B * NT])
        scr = sb("scr", [P, 4, B * NT])
        xn = sb("xn", [P, NT, C])
        xT = sb("xT", [P, 2, T])
        lg = sb("lg", [P, NT, E])
        lmax = sb("lmax", [P, NT])
        sh = sb("sh", [P, NT, E])
        ex = sb("ex", [P, NT, E])
        first = sb("first", [P, NT, E])
        wt = sb("wt", [P, NT])
        best = sb("best", [P, NT])
        coef = sb("coef", [P, NT, E])
        coefT = sb("coefT", [E, NT, P])
        acc = sb("acc", [P, 2, C])

        bank = [ctx.enter_context(nc.psum_tensor(f"f{phase}_bank{i}", [P, 512], fp32)) for i in range(8)]
        XB, LG, BI, Y = bank[0:2], bank[2], bank[3], bank[4:8]

        s_const, s_var, s_sqrt = sem("const_loaded"), sem("variance"), sem("sqrt_done")
        s_batch = sem("batch_done")
        s_xn = sem("xn_ready")
        s_tx = sem("x_transposed")
        s_xT = sem("xT_ready")
        s_lg = sem("logits_done")
        s_route = sem("route_steps")
        s_ex = sem("exp_done")
        s_tc = sem("coef_transposed")
        s_bi = sem("bias_done")
        s_acc = sem("acc_steps")
        s_y = [sem(f"expert_pair{j}") for j in range(4)]
        LOADS = 16 * 6
        ROUTE, ACCS = 11, E + 1
        block = ctx.enter_context(nc.Block())

        @block.sync
        def _(sp):
            for dst, src in [(rw[:], w["r_wT"].rearrange("(k p) e -> p k e", p=P)),
                             (rb[:], w["r_b"].partition_broadcast(P)),
                             (eb[:], w["e_b"]), (rank[:], w["rank"])]:
                sp.dma_start(dst, src).then_inc(s_const, 16)
            for kc in range(2):
                sp.dma_start(ew[:, kc], w["e_wT"][:, kc * P:(kc + 1) * P, :].rearrange("e p o -> p e o"))\
                  .then_inc(s_const, 16)

        @block.vector
        def _(dve):
            ln_rstd(nc, dve, stats, mean, rstd, scr, s_var, s_sqrt)
            dve.wait_ge(s_const, LOADS)
            V = nc.vector
            TTE = [P, NT, E]
            with dve.Fori(0, B) as n:
                dve.wait_ge(s_batch, n + 1)
                for t in range(NT):
                    tt = n * NT + t
                    V.tensor_scalar(xn[:, t, :], X[:, bass.ds(tt, 1), :], mean[:, bass.ds(tt, 1)],
                                    rstd[:, bass.ds(tt, 1)], ALU.subtract, ALU.mult).then_inc(s_xn, 1)
                count = 0

                def step(ins):
                    nonlocal count
                    ins.then_inc(s_route, 1)
                    count += 1
                    dve.wait_ge(s_route, n * ROUTE + count)

                dve.wait_ge(s_lg, n + 1)
                step(V.tensor_tensor(out=lg[:], in0=LG[:, 0:NT * E].rearrange("p (t e) -> p t e", e=E),
                                     in1=rb[:].unsqueeze(1).broadcast_to(TTE), op=ALU.add))
                step(V.tensor_reduce(out=lmax[:], in_=lg[:], axis=AX.X, op=ALU.max))
                step(V.tensor_tensor(out=sh[:], in0=lg[:], in1=lmax[:].unsqueeze(2).broadcast_to(TTE),
                                     op=ALU.subtract))
                step(V.tensor_scalar(first[:], sh[:], 0.0, None, ALU.is_ge))
                step(V.tensor_tensor(out=first[:], in0=first[:], in1=rank[:].unsqueeze(1).broadcast_to(TTE),
                                     op=ALU.mult))
                step(V.tensor_reduce(out=best[:], in_=first[:], axis=AX.X, op=ALU.max))
                step(V.tensor_tensor(out=first[:], in0=first[:], in1=best[:].unsqueeze(2).broadcast_to(TTE),
                                     op=ALU.is_equal))
                dve.wait_ge(s_ex, n + 1)
                step(V.tensor_reduce(out=wt[:], in_=ex[:], axis=AX.X, op=ALU.add))
                step(V.reciprocal(best[:], wt[:]))
                step(V.tensor_tensor(out=coef[:], in0=first[:], in1=best[:].unsqueeze(2).broadcast_to(TTE),
                                     op=ALU.mult))
                dve.wait_ge(s_tc, n + 1)
                step(V.tensor_copy(coefT[:], LG[0:E, 0:NT * P].rearrange("e (t p) -> e t p", t=NT)))
                for t in range(NT):
                    a = acc[:, t % 2, :]
                    base = n * NT * ACCS + t * ACCS
                    dve.wait_ge(s_bi, n * NT + t + 1)
                    x = X[:, bass.ds(n * NT + t, 1), :]
                    V.tensor_tensor(out=a.unsqueeze(1), in0=x, in1=BI[:, 0:C].unsqueeze(1), op=ALU.add)\
                     .then_inc(s_acc, 1)
                    for e in range(E):
                        if e % 2 == 0:
                            dve.wait_ge(s_y[e // 2], n * NT + t + 1)
                        dve.wait_ge(s_acc, base + e + 1)
                        y = Y[e // 2][:, (e % 2) * C:(e % 2 + 1) * C]
                        if e == E - 1:
                            dve.nop(nofuse=True)
                        V.scalar_tensor_tensor(out=(x.squeeze(1) if e == E - 1 else a), in0=y,
                                               scalar=coef[:, t, e:e + 1], in1=a, op0=ALU.mult, op1=ALU.add)\
                         .then_inc(s_acc, 1)
                    dve.wait_ge(s_acc, base + ACCS)
                    dve.nop(nofuse=True)
                    last = V.bn_stats(stats[:, bass.ds(n * NT + t, 1), :], x)
                last.then_inc(s_batch, 1)

        @block.scalar
        def _(act):
            ln_sqrt(nc, act, scr, s_var, s_sqrt)
            with act.Fori(0, B) as n:
                for kc in range(2):
                    act.wait_ge(s_tx, n * 2 + kc + 1)
                    nc.scalar.activation(xT[:, kc, :], XB[kc][:], ACT.Copy).then_inc(s_xT, 1)
                act.wait_ge(s_route, n * ROUTE + 3)
                nc.scalar.activation(ex[:], sh[:], ACT.Exp).then_inc(s_ex, 1)

        @block.tensor
        def _(pe):
            mm = nc.tensor.matmul
            pe.sem_inc(s_batch, 1)
            pe.wait_ge(s_const, LOADS)
            with pe.Fori(0, B) as n:
                for kc in range(2):
                    for t in range(NT):
                        if kc == 0:
                            pe.wait_ge(s_xn, n * NT + t + 1)
                        last = nc.tensor.transpose(XB[kc][:, t * P:(t + 1) * P], xn[:, t, kc * P:(kc + 1) * P],
                                                   ident[:])
                    last.then_inc(s_tx, 1)
                pe.wait_ge(s_xT, n * 2 + 2)
                for t in range(NT):
                    for kc in range(2):
                        last = mm(LG[:, t * E:(t + 1) * E], xT[:, kc, t * P:(t + 1) * P], rw[:, kc, :],
                                  start=(kc == 0), stop=(kc == 1))
                last.then_inc(s_lg, 1)

                def experts(t):
                    for j in range(4):
                        if t >= 1:
                            pe.wait_ge(s_acc, n * NT * ACCS + (t - 1) * ACCS + 2 * j + 3)
                        for kc in range(2):
                            last = mm(Y[j][:], xT[:, kc, t * P:(t + 1) * P], ew[:, kc, 2 * j:2 * j + 2, :],
                                      start=(kc == 0), stop=(kc == 1))
                        last.then_inc(s_y[j], 1)

                def bias(t):
                    if t >= 1:
                        pe.wait_ge(s_acc, n * NT * ACCS + (t - 1) * ACCS + 1)
                    mm(BI[:, 0:C], coefT[:, t, :], eb[:], start=True, stop=True).then_inc(s_bi, 1)

                experts(0)
                pe.wait_ge(s_route, n * ROUTE + 10)
                for t in range(NT):
                    last = nc.tensor.transpose(LG[0:E, t * P:(t + 1) * P], coef[:, t, :], ident[:])
                last.then_inc(s_tc, 1)
                pe.wait_ge(s_route, (n + 1) * ROUTE)
                bias(0)
                for t in range(1, NT):
                    experts(t)
                    bias(t)
def landmark_attention(nc, X, stats, ident, w):
    with ExitStack() as ctx:
        sb = lambda name, shape, dt=fp32: ctx.enter_context(nc.sbuf_tensor("b_" + name, shape, dt))
        sem = lambda name: ctx.enter_context(nc.semaphore("b_" + name))

        M = 64
        HH, H8 = 2, 8
        NS = H // 2
        AW = P + HD
        ITERS = 6
        GROUPS = [(0, 3), (3, 6), (6, 8)]
        NU = 2 * NS

        wq = sb("wq", [P, 2, 3 * C])
        wp = sb("wp", [P, 2, C])
        hmask = sb("hmask", [P, H8])
        bones = sb("bones", [P, P])
        rstd = sb("rstd", [P, B * NT])
        mean = sb("mean", [P, B * NT])
        scr = sb("scr", [P, 4, B * NT])

        xn = sb("xn", [P, NT, C])
        xT = sb("xT", [P, 2, T])
        qT = sb("qT", [P, HH, T])
        kT = sb("kT", [P, HH, T])
        vv = sb("vv", [P, NT, C])
        lsum = sb("lsum", [P, 4, M])
        klm = sb("klm", [P, HH, M])
        bdQ = sb("bdQ", [P, HH, H8, M])
        bdKl = sb("bdKl", [P, HH, H8, M])
        k2 = sb("k2", [P, NS, M])
        k2max = sb("k2max", [P, NS])
        k2sum = sb("k2sum", [P, NS])
        bdK2 = sb("bdK2", [P, NS, P])
        k2T = sb("k2T", [P, NS, P])
        dmax = sb("dmax", [P, NS])
        dinv = sb("dinv", [P, NS])
        aw = sb("aw", [P, NS, AW])
        aw3 = sb("aw3", [P, NS, AW])
        rq = sb("rq", [P, NS, AW])
        uq = sb("uq", [P, NS, AW])
        tm = sb("tm", [P, NS, AW])
        zbd = sb("zbd", [P, NS, 2 * HD])
        smax = sb("smax", [P, 2, H8])
        sh = sb("sh", [P, 2, T])
        pr = sb("pr", [P, 2, T])
        esum = sb("esum", [P, NU, H8])
        p3T = sb("p3T", [P, 2, NT, P])
        p1T = sb("p1T", [P, NS, T])
        svT = sb("svT", [P, HH, T])

        bank = [ctx.enter_context(nc.psum_tensor(f"b_bank{i}", [P, 512], fp32)) for i in range(8)]
        S, TB, I, G = bank[0:2], bank[2], bank[3:6], bank[6:8]

        ORDER = ["xT0", "xT1", "q0", "k0", "q1", "k1", "S2", "v0", "v1", "score0", "score1", "turn0"]
        mid = {2: ["d0", "d1"], 3: ["kT0", "kT1"], 4: ["A0", "A1"]}
        for u in range(2, NS):
            ORDER += [f"score{u}"] + mid.get(u, []) + [f"turn{u - 1}", f"w{u - 2}"]
        ORDER += [f"turn{NS - 1}", f"w{NS - 2}", f"w{NS - 1}"]
        u = NS
        for i in range(ITERS):
            for half in ("R", "N"):
                ORDER += [f"{half}{i}.{g}" for g in range(len(GROUPS))]
                if u < NU:
                    ORDER += [f"score{u}"]
                if NS + 1 < u <= NU + 1:
                    ORDER += [f"turn{u - 2}"]
                u += 1
        ORDER += ["Z", "sv0", "sv1"] + [f"pj{t}" for t in range(NT)]
        USES = [o for o in ORDER if not o.startswith(("score", "turn", "R", "N"))]
        PER = [(len(USES) + 1) // 2, len(USES) // 2]

        s_const = sem("const_loaded")
        s_zero = sem("zeroed")
        s_var = sem("variance")
        s_sqrt = sem("sqrt_done")
        s_batch = sem("batch_done")
        s_xn = sem("xn_ready")
        s_lm = sem("landmark_steps")
        s_k2e = sem("kernel2_exp")
        s_k2 = sem("kernel2_steps")
        s_dinv = sem("dinv_steps")
        s_full = [sem("g_full0"), sem("g_full1")]
        s_empty = [sem("g_empty0"), sem("g_empty1")]
        s_scores = sem("scores_ready")
        s_max = sem("row_max")
        s_sh = sem("scores_shifted")
        s_exp = sem("exp_done")
        s_es = sem("exp_sum_steps")
        s_norm = sem("probs_normalised")
        s_tp = sem("probs_transposed")
        s_pT = sem("pT_ready")
        s_rinv = sem("kernel3_sum_inverse")
        s_sq = sem("square_done")
        s_rq = sem("square_copied")
        s_uq = sem("uq_ready")
        s_pd = sem("product_done")
        s_aw3 = sem("aw3_ready")
        s_tm = sem("tm_ready")
        s_aw = sem("aw_ready")

        def g(name):
            i = USES.index(name)
            return i % 2, i // 2

        def full(eng, n, name):
            b, k = g(name)
            eng.wait_ge(s_full[b], n * PER[b] + k + 1)
            return G[b]

        def filled(ins, name):
            ins.then_inc(s_full[g(name)[0]], 1)

        def emptied(ins, name):
            ins.then_inc(s_empty[g(name)[0]], 1)

        def out_of(eng, n, name):
            b, k = g(name)
            eng.wait_ge(s_empty[b], n * PER[b] + k + 2)

        def out_of_all(eng, n, names, claimed=None):
            for b in range(2):
                ks = [g(x)[1] for x in names if g(x)[0] == b]
                if ks and (claimed is None or g(claimed)[0] != b):
                    eng.wait_ge(s_empty[b], n * PER[b] + max(ks) + 2)

        def claim(pe, n, name):
            b, k = g(name)
            pe.wait_ge(s_empty[b], n * PER[b] + k + 1)
            return G[b]

        def step(n, i, gr):
            return n * ITERS * 3 + i * 3 + gr + 1

        LOADS = 16 * 4
        block = ctx.enter_context(nc.Block())

        @block.sync
        def _(sp):
            for dst, src in [(wq[:], w["b_w_qkv"].rearrange("(k p) n -> p k n", p=P)),
                             (wp[:], w["b_w_proj"].rearrange("(k p) n -> p k n", p=P)),
                             (hmask[:], w["headmask"]), (bones[:], w["blockones"])]:
                sp.dma_start(dst, src).then_inc(s_const, 16)

        @block.gpsimd
        def _(pool):
            nc.gpsimd.memset(bdK2[:], 0.0).then_inc(s_zero, 1)
            nc.gpsimd.memset(zbd[:], 0.0).then_inc(s_zero, 1)
            with pool.Fori(0, B) as n:
                for u in range(NS, NU):
                    pool.wait_ge(s_es, n * 2 * NS + 2 * (u - NS) + 2)
                    p = pr[:, u % 2].rearrange("p (h m) -> p h m", m=M)
                    nc.gpsimd.tensor_tensor(out=p, in0=p, in1=esum[:, u, :].unsqueeze(2).broadcast_to([P, H8, M]),
                                            op=ALU.mult).then_inc(s_norm, 1)
                pool.wait_ge(s_norm, (n + 1) * NS)
                pool.nop(nofuse=True)

        def rinv(dve, n, s):
            dve.wait_ge(s_exp, n * NU + s + 1)
            nc.vector.reciprocal(esum[:, s, 1:2], esum[:, s, 0:1]).then_inc(s_rinv, 1)

        def sums(dve, n, u):
            v = u - NS
            dve.wait_ge(s_exp, n * NU + u + 1)
            nc.vector.tensor_reduce(out=smax[:, u % 2, :], in_=pr[:, u % 2].rearrange("p (h m) -> p h m", m=M),
                                    axis=AX.X, op=ALU.add).then_inc(s_es, 1)
            dve.wait_ge(s_es, n * 2 * NS + 2 * v + 1)
            nc.vector.reciprocal(esum[:, u, :], smax[:, u % 2, :]).then_inc(s_es, 1)
            dve.wait_ge(s_es, n * 2 * NS + 2 * v + 2)

        @block.vector
        def _(dve):
            ln_rstd(nc, dve, stats, mean, rstd, scr, s_var, s_sqrt)
            dve.wait_ge(s_const, LOADS)
            dve.wait_ge(s_zero, 2)
            V = nc.vector
            with dve.Fori(0, B) as n:
                dve.wait_ge(s_batch, n + 1)
                for t in range(NT):
                    tt = n * NT + t
                    V.tensor_scalar(xn[:, t, :], X[:, bass.ds(tt, 1), :], mean[:, bass.ds(tt, 1)],
                                    rstd[:, bass.ds(tt, 1)], ALU.subtract, ALU.mult).then_inc(s_xn, 1)
                lm = 0
                for item in ORDER:
                    if item[0] in "qk" and item[1].isdigit():
                        isk, hh = item[0] == "k", int(item[1])
                        src, dst = (kT, bdKl) if isk else (qT, bdQ)
                        ls = lsum[:, 2 * isk + hh, :]
                        out_of(dve, n, item)
                        V.tensor_reduce(out=ls, in_=src[:, hh, :].rearrange("p (m j) -> p m j", j=T // M),
                                        axis=AX.X, op=ALU.add).then_inc(s_lm, 1)
                        lm += 1
                        dve.wait_ge(s_lm, n * 10 + lm)
                        if isk:
                            V.tensor_scalar(klm[:, hh, :], ls, M / T, None, ALU.mult).then_inc(s_lm, 1)
                            lm += 1
                        V.scalar_tensor_tensor(
                            out=dst[:, hh], in0=ls.unsqueeze(1).broadcast_to([P, H8, M]), scalar=M / T,
                            in1=hmask[:].unsqueeze(2).broadcast_to([P, H8, M]),
                            op0=ALU.mult, op1=ALU.mult).then_inc(s_lm, 1)
                        lm += 1
                    elif item == "S2":
                        gb = full(dve, n, item)
                        s2 = gb[:].rearrange("p (s m) -> p s m", m=M)
                        V.tensor_reduce(out=k2max[:], in_=s2, axis=AX.X, op=ALU.max).then_inc(s_k2, 1)
                        dve.wait_ge(s_k2, n * 5 + 1)
                        emptied(V.tensor_tensor(out=k2[:], in0=s2,
                                                in1=k2max[:].unsqueeze(2).broadcast_to([P, NS, M]),
                                                op=ALU.subtract), item)
                    elif item == "v1":
                        dve.wait_ge(s_k2e, n + 1)
                        V.tensor_reduce(out=k2sum[:], in_=k2[:], axis=AX.X, op=ALU.add).then_inc(s_k2, 1)
                        dve.wait_ge(s_k2, n * 5 + 2)
                        V.reciprocal(k2max[:], k2sum[:]).then_inc(s_k2, 1)
                        dve.wait_ge(s_k2, n * 5 + 3)
                        for e in range(2):
                            r = slice(64 * e, 64 * e + 64)
                            V.tensor_tensor(out=bdK2[r, :, 64 * e:64 * e + 64], in0=k2[r],
                                            in1=k2max[r, :].unsqueeze(2).broadcast_to([64, NS, M]),
                                            op=ALU.mult).then_inc(s_k2, 1)
                    elif item in ("d0", "d1"):
                        j = int(item[1])
                        gb = full(dve, n, item)
                        emptied(V.tensor_reduce(out=dmax[:, 4 * j:4 * j + 4],
                                                in_=gb[:].rearrange("p (s m) -> p s m", m=P),
                                                axis=AX.X, op=ALU.max), item)
                        if j == 1:
                            out_of_all(dve, n, ["d0", "d1"])
                            V.reciprocal(dinv[:], dmax[:]).then_inc(s_dinv, 1)
                    elif item in ("A0", "A1"):
                        j = int(item[1])
                        gb = full(dve, n, item)
                        dve.wait_ge(s_dinv, n + 1)
                        emptied(V.tensor_tensor(
                            out=aw[:, 4 * j:4 * j + 4, 0:P], in0=gb[:].rearrange("p (s m) -> p s m", m=P),
                            in1=dinv[:, 4 * j:4 * j + 4].unsqueeze(2).broadcast_to([P, 4, P]), op=ALU.mult), item)
                    elif item.startswith("score"):
                        u = int(item[5:])
                        dve.wait_ge(s_scores, n * NU + u + 1)
                        if u < NS:
                            V.tensor_reduce(out=smax[:, u % 2, 0:1], in_=S[u % 2][:], axis=AX.X, op=ALU.max,
                                            negate=True).then_inc(s_max, 1)
                        else:
                            sc = S[u % 2][:].rearrange("p (h m) -> p h m", m=M)
                            V.tensor_reduce(out=smax[:, u % 2, :], in_=sc, axis=AX.X, op=ALU.max)\
                             .then_inc(s_max, 1)
                            dve.wait_ge(s_max, n * NU + u + 1)
                            if u >= NS + 2:
                                dve.wait_ge(s_exp, n * NU + u - 1)
                            V.tensor_tensor(out=sh[:, u % 2].rearrange("p (h m) -> p h m", m=M), in0=sc,
                                            in1=smax[:, u % 2, :].unsqueeze(2).broadcast_to([P, H8, M]),
                                            op=ALU.subtract).then_inc(s_sh, 1)
                            if u > NS:
                                sums(dve, n, u - 1)
                    elif item[0] == "w":
                        s = int(item[1:])
                        rinv(dve, n, s)
                        gb = full(dve, n, item)
                        dve.wait_ge(s_rinv, n * NS + s + 1)
                        emptied(V.tensor_scalar(aw[:, s, P:AW], gb[:, 0:HD], esum[:, s, 1:2], None, ALU.mult), item)
                    elif item[0] == "R":
                        i, gr = int(item[1]), int(item[3])
                        a, b = GROUPS[gr]
                        k = slice(0, AW) if i < ITERS - 1 else slice(P, AW)
                        dve.wait_ge(s_rq, step(n, i, gr))
                        V.scalar_tensor_tensor(out=uq[:, a:b, k], in0=aw[:, a:b, k], scalar=1.75,
                                               in1=rq[:, a:b, k], op0=ALU.mult, op1=ALU.subtract)\
                         .then_inc(s_uq, 1)
                        dve.wait_ge(s_aw3, step(n, i, gr))
                        V.scalar_tensor_tensor(out=tm[:, a:b, k], in0=rq[:, a:b, k], scalar=-15.0,
                                               in1=aw3[:, a:b, k], op0=ALU.mult, op1=ALU.add).then_inc(s_tm, 1)
                    elif item[0] == "N":
                        i, gr = int(item[1]), int(item[3])
                        a, b = GROUPS[gr]
                        k = slice(0, AW) if i < ITERS - 1 else slice(P, AW)
                        dve.wait_ge(s_tm, step(n, i, gr))
                        dve.wait_ge(s_pd, step(n, i, gr))
                        V.scalar_tensor_tensor(
                            out=aw[:, a:b, k],
                            in0=I[gr][:, 0:(b - a) * AW].rearrange("p (s m) -> p s m", m=AW)[:, :, k],
                            scalar=4.0, in1=tm[:, a:b, k], op0=ALU.mult, op1=ALU.add).then_inc(s_aw, 1)
                    elif item == "Z":
                        gb = full(dve, n, item)
                        for e in range(2):
                            r = slice(64 * e, 64 * e + 64)
                            last = V.tensor_tensor(
                                out=zbd[r, :, HD * e:HD * e + HD],
                                in0=gb[r, 0:NS * HD].rearrange("p (s d) -> p s d", d=HD),
                                in1=dinv[r, :].unsqueeze(2).broadcast_to([64, NS, HD]), op=ALU.mult)
                        emptied(last, item)
                    elif item.startswith("pj"):
                        t = int(item[2])
                        gb = full(dve, n, item)
                        x = X[:, bass.ds(n * NT + t, 1), :]
                        emptied(V.tensor_tensor(out=x, in0=x, in1=gb[:, 0:C].unsqueeze(1), op=ALU.add), item)
                        out_of(dve, n, item)
                        dve.nop(nofuse=True)
                        last = V.bn_stats(stats[:, bass.ds(n * NT + t, 1), :], x)
                        if t == NT - 1:
                            last.then_inc(s_batch, 1)
                    if item == f"score{NU - 1}":
                        sums(dve, n, NU - 1)

        @block.scalar
        def _(act):
            ln_sqrt(nc, act, scr, s_var, s_sqrt)
            A = nc.scalar.activation
            with act.Fori(0, B) as n:
                for item in ORDER:
                    if item[:2] == "xT":
                        emptied(A(xT[:, int(item[2]), :], full(act, n, item)[:], ACT.Copy), item)
                    elif item[0] == "q":
                        emptied(A(qT[:, int(item[1]), :], full(act, n, item)[:], ACT.Copy,
                                  scale=float(HD) ** -0.5), item)
                    elif item in ("k0", "k1"):
                        emptied(A(kT[:, int(item[1]), :], full(act, n, item)[:], ACT.Copy), item)
                    elif item in ("v0", "v1"):
                        if item == "v0":
                            out_of(act, n, "S2")
                            A(k2[:], k2[:], ACT.Exp).then_inc(s_k2e, 1)
                        j = 2 * int(item[1])
                        emptied(A(vv[:, j:j + 2, :], full(act, n, item)[:].rearrange("p (t c) -> p t c", t=2),
                                  ACT.Copy), item)
                    elif item in ("kT0", "kT1"):
                        j = 4 * int(item[2])
                        emptied(A(k2T[:, j:j + 4, :], full(act, n, item)[:].rearrange("p (s m) -> p s m", m=P),
                                  ACT.Copy), item)
                    elif item.startswith("score"):
                        u = int(item[5:])
                        if u >= 2:
                            act.wait_ge(s_tp, n * NU + u - 1)
                        if u < NS:
                            act.wait_ge(s_max, n * NU + u + 1)
                            A(pr[:, u % 2], S[u % 2][:], ACT.Exp, bias=smax[:, u % 2, 0:1],
                              accum_out=esum[:, u, 0:1]).then_inc(s_exp, 1)
                        else:
                            act.wait_ge(s_sh, n * NS + u - NS + 1)
                            A(pr[:, u % 2], sh[:, u % 2], ACT.Exp).then_inc(s_exp, 1)
                    elif item.startswith("turn"):
                        u = int(item[4:])
                        act.wait_ge(s_tp, n * NU + u + 1)
                        tb = TB[:].rearrange("p (j q) -> p j q", j=4)
                        if u < NS:
                            if u >= 2:
                                b, k = g(f"w{u - 2}")
                                act.wait_ge(s_full[b], n * PER[b] + k + 1)
                            A(p3T[:, u % 2], tb, ACT.Copy).then_inc(s_pT, 1)
                        else:
                            t, hh = (u - NS) // 2, (u - NS) % 2
                            A(p1T[:, 4 * hh:4 * hh + 4, t * P:(t + 1) * P], tb, ACT.Copy).then_inc(s_pT, 1)
                    elif item[0] == "R":
                        i, gr = int(item[1]), int(item[3])
                        a, b = GROUPS[gr]
                        if i == 0 and gr == 0:
                            out_of_all(act, n, ["A0", "A1"] + [f"w{s}" for s in range(NS)])
                        k = slice(0, AW) if i < ITERS - 1 else slice(P, AW)
                        if i > 0:
                            act.wait_ge(s_aw, step(n, i - 1, gr))
                        A(aw3[:, a:b, k], aw[:, a:b, k], ACT.Copy, scale=3.25).then_inc(s_aw3, 1)
                        act.wait_ge(s_sq, step(n, i, gr))
                        A(rq[:, a:b, :], I[gr][:, 0:(b - a) * AW].rearrange("p (s m) -> p s m", m=AW), ACT.Copy,
                          scale=0.25).then_inc(s_rq, 1)
                    elif item[:2] == "sv":
                        emptied(A(svT[:, int(item[2]), :], full(act, n, item)[:], ACT.Copy), item)

        @block.tensor
        def _(pe):
            mm = nc.tensor.matmul
            for sm in (s_empty[0], s_empty[1], s_batch):
                pe.sem_inc(sm, 1)
            pe.wait_ge(s_const, LOADS)
            pe.wait_ge(s_zero, 2)
            with pe.Fori(0, B) as n:
                for item in ORDER:
                    gb = claim(pe, n, item) if item in USES else None
                    if item[:2] == "xT":
                        kc = int(item[2])
                        for t in range(NT):
                            if kc == 0:
                                pe.wait_ge(s_xn, n * NT + t + 1)
                            last = nc.tensor.transpose(gb[:, t * P:(t + 1) * P], xn[:, t, kc * P:(kc + 1) * P],
                                                       ident[:])
                    elif item in ("q0", "q1", "k0", "k1"):
                        blk = 2 * (item[0] == "k") + int(item[1])
                        if item == "q0":
                            out_of_all(pe, n, ["xT0", "xT1"], item)
                        for kc in range(2):
                            last = mm(gb[:], wq[:, kc, blk * P:(blk + 1) * P], xT[:, kc, :],
                                      start=(kc == 0), stop=(kc == 1))
                    elif item in ("v0", "v1"):
                        for j in range(2):
                            t = 2 * int(item[1]) + j
                            for kc in range(2):
                                last = mm(gb[:, j * C:(j + 1) * C], xT[:, kc, t * P:(t + 1) * P],
                                          wq[:, kc, 2 * C:3 * C], start=(kc == 0), stop=(kc == 1))
                    elif item == "S2":
                        pe.wait_ge(s_lm, (n + 1) * 10)
                        for s in range(NS):
                            hh, h0 = s // 4, 2 * (s % 4)
                            last = mm(gb[:, s * M:(s + 1) * M], bdQ[:, hh, h0:h0 + 2, :], klm[:, hh, :],
                                      start=True, stop=True)
                    elif item in ("d0", "d1"):
                        j = int(item[1])
                        pe.wait_ge(s_k2, n * 5 + 5)
                        last = mm(gb[:], bones[:], bdK2[:, 4 * j:4 * j + 4, :], start=True, stop=True)
                    elif item in ("kT0", "kT1"):
                        for j in range(4):
                            s = 4 * int(item[2]) + j
                            last = nc.tensor.transpose(gb[:, j * P:(j + 1) * P], bdK2[:, s, :], ident[:])
                    elif item in ("A0", "A1"):
                        out_of_all(pe, n, [f"kT{item[1]}"], item)
                        for j in range(4):
                            s = 4 * int(item[1]) + j
                            last = mm(gb[:, j * P:(j + 1) * P], k2T[:, s, :], k2T[:, s, :], start=True, stop=True)
                    elif item.startswith("score"):
                        u = int(item[5:])
                        if 2 <= u < NS + 2:
                            pe.wait_ge(s_exp, n * NU + u - 1)
                        elif u >= NS + 2:
                            pe.wait_ge(s_sh, n * NS + u - NS - 1)
                        if u < NS:
                            hh, h0 = u // 4, 2 * (u % 4)
                            last = mm(S[u % 2][:], bdQ[:, hh, h0:h0 + 2, :], kT[:, hh, :], start=True, stop=True)
                        else:
                            t, hh = (u - NS) // 2, (u - NS) % 2
                            last = mm(S[u % 2][:], qT[:, hh, t * P:(t + 1) * P], bdKl[:, hh], start=True, stop=True)
                        last.then_inc(s_scores, 1)
                    elif item.startswith("turn"):
                        u = int(item[4:])
                        if u < NS:
                            pe.wait_ge(s_exp, n * NU + u + 1)
                        else:
                            pe.wait_ge(s_norm, n * NS + u - NS + 1)
                        if u >= 1:
                            pe.wait_ge(s_pT, n * NU + u)
                        for j in range(4):
                            last = nc.tensor.transpose(TB[:, j * P:(j + 1) * P], pr[:, u % 2, j * P:(j + 1) * P],
                                                       ident[:])
                        last.then_inc(s_tp, 1)
                    elif item[0] == "w":
                        s = int(item[1:])
                        pe.wait_ge(s_pT, n * NU + s + 1)
                        if s == 0:
                            out_of_all(pe, n, ["v0", "v1"], item)
                        for t in range(NT):
                            for j in range(4):
                                hd = 2 * s + j // 2
                                last = mm(gb[32 * j:32 * j + 32, 0:HD], p3T[:, s % 2, t, 32 * j:32 * j + 32],
                                          vv[:, t, hd * HD:(hd + 1) * HD], start=(t == 0), stop=(t == NT - 1))
                    elif item[0] == "R":
                        i, gr = int(item[1]), int(item[3])
                        if i == 0 and gr == 0:
                            out_of_all(pe, n, ["A0", "A1"] + [f"w{s}" for s in range(NS)])
                        if i > 0:
                            pe.wait_ge(s_aw, step(n, i - 1, gr))
                        a, b = GROUPS[gr]
                        for s in range(a, b):
                            last = mm(I[gr][:, (s - a) * AW:(s - a + 1) * AW], aw[:, s, 0:P], aw[:, s, :],
                                      start=True, stop=True)
                        last.then_inc(s_sq, 1)
                    elif item[0] == "N":
                        i, gr = int(item[1]), int(item[3])
                        a, b = GROUPS[gr]
                        k = 0 if i < ITERS - 1 else P
                        pe.wait_ge(s_uq, step(n, i, gr))
                        for s in range(a, b):
                            last = mm(I[gr][:, (s - a) * AW + k:(s - a + 1) * AW], rq[:, s, 0:P], uq[:, s, k:AW],
                                      start=True, stop=True)
                        last.then_inc(s_pd, 1)
                    elif item == "Z":
                        pe.wait_ge(s_aw, step(n, ITERS - 1, 2))
                        for s in range(NS):
                            last = mm(gb[:, s * HD:(s + 1) * HD], bdK2[:, s, :], aw[:, s, P:AW],
                                      start=True, stop=True)
                    elif item[:2] == "sv":
                        hh = int(item[2])
                        out_of_all(pe, n, ["Z"], item)
                        pe.wait_ge(s_pT, (n + 1) * NU)
                        for j in range(4):
                            last = mm(gb[32 * j:32 * j + 32, :], zbd[:, 4 * hh + j, :], p1T[:, 4 * hh + j, :],
                                      start=True, stop=True)
                    elif item[:2] == "pj":
                        t = int(item[2])
                        if t == 0:
                            out_of_all(pe, n, ["sv0", "sv1"], item)
                        for hh in range(HH):
                            last = mm(gb[:, 0:C], svT[:, hh, t * P:(t + 1) * P], wp[:, hh, :],
                                      start=(hh == 0), stop=(hh == 1))
                    if gb is not None:
                        filled(last, item)


def load_x(nc, x, X, stats, ident):
    with ExitStack() as ctx:
        s_x = [ctx.enter_context(nc.semaphore(f"x_loaded{b}")) for b in range(B)]
        s_id = ctx.enter_context(nc.semaphore("identity"))
        block = ctx.enter_context(nc.Block())

        @block.sync
        def _(sp):
            xv = x.rearrange("b (t p) c -> b p t c", p=P)
            for b in range(B):
                sp.dma_start(X[:, b * NT:(b + 1) * NT, :], xv[b]).then_inc(s_x[b], 16)

        @block.gpsimd
        def _(pool):
            nc.gpsimd.memset(ident[:], 0.0).then_inc(s_id, 1)
            pool.wait_ge(s_id, 1)
            nc.gpsimd.affine_select(out=ident[:], in_=ident[:], compare_op=ALU.not_equal, fill=1.0, base=0,
                                    pattern=[[-1, P]], channel_multiplier=1).then_inc(s_id, 1)

        @block.vector
        def _(dve):
            for b in range(B):
                dve.wait_ge(s_x[b], 16)
                for t in range(b * NT, (b + 1) * NT):
                    nc.vector.bn_stats(stats[:, t, :], X[:, t, :])


def store_x(nc, X, out):
    with ExitStack() as ctx:
        s_out = ctx.enter_context(nc.semaphore("x_stored"))
        block = ctx.enter_context(nc.Block())

        @block.sync
        def _(sp):
            ov = out.rearrange("b (t p) c -> b p t c", p=P)
            for b in range(B):
                sp.dma_start(ov[b], X[:, b * NT:(b + 1) * NT, :]).then_inc(s_out, 16)
            sp.wait_ge(s_out, 16 * B)


def build(nc, w, out, phases="AFBF"):
    with ExitStack() as ctx:
        X = ctx.enter_context(nc.sbuf_tensor("X", [P, B * NT, C], fp32))
        stats = ctx.enter_context(nc.sbuf_tensor("stats", [P, B * NT, 6], fp32))
        ident = ctx.enter_context(nc.sbuf_tensor("ident", [P, P], fp32))
        load_x(nc, w["x"], X, stats, ident)
        for i, ph in enumerate(phases):
            if ph == "A":
                cluster_attention(nc, X, stats, ident, w)
            elif ph == "F":
                moe_ffn(nc, X, stats, ident, w, i)
            elif ph == "B":
                landmark_attention(nc, X, stats, ident, w)
        store_x(nc, X, out)


def _tables():
    import math
    import numpy as np
    gs, ncl, per = 64, 64, 8
    pos = np.arange(ncl + gs, dtype=np.float32)[:, None]
    div = np.exp(np.arange(0, HD, 2, dtype=np.float32) * np.float32(-math.log(10000.0) / HD))
    ang = (pos * div).astype(np.float32)
    S = np.stack([np.sin(ang), np.cos(ang)], axis=-1).reshape(ncl + gs, HD).astype(np.float32)
    order = np.array([d // 2 + (HD // 2) * (d % 2) for d in range(HD)])
    R = S[:, order]
    dims = np.arange(P) % HD
    tabq = R[:gs][:, dims].T
    posk = (np.arange(T) // gs) * per + np.arange(T) % gs
    tabk = R[posk][:, dims].T
    tabc = R[:ncl][:, dims].T[:, None, :] * (np.arange(P)[:, None] // HD == np.arange(8)[None])[:, :, None]
    own16 = (np.arange(P)[:, None] // per == np.arange(32)[None]).astype(np.float32)
    row = np.arange(P)
    g = 2 * np.arange(NT)[None, :] + (row // gs)[:, None]
    col = np.arange(2 * gs)
    local = (col // gs)[None, :] == (row // gs)[:, None]
    seen = np.where(local[:, None, :], (col % gs)[None, None, :] <= (row % gs)[:, None, None],
                    (col % gs)[None, None, :] < (g * per)[:, :, None])
    maska = np.where(seen, 0.0, -1e30)
    f = lambda a: np.ascontiguousarray(a, dtype=np.float32)
    rank = np.broadcast_to(E - np.arange(E), (P, E))
    return {"rank": f(rank), "tabq": f(tabq), "tabk": f(tabk), "tabc": f(tabc), "own16": f(own16), "maska": f(maska),
            "headmask": f(np.arange(P)[:, None] // HD == np.arange(8)[None]),
            "blockones": f(np.arange(P)[:, None] // 64 == (np.arange(P)[None] // 64))}


def _layout(i):
    import numpy as np
    c = np.ascontiguousarray
    i = {k: np.asarray(v) for k, v in i.items()}
    return {"x": c(i["L0_attn_a_x"]),
            "a_w_attnT": c(i["L0_attn_a_w_attn"].T), "a_w_projT": c(i["L0_attn_a_w_proj"].T),
            "a_b_attn": c(i["L0_attn_a_b_attn"]), "a_bqk": c(i["L0_attn_a_b_attn"][:2 * C].reshape(4, P).T),
            "a_b_proj": c(i["L0_attn_a_b_proj"]), "a_w_assign": c(i["L0_attn_a_w_assign"]),
            "b_w_qkv": c(i["L0_attn_b_w_qkv"]), "b_w_proj": c(i["L0_attn_b_w_proj"]),
            "r_wT": c(i["L0_ffn_router_w"].T), "r_b": c(i["L0_ffn_router_b"]),
            "e_wT": c(i["L0_ffn_expert_w"].transpose(0, 2, 1)), "e_b": c(i["L0_ffn_expert_b"])}


def kernel(**inputs):
    import concourse.bacc as bacc
    from concourse.bass_utils import run_bass_kernel_spmd as run
    nc = bacc.Bacc("TRN2", target_bir_lowering=False, num_devices=1)
    arrays = {**_layout(inputs), **_tables()}
    w = {n: nc.dram_tensor(f"in_{n}", a.shape, mybir.dt.from_np(a.dtype), kind="ExternalInput").ap()
         for n, a in arrays.items()}
    out = nc.dram_tensor("out", (B, T, C), fp32, kind="ExternalOutput").ap()
    build(nc, w, out)
    r = run(nc, [{f"in_{n}": a for n, a in arrays.items()}], core_ids=[0])
    return r.results[0]["out"]
```

```python
import concourse.bass as bass
from concourse import mybir
from contextlib import ExitStack

fp32 = mybir.dt.float32
bf16 = mybir.dt.bfloat16
ALU = mybir.AluOpType
ACT = mybir.ActivationFunctionType
AX = mybir.AxisListType

P = 128
B, T, C = 8, 512, 256
H, HD = 16, 16
NT = T // P
E = 8
EPS = 1e-5


def steps(eng, step, body):
    def partial(n):
        for ahead, item in step:
            if 0 <= n + ahead < B:
                body(item, n + ahead, (n + ahead) % 2)

    partial(-2)
    partial(-1)
    with eng.Fori(0, B // 2 - 1) as j:
        for par in range(2):
            for ahead, item in step:
                body(item, j * 2 + (par + ahead), (par + ahead) % 2)
    partial(B - 2)
    partial(B - 1)


def wait_later(eng, sem, value):
    if not isinstance(value, int) or value >= 1:
        eng.wait_ge(sem, value)


class Uses:

    def __init__(self, banks, full, empty, names):
        self.banks, self.full, self.empty, self.names = banks, full, empty, names
        self.per = [len(names[i::len(banks)]) for i in range(len(banks))]

    def at(self, name):
        i = self.names.index(name)
        return i % len(self.banks), i // len(self.banks)

    def claim(self, pe, n, name):
        b, k = self.at(name)
        pe.wait_ge(self.empty[b], n * self.per[b] + (k + 1))
        return self.banks[b]

    def filled(self, ins, name):
        ins.then_inc(self.full[self.at(name)[0]], 1)

    def filled_bank(self, eng, n, name):
        b, k = self.at(name)
        eng.wait_ge(self.full[b], n * self.per[b] + (k + 1))
        return self.banks[b]

    def emptied(self, ins, name):
        ins.then_inc(self.empty[self.at(name)[0]], 1)

    def brought_out(self, eng, n, names, claimed=None):
        for b in range(len(self.banks)):
            ks = [self.at(x)[1] for x in names if self.at(x)[0] == b]
            if ks and (claimed is None or self.at(claimed)[0] != b):
                eng.wait_ge(self.empty[b], n * self.per[b] + (max(ks) + 2))


def first_stats(nc, dve, X, stats, s_x, s_stats):
    for b in range(B):
        dve.wait_ge(s_x[b], 16)
        for t in range(b * NT, (b + 1) * NT):
            nc.vector.bn_stats(stats[:, t, :], X[:, t, :]).then_inc(s_stats, 1)
    dve.wait_ge(s_stats, B * NT)


def ln_rstd(nc, dve, stats, mean, rstd, scr, s_var, s_sqrt):
    me, mo = stats[:, :, 1], stats[:, :, 4]
    half, dif, var, std = (scr[:, i, :] for i in range(4))
    tt = nc.vector.tensor_tensor
    tt(out=half, in0=me, in1=mo, op=ALU.add).then_inc(s_var, 1)
    tt(out=dif, in0=me, in1=mo, op=ALU.subtract).then_inc(s_var, 1)
    tt(out=var, in0=stats[:, :, 2], in1=stats[:, :, 5], op=ALU.add).then_inc(s_var, 1)
    dve.wait_ge(s_var, 3)
    nc.vector.tensor_scalar(mean[:], half, 0.5, None, ALU.mult).then_inc(s_var, 1)
    nc.vector.tensor_scalar(var, var, 1.0 / C, EPS, ALU.mult, ALU.add).then_inc(s_var, 1)
    nc.vector.tensor_scalar(dif, dif, 0.5, None, ALU.mult).then_inc(s_var, 1)
    dve.wait_ge(s_var, 6)
    tt(out=half, in0=dif, in1=dif, op=ALU.mult).then_inc(s_var, 1)
    dve.wait_ge(s_var, 7)
    tt(out=var, in0=var, in1=half, op=ALU.add).then_inc(s_var, 1)
    dve.wait_ge(s_sqrt, 1)
    nc.vector.reciprocal(rstd[:], std).then_inc(s_var, 1)
    dve.wait_ge(s_var, 9)
    tt(out=half, in0=rstd[:], in1=rstd[:], op=ALU.mult).then_inc(s_var, 1)
    dve.wait_ge(s_var, 10)
    tt(out=half, in0=half, in1=var, op=ALU.mult).then_inc(s_var, 1)
    dve.wait_ge(s_var, 11)
    nc.vector.tensor_scalar(half, half, -0.5, 1.5, ALU.mult, ALU.add).then_inc(s_var, 1)
    dve.wait_ge(s_var, 12)
    tt(out=rstd[:], in0=rstd[:], in1=half, op=ALU.mult).then_inc(s_var, 1)
    dve.wait_ge(s_var, 13)


def ln_sqrt(nc, act, scr, s_var, s_sqrt):
    act.wait_ge(s_var, 8)
    nc.scalar.activation(scr[:, 3, :], scr[:, 2, :], ACT.Sqrt).then_inc(s_sqrt, 1)


def cluster_attention(nc, X, stats, ident, w, s_x, more_loads):
    with ExitStack() as ctx:
        sb = lambda name, shape, dt=fp32: ctx.enter_context(nc.sbuf_tensor("a_" + name, shape, dt))
        sem = lambda name: ctx.enter_context(nc.semaphore("a_" + name))

        GS = 64
        NCL = 64
        KEYS = GS + NCL
        HQ = 4
        UNITS = NT * (H // HQ)
        DV = HD + 1
        HH = 2
        H8 = H // HH
        RING = 4

        wqkT = sb("wqkT", [P, 2, 2 * C])
        wvT = sb("wvT", [P, 2, C])
        wpT = sb("wpT", [P, 2, C])
        bqk = sb("bqk", [P, 4])
        bv = sb("bv", [P, C])
        bp = sb("bp", [P, C])
        wassign = sb("wassign", [P, NT, C])
        tabq = sb("tabq", [P, GS])
        tabk = sb("tabk", [P, T])
        tabc = sb("tabc", [P, H8, NCL])
        own16 = sb("own16", [P, 32])
        mask = sb("mask", [P, NT, KEYS])
        rstd = sb("rstd", [P, B * NT])
        mean = sb("mean", [P, B * NT])
        scr = sb("scr", [P, 4, B * NT])

        xn = sb("xn", [P, NT, C])
        xT = sb("xT", [P, 2, T])
        dump = sb("dump", [P, C])
        logit = sb("logit", [P, NT])
        lrow = sb("lrow", [NT, T // NT])
        lmax = sb("lmax", [NT, 16])
        lexp = sb("lexp", [NT, T // NT])
        lsum = sb("lsum", [NT, 16])
        lw = sb("lw", [NT, T // NT])
        wsel = sb("wsel", [P, NT, 32])
        xbar = sb("xbar", [P, C])
        xbT = sb("xbT", [P, 2, 2, NCL])
        qT = sb("qT", [P, 2, HH, T])
        kT = sb("kT", [P, HH, T])
        bdK = sb("bdK", [P, 2, HH, H8, T])
        bdC = sb("bdC", [P, 2, HH, H8, NCL])
        cvb = sb("cvb", [P, C])
        V = [sb(f"V{e}", [P, 2, NT, H, DV]) for e in range(2)]
        smax = sb("smax", [P, RING, HQ])
        pr = sb("pr", [P, RING, HQ, KEYS])
        pT = sb("pT", [P, 2, HQ, P])
        rsum = sb("rsum", [P, 2, H])
        y = sb("y", [P, 2, C])
        yT = sb("yT", [P, 2, 2, P])

        bank = [ctx.enter_context(nc.psum_tensor(f"a_bank{i}", [P, 512], fp32)) for i in range(8)]
        S, TB, O, PB, MB = bank[0:2], bank[2:4], bank[4], bank[5:7], bank[7]

        PREP = ["xn", "lg", "xT0", "xT1", "lgT", "q0", "lexp", "k0", "k1", "lsum", "wT", "q1", "xb", "v0", "xbT",
                "ckv", "v1", "vcl"]
        LAG = 3

        def unit(kind, u):
            return (1 + u // UNITS, f"{kind}{u % UNITS}")

        STEP, prep = [], list(PREP)
        for u in range(UNITS):
            t = u // 4
            STEP += [unit("score", u + LAG + 1), unit("turn", u + 1), unit("exp", u + LAG), unit("weigh", u)]
            STEP += [(2, x) for x in prep[:1 + (u % 2)]]
            prep = prep[1 + (u % 2):]
            if u % 4 == 0:
                STEP += [(t > 0, f"yT{(t - 1) % NT}")]
            if u % 4 == 1:
                STEP += [(t > 0, f"pj{(t - 1) % NT}")]
            if u % 4 == 3:
                STEP += [(1, f"norm{t}")]
            if u + LAG + 1 == UNITS - 1:
                assert not prep

        s_const = sem("const_loaded")
        s_zero = sem("zeroed")
        s_stats, s_var = sem("first_stats"), sem("variance")
        s_sqrt = sem("sqrt_done")
        s_xn = sem("xn_ready")
        s_logit = sem("logit_ready")
        s_lexp = sem("logit_exp")
        s_lsum = sem("cluster_softmax_steps")
        s_lw = sem("cluster_weights")
        s_bdk = sem("bdk_ready")
        s_vc = sem("cluster_v_placed")
        s_bias = sem("x_biased")
        s_scores = sem("scores_ready")
        s_masked = sem("scores_masked")
        s_max = sem("row_max")
        s_sh = sem("scores_shifted")
        s_exp = sem("exp_done")
        s_tp = sem("probs_transposed")
        s_pT = sem("pT_ready")
        s_pv = sem("pv_done")
        s_rsum = sem("rsum_ready")
        s_y = sem("y_ready")

        used = [x for x in PREP if x not in ("xn", "lg", "lexp", "lsum", "vcl")]
        pre = Uses(PB, [sem("prep_full0"), sem("prep_full1")], [sem("prep_empty0"), sem("prep_empty1")], used)
        out = Uses([MB], [sem("main_full")], [sem("main_empty")], [f"{x}{t}" for t in range(NT) for x in ("yT", "pj")])

        LOADS = 16 * 12
        block = ctx.enter_context(nc.Block())

        @block.sync
        def _(sp):
            cw = w["a_w_attnT"]
            loads = [(wqkT[:], cw[:, 0:2 * C].rearrange("(k p) n -> p k n", p=P)),
                     (wvT[:], cw[:, 2 * C:3 * C].rearrange("(k p) n -> p k n", p=P)),
                     (wpT[:], w["a_w_projT"].rearrange("(k p) n -> p k n", p=P)),
                     (bqk[:], w["a_bqk"]),
                     (bv[:], w["a_b_attn"][2 * C:3 * C].partition_broadcast(P)),
                     (bp[:], w["a_b_proj"].partition_broadcast(P)),
                     (tabq[:], w["tabq"]), (tabk[:], w["tabk"]),
                     (tabc[:], w["tabc"]), (own16[:], w["own16"]), (mask[:], w["maska"]),
                     (wassign[:], w["a_w_assign"].rearrange("(t p) n -> p t n", p=P))]
            for dst, src in loads:
                sp.dma_start(dst, src).then_inc(s_const, 16)
            more_loads(sp)
            sp.wait_ge(s_zero, 2)
            with sp.Fori(0, B // 2) as j:
                for par in range(2):
                    n = j * 2 + par
                    for hh in range(HH):
                        pre.brought_out(sp, n, [f"k{hh}"])
                        sp.nop(nofuse=True)
                        for h in range(H8):
                            sp.dma_start(bdK[h * HD:(h + 1) * HD, par, hh, h, :], kT[h * HD:(h + 1) * HD, hh, :])\
                              .then_inc(s_bdk, 16)
                    sp.wait_ge(s_bdk, (n + 1) * (H * 16))
                    sp.nop(nofuse=True)

        @block.gpsimd
        def _(pool):
            nc.gpsimd.memset(bdK[:], 0.0).then_inc(s_zero, 1)
            for e in range(2):
                last = nc.gpsimd.memset(V[e][:], 1.0)
            last.then_inc(s_zero, 1)
            pool.wait_ge(s_zero, 2)
            pool.wait_ge(s_const, LOADS)

            def body(item, n, par):
                if item == "xn":
                    pool.wait_ge(s_xn, (n + 1) * NT)
                    xb = X[:, bass.ds(n * NT, NT), :]
                    nc.gpsimd.tensor_tensor(out=xb, in0=xb, in1=bp[:].unsqueeze(1).broadcast_to([P, NT, C]),
                                            op=ALU.add).then_inc(s_bias, 1)
                    pool.wait_ge(s_bias, n + 1)
                    pool.nop(nofuse=True)
                elif item.startswith("score"):
                    u = int(item[5:])
                    pool.wait_ge(s_max, n * UNITS + (u + 1))
                    nc.gpsimd.tensor_tensor(
                        out=pr[:, u % RING], in0=pr[:, u % RING],
                        in1=smax[:, u % RING, :].unsqueeze(2).broadcast_to([P, HQ, KEYS]),
                        op=ALU.subtract).then_inc(s_sh, 1)
                    pool.wait_ge(s_sh, n * UNITS + (u + 1))
                    pool.nop(nofuse=True)

            steps(pool, STEP, body)

        @block.vector
        def _(dve):
            V_ = nc.vector
            first_stats(nc, dve, X, stats, s_x, s_stats)
            ln_rstd(nc, dve, stats, mean, rstd, scr, s_var, s_sqrt)
            dve.wait_ge(s_const, LOADS)
            dve.wait_ge(s_zero, 2)

            def body(item, n, par):
                if item == "xn":
                    for t in range(NT):
                        tt = n * NT + t
                        V_.tensor_scalar(xn[:, t, :], X[:, bass.ds(tt, 1), :], mean[:, bass.ds(tt, 1)],
                                         rstd[:, bass.ds(tt, 1)], ALU.subtract, ALU.mult).then_inc(s_xn, 1)
                elif item == "lg":
                    for t in range(NT):
                        dve.wait_ge(s_xn, n * NT + (t + 1))
                        V_.tensor_tensor_reduce(
                            out=dump[:], in0=xn[:, t, :], in1=wassign[:, t, :], scale=1.0, scalar=0.0,
                            op0=ALU.mult, op1=ALU.add, accum_out=logit[:, t:t + 1]).then_inc(s_logit, 1)
                        dve.wait_ge(s_logit, n * NT + (t + 1))
                elif item == "lgT":
                    row = pre.filled_bank(dve, n, item)[0:NT, 0:P].rearrange("t (c j) -> t c j", j=8)
                    V_.tensor_reduce(out=lmax[:], in_=row, axis=AX.X, op=ALU.max).then_inc(s_lsum, 1)
                    dve.wait_ge(s_lsum, n * 3 + 1)
                    pre.emptied(V_.tensor_tensor(
                        out=lrow[:].rearrange("t (c j) -> t c j", j=8), in0=row,
                        in1=lmax[:].unsqueeze(2).broadcast_to([NT, 16, 8]), op=ALU.subtract), item)
                elif item == "lsum":
                    ex = lexp[:].rearrange("t (c j) -> t c j", j=8)
                    dve.wait_ge(s_lexp, n + 1)
                    V_.tensor_reduce(out=lsum[:], in_=ex, axis=AX.X, op=ALU.add).then_inc(s_lsum, 1)
                    dve.wait_ge(s_lsum, n * 3 + 2)
                    V_.reciprocal(lmax[:], lsum[:]).then_inc(s_lsum, 1)
                    dve.wait_ge(s_lsum, n * 3 + 3)
                    V_.tensor_tensor(out=lw[:].rearrange("t (c j) -> t c j", j=8), in0=ex,
                                     in1=lmax[:].unsqueeze(2).broadcast_to([NT, 16, 8]), op=ALU.mult)\
                      .then_inc(s_lw, 1)
                elif item == "wT":
                    gb = pre.filled_bank(dve, n, item)
                    pre.emptied(V_.tensor_tensor(
                        out=wsel[:], in0=gb[:, 0:NT].unsqueeze(2).broadcast_to([P, NT, 32]),
                        in1=own16[:].unsqueeze(1).broadcast_to([P, NT, 32]), op=ALU.mult), item)
                elif item in ("q0", "q1"):
                    hh = int(item[1])
                    gb = pre.filled_bank(dve, n, item)
                    pre.emptied(V_.scalar_tensor_tensor(
                        out=qT[:, par, hh, :].rearrange("p (g j) -> p g j", j=GS),
                        in0=gb[:].rearrange("p (g j) -> p g j", j=GS), scalar=bqk[:, hh:hh + 1],
                        in1=tabq[:].unsqueeze(1).broadcast_to([P, T // GS, GS]), op0=ALU.add, op1=ALU.mult), item)
                elif item in ("k0", "k1"):
                    hh = int(item[1])
                    gb = pre.filled_bank(dve, n, item)
                    pre.emptied(V_.scalar_tensor_tensor(
                        out=kT[:, hh, :], in0=gb[:], scalar=bqk[:, 2 + hh:3 + hh], in1=tabk[:],
                        op0=ALU.add, op1=ALU.mult), item)
                elif item == "ckv":
                    gb = pre.filled_bank(dve, n, item)
                    for hh in range(HH):
                        V_.scalar_tensor_tensor(
                            out=bdC[:, par, hh],
                            in0=gb[:, hh * P:hh * P + NCL].unsqueeze(1).broadcast_to([P, H8, NCL]),
                            scalar=bqk[:, 2 + hh:3 + hh], in1=tabc[:], op0=ALU.add, op1=ALU.mult)
                    pre.emptied(V_.tensor_tensor(out=cvb[:], in0=gb[:, 256:512], in1=bv[:], op=ALU.add), item)
                elif item in ("v0", "v1"):
                    i = int(item[1])
                    gb = pre.filled_bank(dve, n, item)
                    for e in range(2):
                        r = slice(64 * e, 64 * e + 64)
                        last = V_.tensor_tensor(
                            out=V[e][r, par, 2 * i:2 * i + 2, :, 0:HD],
                            in0=gb[r, :].rearrange("p (t h d) -> p t h d", t=2, h=H),
                            in1=bv[r, :].rearrange("p (h d) -> p h d", h=H).unsqueeze(1)
                            .broadcast_to([64, 2, H, HD]), op=ALU.add)
                    pre.emptied(last, item)
                elif item.startswith("score"):
                    u = int(item[5:])
                    t = u // 4
                    dve.wait_ge(s_scores, n * UNITS + (u + 1))
                    wait_later(dve, s_tp, n * UNITS + (u - RING + 1))
                    V_.tensor_tensor(out=pr[:, u % RING], in0=S[u % 2][:].rearrange("p (h k) -> p h k", h=HQ),
                                     in1=mask[:, t, :].unsqueeze(1).broadcast_to([P, HQ, KEYS]), op=ALU.add)\
                      .then_inc(s_masked, 1)
                    dve.wait_ge(s_masked, n * UNITS + (u + 1))
                    V_.tensor_reduce(out=smax[:, u % RING, :], in_=pr[:, u % RING], axis=AX.X, op=ALU.max)\
                      .then_inc(s_max, 1)
                elif item.startswith("norm"):
                    t = int(item[4:])
                    dve.wait_ge(s_pv, n * UNITS + (4 * t + 4))
                    wait_later(dve, s_y, n * NT + (t - 1))
                    o = O[:, 0:H * DV].rearrange("p (h d) -> p h d", d=DV)
                    V_.reciprocal(rsum[:, t % 2, :], o[:, :, HD:DV]).then_inc(s_rsum, 1)
                    dve.wait_ge(s_rsum, n * NT + (t + 1))
                    V_.tensor_tensor(
                        out=y[:, t % 2, :].rearrange("p (h d) -> p h d", h=H), in0=o[:, :, 0:HD],
                        in1=rsum[:, t % 2, :].unsqueeze(2).broadcast_to([P, H, HD]), op=ALU.mult).then_inc(s_y, 1)
                elif item.startswith("pj"):
                    t = int(item[2:])
                    gb = out.filled_bank(dve, n, item)
                    if t == 0:
                        dve.wait_ge(s_bias, n + 1)
                    x = X[:, bass.ds(n * NT + t, 1), :]
                    out.emptied(V_.tensor_tensor(out=x, in0=x, in1=gb[:, 0:C].unsqueeze(1), op=ALU.add), item)
                    out.brought_out(dve, n, [item])
                    dve.nop(nofuse=True)
                    V_.bn_stats(stats[:, bass.ds(n * NT + t, 1), :], x)

            steps(dve, STEP, body)

        @block.scalar
        def _(act):
            ln_sqrt(nc, act, scr, s_var, s_sqrt)

            def body(item, n, par):
                if item in ("xT0", "xT1"):
                    gb = pre.filled_bank(act, n, item)
                    pre.emptied(nc.scalar.activation(xT[:, int(item[2]), :], gb[:], ACT.Copy), item)
                elif item == "lexp":
                    pre.brought_out(act, n, ["lgT"])
                    nc.scalar.activation(lexp[:], lrow[:], ACT.Exp).then_inc(s_lexp, 1)
                elif item == "xb":
                    gb = pre.filled_bank(act, n, item)
                    pre.emptied(nc.scalar.activation(xbar[:], gb[:, 0:C], ACT.Copy), item)
                elif item == "xbT":
                    gb = pre.filled_bank(act, n, item)
                    for kc in range(2):
                        for dup in range(2):
                            last = nc.scalar.activation(
                                xbT[:, kc, dup, :].rearrange("p (t c) -> p t c", t=NT),
                                gb[:, kc * P:(kc + 1) * P].rearrange("p (t c) -> p t c", t=NT)[:, :, 0:16],
                                ACT.Copy)
                    pre.emptied(last, item)
                elif item == "vcl":
                    pre.brought_out(act, n, ["ckv"])
                    for e, r in ((0, 64), (1, 0)):
                        nc.scalar.activation(
                            V[e][r:r + 64, par, :, :, 0:HD],
                            cvb[r:r + 64, :].rearrange("p (h d) -> p h d", h=H).unsqueeze(1)
                            .broadcast_to([64, NT, H, HD]), ACT.Copy).then_inc(s_vc, 1)
                elif item.startswith("exp"):
                    u = int(item[3:])
                    act.wait_ge(s_sh, n * UNITS + (u + 1))
                    nc.scalar.activation(pr[:, u % RING], pr[:, u % RING], ACT.Exp, scale=float(HD) ** -0.5)\
                      .then_inc(s_exp, 1)
                elif item.startswith("turn"):
                    u = int(item[4:])
                    act.wait_ge(s_tp, n * UNITS + (u + 1))
                    wait_later(act, s_pv, n * UNITS + (u - 1))
                    nc.scalar.activation(pT[:, u % 2], TB[u % 2][:].rearrange("p (h q) -> p h q", h=HQ),
                                         ACT.Copy).then_inc(s_pT, 1)
                elif item.startswith("yT"):
                    gb = out.filled_bank(act, n, item)
                    out.emptied(nc.scalar.activation(yT[:, int(item[2:]) % 2],
                                                     gb[:, 0:C].rearrange("p (k q) -> p k q", k=2), ACT.Copy), item)

            steps(act, STEP, body)

        @block.tensor
        def _(pe):
            mm = nc.tensor.matmul
            for sm in (*pre.empty, *out.empty):
                pe.sem_inc(sm, 1)
            pe.wait_ge(s_const, LOADS)
            pe.wait_ge(s_zero, 2)

            def body(item, n, par):
                gb = last = None
                if item in pre.names:
                    gb = pre.claim(pe, n, item)
                elif item in out.names:
                    gb = out.claim(pe, n, item)
                if item in ("xT0", "xT1"):
                    kc = int(item[2])
                    for t in range(NT):
                        if kc == 0:
                            pe.wait_ge(s_xn, n * NT + (t + 1))
                        last = nc.tensor.transpose(gb[:, t * P:(t + 1) * P], xn[:, t, kc * P:(kc + 1) * P], ident[:])
                elif item == "lgT":
                    pe.wait_ge(s_logit, (n + 1) * NT)
                    last = nc.tensor.transpose(gb[0:NT, 0:P], logit[:], ident[:])
                elif item in ("q0", "q1", "k0", "k1"):
                    blk = 2 * (item[0] == "k") + int(item[1])
                    pre.brought_out(pe, n, ["xT0", "xT1"], item)
                    for kc in range(2):
                        last = mm(gb[:], wqkT[:, kc, blk * P:(blk + 1) * P], xT[:, kc, :],
                                  start=(kc == 0), stop=(kc == 1))
                elif item == "wT":
                    pe.wait_ge(s_lw, n + 1)
                    pe.nop(nofuse=True)
                    last = nc.tensor.transpose(gb[:, 0:NT], lw[:], ident[0:NT, 0:NT])
                elif item == "xb":
                    pre.brought_out(pe, n, ["wT"], item)
                    for t in range(NT):
                        last = mm(gb[32 * t:32 * t + 32, 0:C], wsel[:, t, :], xn[:, t, :], start=True, stop=True)
                elif item == "xbT":
                    pre.brought_out(pe, n, ["xb"], item)
                    for kc in range(2):
                        last = nc.tensor.transpose(gb[:, kc * P:(kc + 1) * P], xbar[:, kc * P:(kc + 1) * P], ident[:])
                elif item == "ckv":
                    pre.brought_out(pe, n, ["xbT"], item)
                    for hh in range(HH):
                        for kc in range(2):
                            mm(gb[:, hh * P:(hh + 1) * P], wqkT[:, kc, (2 + hh) * P:(3 + hh) * P],
                               xbT[:, kc, :, :], start=(kc == 0), stop=(kc == 1))
                    for kc in range(2):
                        last = mm(gb[:, 256:512], xbT[:, kc, :, :], wvT[:, kc, :], start=(kc == 0), stop=(kc == 1))
                elif item in ("v0", "v1"):
                    for t in (2 * int(item[1]), 2 * int(item[1]) + 1):
                        for kc in range(2):
                            last = mm(gb[:, (t % 2) * C:(t % 2 + 1) * C], xT[:, kc, t * P:(t + 1) * P],
                                      wvT[:, kc, :], start=(kc == 0), stop=(kc == 1))
                elif item.startswith("score"):
                    u = int(item[5:])
                    t, hq = u // 4, u % 4
                    hh, h0 = hq // 2, (hq % 2) * HQ
                    if u == 0:
                        pre.brought_out(pe, n, ["q0", "q1", "ckv"])
                        pe.wait_ge(s_bdk, (n + 1) * (H * 16))
                    wait_later(pe, s_masked, n * UNITS + (u - 1))
                    s4 = S[u % 2][:].rearrange("p (h k) -> p h k", h=HQ)
                    hs = slice(h0, h0 + HQ)
                    for part in range(2):
                        for e in range(2):
                            r = slice(64 * e, 64 * e + 64)
                            q = slice(t * P + 64 * e, t * P + 64 * e + 64)
                            cols = slice(64 * ((part + e) % 2), 64 * ((part + e) % 2) + 64)
                            rhs = bdK[:, par, hh, hs, q] if part == 0 else bdC[:, par, hh, hs, :]
                            last = mm(s4[r, :, cols], qT[:, par, hh, q], rhs, start=True, stop=True)
                    last.then_inc(s_scores, 1)
                elif item.startswith("turn"):
                    u = int(item[4:])
                    pe.wait_ge(s_exp, n * UNITS + (u + 1))
                    wait_later(pe, s_pT, n * UNITS + (u - 1))
                    for h in range(HQ):
                        last = nc.tensor.transpose(TB[u % 2][:, h * P:(h + 1) * P], pr[:, u % RING, h, :], ident[:])
                    last.then_inc(s_tp, 1)
                elif item.startswith("weigh"):
                    u = int(item[5:])
                    t, hq = u // 4, u % 4
                    pe.wait_ge(s_pT, n * UNITS + (u + 1))
                    if u == 0:
                        pre.brought_out(pe, n, ["v0", "v1"])
                        pe.wait_ge(s_vc, n * 2 + 2)
                    if hq == 0:
                        wait_later(pe, s_y, n * NT + t)
                    for h in range(HQ):
                        for j in range(4):
                            hd = hq * HQ + h
                            last = mm(O[32 * j:32 * j + 32, hd * DV:(hd + 1) * DV],
                                      pT[:, u % 2, h, 32 * j:32 * j + 32], V[j // 2][:, par, t, hd, :],
                                      start=True, stop=True)
                    last.then_inc(s_pv, 1)
                elif item.startswith("yT"):
                    t = int(item[2:])
                    pe.wait_ge(s_y, n * NT + (t + 1))
                    for kc in range(2):
                        last = nc.tensor.transpose(gb[:, kc * P:(kc + 1) * P], y[:, t % 2, kc * P:(kc + 1) * P],
                                                   ident[:])
                elif item.startswith("pj"):
                    t = int(item[2:])
                    for kc in range(2):
                        last = mm(gb[:, 0:C], yT[:, t % 2, kc, :], wpT[:, kc, :], start=(kc == 0), stop=(kc == 1))
                if item in pre.names:
                    pre.filled(last, item)
                elif item in out.names:
                    out.filled(last, item)

            steps(pe, STEP, body)
def moe_ffn(nc, X, stats, ident, weights, phase, more_loads, out):
    with ExitStack() as ctx:
        sb = lambda name, shape, dt=fp32: ctx.enter_context(nc.sbuf_tensor(f"f{phase}_" + name, shape, dt))
        sem = lambda name: ctx.enter_context(nc.semaphore(f"f{phase}_" + name))

        rw, rb, ew, eb, rank = weights.tensors
        rstd = sb("rstd", [P, B * NT])
        mean = sb("mean", [P, B * NT])
        scr = sb("scr", [P, 4, B * NT])
        xn = sb("xn", [P, NT, C])
        xT = sb("xT", [P, 2, 2, T])
        lg = sb("lg", [P, NT, E])
        lmax = sb("lmax", [P, NT])
        sh = sb("sh", [P, NT, E])
        ex = sb("ex", [P, NT, E])
        first = sb("first", [P, NT, E])
        wt = sb("wt", [P, NT])
        best = sb("best", [P, NT])
        coef = sb("coef", [P, 2, NT, E])
        coefT = sb("coefT", [E, 2, NT, P])
        acc = sb("acc", [P, 2, C])

        bank = [ctx.enter_context(nc.psum_tensor(f"f{phase}_bank{i}", [P, 512], fp32)) for i in range(8)]
        XB, LG, BI, Y = bank[0:2], bank[2], bank[3], bank[4:8]

        s_var, s_sqrt = sem("variance"), sem("sqrt_done")
        s_xn = sem("xn_ready")
        s_out = sem("x_stored")
        s_route = sem("route_steps")
        s_ex = sem("exp_done")
        s_acc = sem("pair_begun")

        beside = {(0, 0): ["xn"], (0, 2): ["xT0"], (1, 0): ["xT1"], (1, 2): ["lg"], (1, 3): ["shift"],
                  (2, 1): ["exp", "first"], (2, 3): ["coef"], (3, 1): ["cT"]}
        STEP = []
        for t in range(NT):
            STEP.append((0, f"b{t}"))
            for j in range(4):
                STEP.append((0, f"y{t}.{j}"))
                STEP += [(1, x) for x in beside.get((t, j), [])]

        def uses(banks, label, names):
            return Uses(banks, [sem(f"{label}_full{i}") for i in range(len(banks))],
                        [sem(f"{label}_empty{i}") for i in range(len(banks))], names)

        turned = uses(XB, "turned", ["xT0", "xT1"])
        routed = uses([LG], "routed", ["lg", "cT"])
        biased = uses([BI], "biased", [f"b{t}" for t in range(NT)])
        pairs = uses(Y, "pair", [f"y{t}.{j}" for t in range(NT) for j in range(4)])
        USES = (turned, routed, biased, pairs)
        ROUTE = 9
        block = ctx.enter_context(nc.Block())

        @block.sync
        def _(sp):
            more_loads(sp)
            if out is not None:
                ov = out.rearrange("b (t p) c -> b p t c", p=P)
                for b in range(B):
                    pairs.brought_out(sp, b, [f"y{NT - 1}.3"])
                    sp.dma_start(ov[b], X[:, b * NT:(b + 1) * NT, :]).then_inc(s_out, 16)
                sp.wait_ge(s_out, 16 * B)

        @block.vector
        def _(dve):
            ln_rstd(nc, dve, stats, mean, rstd, scr, s_var, s_sqrt)
            dve.wait_ge(weights.loaded, weights.all)
            V = nc.vector
            TTE = [P, NT, E]

            def body(item, n, par):
                def steps_from(first):
                    count = [first]

                    def step(ins):
                        ins.then_inc(s_route, 1)
                        count[0] += 1
                        dve.wait_ge(s_route, n * ROUTE + count[0])
                    return step

                if item == "xn":
                    for t in range(NT):
                        tt = n * NT + t
                        V.tensor_scalar(xn[:, t, :], X[:, bass.ds(tt, 1), :], mean[:, bass.ds(tt, 1)],
                                        rstd[:, bass.ds(tt, 1)], ALU.subtract, ALU.mult).then_inc(s_xn, 1)
                elif item == "shift":
                    gb = routed.filled_bank(dve, n, "lg")
                    step = steps_from(0)
                    V.tensor_tensor(out=lg[:], in0=gb[:, 0:NT * E].rearrange("p (t e) -> p t e", e=E),
                                    in1=rb[:].unsqueeze(1).broadcast_to(TTE), op=ALU.add)\
                     .then_inc(routed.empty[0], 1)
                    routed.brought_out(dve, n, ["lg"])
                    step(V.tensor_reduce(out=lmax[:], in_=lg[:], axis=AX.X, op=ALU.max))
                    step(V.tensor_tensor(out=sh[:], in0=lg[:], in1=lmax[:].unsqueeze(2).broadcast_to(TTE),
                                         op=ALU.subtract))
                elif item == "first":
                    step = steps_from(2)
                    step(V.tensor_scalar(first[:], sh[:], 0.0, None, ALU.is_ge))
                    step(V.tensor_tensor(out=first[:], in0=first[:], in1=rank[:].unsqueeze(1).broadcast_to(TTE),
                                         op=ALU.mult))
                    step(V.tensor_reduce(out=best[:], in_=first[:], axis=AX.X, op=ALU.max))
                    step(V.tensor_tensor(out=first[:], in0=first[:], in1=best[:].unsqueeze(2).broadcast_to(TTE),
                                         op=ALU.is_equal))
                elif item == "coef":
                    dve.wait_ge(s_ex, n + 1)
                    step = steps_from(6)
                    step(V.tensor_reduce(out=wt[:], in_=ex[:], axis=AX.X, op=ALU.add))
                    step(V.reciprocal(best[:], wt[:]))
                    step(V.tensor_tensor(out=coef[:, par], in0=first[:],
                                         in1=best[:].unsqueeze(2).broadcast_to(TTE), op=ALU.mult))
                elif item == "cT":
                    gb = routed.filled_bank(dve, n, item)
                    routed.emptied(V.tensor_copy(coefT[:, par], gb[0:E, :].rearrange("e (t p) -> e t p", t=NT)),
                                   item)
                elif item[0] == "b":
                    t = int(item[1])
                    gb = biased.filled_bank(dve, n, item)
                    x = X[:, bass.ds(n * NT + t, 1), :]
                    biased.emptied(V.tensor_tensor(out=acc[:, t % 2].unsqueeze(1), in0=x,
                                                   in1=gb[:, 0:C].unsqueeze(1), op=ALU.add), item)
                elif item[0] == "y":
                    t, j = int(item[1]), int(item[3])
                    a = acc[:, t % 2]
                    gb = pairs.filled_bank(dve, n, item)
                    if j == 0:
                        biased.brought_out(dve, n, [f"b{t}"])
                    else:
                        pairs.brought_out(dve, n, [f"y{t}.{j - 1}"])
                    V.scalar_tensor_tensor(out=a, in0=gb[:, 0:C], scalar=coef[:, par, t, 2 * j:2 * j + 1], in1=a,
                                           op0=ALU.mult, op1=ALU.add).then_inc(s_acc, 1)
                    dve.wait_ge(s_acc, n * (4 * NT) + (4 * t + j + 1))
                    x = X[:, bass.ds(n * NT + t, 1), :]
                    if j == 3:
                        dve.nop(nofuse=True)
                    pairs.emptied(V.scalar_tensor_tensor(
                        out=(x.squeeze(1) if j == 3 else a), in0=gb[:, C:2 * C],
                        scalar=coef[:, par, t, 2 * j + 1:2 * j + 2], in1=a, op0=ALU.mult, op1=ALU.add), item)
                    if j == 3:
                        pairs.brought_out(dve, n, [item])
                        dve.nop(nofuse=True)
                        V.bn_stats(stats[:, bass.ds(n * NT + t, 1), :], x)

            steps(dve, STEP, body)

        @block.scalar
        def _(act):
            ln_sqrt(nc, act, scr, s_var, s_sqrt)

            def body(item, n, par):
                if item in ("xT0", "xT1"):
                    turned.emptied(nc.scalar.activation(xT[:, par, int(item[2]), :],
                                                        turned.filled_bank(act, n, item)[:], ACT.Copy), item)
                elif item == "exp":
                    act.wait_ge(s_route, n * ROUTE + 2)
                    nc.scalar.activation(ex[:], sh[:], ACT.Exp).then_inc(s_ex, 1)

            steps(act, STEP, body)

        @block.tensor
        def _(pe):
            mm = nc.tensor.matmul
            for use in USES:
                for sm in use.empty:
                    pe.sem_inc(sm, 1)
            pe.wait_ge(weights.loaded, weights.all)

            def body(item, n, par):
                last = None
                use = next((u for u in USES if item in u.names), None)
                gb = use.claim(pe, n, item) if use else None
                if item in ("xT0", "xT1"):
                    kc = int(item[2])
                    for t in range(NT):
                        if kc == 0:
                            pe.wait_ge(s_xn, n * NT + (t + 1))
                        last = nc.tensor.transpose(gb[:, t * P:(t + 1) * P], xn[:, t, kc * P:(kc + 1) * P], ident[:])
                elif item == "lg":
                    turned.brought_out(pe, n, ["xT0", "xT1"])
                    for t in range(NT):
                        for kc in range(2):
                            last = mm(gb[:, t * E:(t + 1) * E], xT[:, par, kc, t * P:(t + 1) * P], rw[:, kc, :],
                                      start=(kc == 0), stop=(kc == 1))
                elif item == "cT":
                    pe.wait_ge(s_route, n * ROUTE + 9)
                    for t in range(NT):
                        last = nc.tensor.transpose(gb[0:E, t * P:(t + 1) * P], coef[:, par, t, :], ident[:])
                elif item[0] == "b":
                    t = int(item[1])
                    if t == 0:
                        routed.brought_out(pe, n, ["cT"])
                    last = mm(gb[:, 0:C], coefT[:, par, t, :], eb[:], start=True, stop=True)
                elif item[0] == "y":
                    t, j = int(item[1]), int(item[3])
                    for kc in range(2):
                        last = mm(gb[:], xT[:, par, kc, t * P:(t + 1) * P], ew[:, kc, 2 * j:2 * j + 2, :],
                                  start=(kc == 0), stop=(kc == 1))
                if use:
                    use.filled(last, item)

            steps(pe, STEP, body)


def landmark_attention(nc, X, stats, ident, weights):
    with ExitStack() as ctx:
        sb = lambda name, shape, dt=fp32: ctx.enter_context(nc.sbuf_tensor("b_" + name, shape, dt))
        sem = lambda name: ctx.enter_context(nc.semaphore("b_" + name))

        M = 64
        HH, H8 = 2, 8
        NS = H // 2
        AW = M + HD
        ITERS = 6
        GROUPS = [(0, 4), (4, 8)]
        NA = NT * HH
        RING = 5

        wq, wp, hmask, bones = weights.tensors
        rstd = sb("rstd", [P, B * NT])
        mean = sb("mean", [P, B * NT])
        scr = sb("scr", [P, 4, B * NT])

        xn = sb("xn", [P, NT, C])
        xT = sb("xT", [P, 2, T])
        qT = sb("qT", [P, 2, HH, T])
        kT = sb("kT", [P, HH, T])
        vv = sb("vv", [P, NT, C])
        lsum = sb("lsum", [P, 4, M])
        klm = sb("klm", [P, HH, P])
        bdQ = sb("bdQ", [P, HH, H8, M])
        bdKl = sb("bdKl", [P, 2, HH, H8, M])
        k2 = sb("k2", [P, NS, M])
        k2max = sb("k2max", [P, NS])
        k2sum = sb("k2sum", [P, NS])
        bdK2 = sb("bdK2", [P, 2, NS, P])
        k2T = sb("k2T", [P, NS, P])
        dmax = sb("dmax", [P, NS])
        dinv = sb("dinv", [P, 2, NS])
        aw = sb("aw", [P, 2, NS, AW])
        abd = sb("abd", [P, 2, NS, P])
        rbd = sb("rbd", [P, NS, P])
        aw3 = sb("aw3", [P, NS, AW])
        uq = sb("uq", [P, NS, AW])
        tm = sb("tm", [P, NS, AW])
        zbd = sb("zbd", [P, NS, 2 * HD])
        nmax = sb("nmax", [P, NS])
        esum = sb("esum", [P, 2, NS])
        pc = sb("pc", [P, 2, T])
        p3T = sb("p3T", [P, 2, NT, P])
        amax = sb("amax", [P, RING, H8])
        asum = sb("asum", [P, RING, 2, H8])
        pa = sb("pa", [P, RING, T])
        p1T = sb("p1T", [P, NS, T])
        svT = sb("svT", [P, HH, T])

        bank = [ctx.enter_context(nc.psum_tensor(f"b_bank{i}", [P, 512], fp32)) for i in range(8)]
        EARLY, LATE, I = bank[0:4], bank[4:6], bank[6:8]

        PREP = ["xn", "xT0", "xT1", "q0", "k0", "q1", "k1", "v0", "v1", "S20", "S21"]
        SQUARE = [["e2"], [], ["m2"], [], [], ["kT0"], ["kT1"], ["d0"], ["d1"], ["A0"], ["A1"]]
        cunits = [[f"{kind}{k - lag}" for kind, lag in (("sc", 0), ("tc", 2), ("w", 3), ("ec", 0))
                   if 0 <= k - lag < NS] for k in range(NS + 3)]
        aunits = [[f"{kind}{k - lag}" for kind, lag in (("ta", 4), ("sa", 0), ("ea", 1), ("na", 2))
                   if 0 <= k - lag < NA] for k in range(NA + 4)]
        inverse = [f"{half}{i}.{gr}" for i in range(ITERS) for half in "RN" for gr in range(len(GROUPS))]
        LAST = ["Z", "sv0", "sv1"] + [f"pj{t}" for t in range(NT)]
        A_FROM = 8
        last_at = [0, 2, 3, 4, 5, 6, 7]
        STEP = []
        fill2 = [["xn"], []] + [[x] for x in PREP[1:]]
        for k, group in enumerate(cunits):
            fill2 += [group] + [x for x in SQUARE[k:k + 1] if x]
        for k, item in enumerate(inverse):
            STEP.append((1, item))
            if k in last_at:
                STEP.append((0, LAST[last_at.index(k)]))
            for m in range(k * len(fill2) // len(inverse), (k + 1) * len(fill2) // len(inverse)):
                STEP += [(2, x) for x in fill2[m]]
            if k >= A_FROM:
                span = len(inverse) - A_FROM
                lo, hi = (k - A_FROM) * len(aunits) // span, (k - A_FROM + 1) * len(aunits) // span
                STEP += [(1, x) for group in aunits[lo:hi] for x in group]

        s_zero, s_var, s_sqrt = sem("zeroed"), sem("variance"), sem("sqrt_done")
        s_xn = sem("xn_ready")
        s_lm = sem("landmark_steps")
        s_k2e = sem("kernel2_exp")
        s_k2 = sem("kernel2_steps")
        s_dinv = sem("dinv_ready")
        s_cmax = sem("kernel3_max")
        s_rinv = sem("kernel3_sum_inverse")
        s_amax = sem("kernel1_max")
        s_asub = sem("kernel1_shifted")
        s_aexp = sem("kernel1_exp")
        s_asum = sem("kernel1_sum_steps")
        s_norm = sem("kernel1_normalised")
        s_sq = sem("square_done")
        s_aw3 = sem("aw3_ready")
        s_rbd = sem("square_placed")
        s_tm = sem("tm_ready")
        s_pd = sem("product_done")
        s_aw = sem("aw_ready")

        def banks_used(ahead, names, banks, label):
            order = [x for a, x in STEP if a in ahead and x in names]
            return Uses(banks, [sem(f"{label}_full{i}") for i in range(len(banks))],
                        [sem(f"{label}_empty{i}") for i in range(len(banks))], order)

        early = banks_used((2,), [x for x in PREP + sum(SQUARE, []) if x not in ("xn", "e2", "m2")]
                           + [f"{k}{u}" for k in ("sc", "tc", "w") for u in range(NS)], EARLY, "early")
        late = banks_used((1,), [f"{k}{u}" for k in ("sa", "ta") for u in range(NA)], LATE, "late")
        late = Uses(late.banks, late.full, late.empty, late.names + LAST)

        def step(n, i, gr):
            return n * (ITERS * len(GROUPS)) + (i * len(GROUPS) + gr + 1)

        block = ctx.enter_context(nc.Block())

        @block.gpsimd
        def _(pool):
            for z in (bdK2, zbd, klm, rbd):
                nc.gpsimd.memset(z[:], 0.0).then_inc(s_zero, 1)
            pool.wait_ge(s_zero, 4)

            def heads(x):
                return x.rearrange("p (h m) -> p h m", m=M)

            def body(item, n, par):
                if item[:2] == "sa":
                    u = int(item[2:])
                    late.brought_out(pool, n, [item])
                    pool.wait_ge(s_amax, n * NA + (u + 1))
                    p = heads(pa[:, u % RING])
                    nc.gpsimd.tensor_tensor(out=p, in0=p, in1=amax[:, u % RING].unsqueeze(2).broadcast_to([P, H8, M]),
                                            op=ALU.subtract).then_inc(s_asub, 1)
                    pool.wait_ge(s_asub, n * NA + (u + 1))
                    pool.nop(nofuse=True)
                elif item[:2] == "na":
                    u = int(item[2:])
                    pool.wait_ge(s_asum, n * (2 * NA) + (2 * u + 2))
                    p = heads(pa[:, u % RING])
                    nc.gpsimd.tensor_tensor(out=p, in0=p,
                                            in1=asum[:, u % RING, 1].unsqueeze(2).broadcast_to([P, H8, M]),
                                            op=ALU.mult).then_inc(s_norm, 1)
                    pool.wait_ge(s_norm, n * NA + (u + 1))
                    pool.nop(nofuse=True)

            steps(pool, STEP, body)

        @block.vector
        def _(dve):
            V = nc.vector
            ln_rstd(nc, dve, stats, mean, rstd, scr, s_var, s_sqrt)
            dve.wait_ge(weights.loaded, weights.all)
            dve.wait_ge(s_zero, 4)
            LM = {"q0": 0, "k0": 2, "q1": 5, "k1": 7}

            def body(item, n, par):
                if item == "xn":
                    for t in range(NT):
                        tt = n * NT + t
                        V.tensor_scalar(xn[:, t, :], X[:, bass.ds(tt, 1), :], mean[:, bass.ds(tt, 1)],
                                        rstd[:, bass.ds(tt, 1)], ALU.subtract, ALU.mult).then_inc(s_xn, 1)
                elif item in LM:
                    isk, hh, lm = item[0] == "k", int(item[1]), LM[item]
                    src = kT[:, hh, :] if isk else qT[:, par, hh, :]
                    dst = bdKl[:, par, hh] if isk else bdQ[:, hh]
                    ls = lsum[:, 2 * isk + hh, :]
                    early.brought_out(dve, n, [item])
                    V.tensor_reduce(out=ls, in_=src.rearrange("p (m j) -> p m j", j=T // M), axis=AX.X,
                                    op=ALU.add).then_inc(s_lm, 1)
                    dve.wait_ge(s_lm, n * 10 + (lm + 1))
                    if isk:
                        V.tensor_scalar(klm[:, hh, 0:M], ls, M / T, None, ALU.mult).then_inc(s_lm, 1)
                    V.scalar_tensor_tensor(
                        out=dst, in0=ls.unsqueeze(1).broadcast_to([P, H8, M]), scalar=M / T,
                        in1=hmask[:].unsqueeze(2).broadcast_to([P, H8, M]),
                        op0=ALU.mult, op1=ALU.mult).then_inc(s_lm, 1)
                elif item in ("S20", "S21"):
                    j = int(item[2])
                    s2 = early.filled_bank(dve, n, item)[:].rearrange("p (s m) -> p s m", m=P)[:, :, 0:M]
                    mx = k2max[:, 4 * j:4 * j + 4]
                    V.tensor_reduce(out=mx, in_=s2, axis=AX.X, op=ALU.max).then_inc(s_k2, 1)
                    dve.wait_ge(s_k2, n * 6 + (j + 1))
                    early.emptied(V.tensor_tensor(out=k2[:, 4 * j:4 * j + 4], in0=s2,
                                                  in1=mx.unsqueeze(2).broadcast_to([P, 4, M]),
                                                  op=ALU.subtract), item)
                elif item == "m2":
                    dve.wait_ge(s_k2e, n + 1)
                    V.tensor_reduce(out=k2sum[:], in_=k2[:], axis=AX.X, op=ALU.add).then_inc(s_k2, 1)
                    dve.wait_ge(s_k2, n * 6 + 3)
                    V.reciprocal(k2max[:], k2sum[:]).then_inc(s_k2, 1)
                    dve.wait_ge(s_k2, n * 6 + 4)
                    for e in range(2):
                        r = slice(64 * e, 64 * e + 64)
                        V.tensor_tensor(out=bdK2[r, par, :, 64 * e:64 * e + 64], in0=k2[r],
                                        in1=k2max[r, :].unsqueeze(2).broadcast_to([64, NS, M]),
                                        op=ALU.mult).then_inc(s_k2, 1)
                elif item in ("d0", "d1"):
                    j = int(item[1])
                    gb = early.filled_bank(dve, n, item)
                    early.emptied(V.tensor_reduce(out=dmax[:, 4 * j:4 * j + 4],
                                                  in_=gb[:].rearrange("p (s m) -> p s m", m=P),
                                                  axis=AX.X, op=ALU.max), item)
                    if j == 1:
                        early.brought_out(dve, n, ["d0", "d1"])
                        V.reciprocal(dinv[:, par], dmax[:]).then_inc(s_dinv, 1)
                elif item in ("A0", "A1"):
                    j = int(item[1])
                    gb = early.filled_bank(dve, n, item)
                    dve.wait_ge(s_dinv, n + 1)
                    ss = slice(4 * j, 4 * j + 4)
                    g4 = gb[:].rearrange("p (s m) -> p s m", m=P)
                    for e in range(2):
                        r = slice(64 * e, 64 * e + 64)
                        V.tensor_tensor(out=aw[r, par, ss, 0:M], in0=g4[r, :, r],
                                        in1=dinv[r, par, ss].unsqueeze(2).broadcast_to([64, 4, M]), op=ALU.mult)
                    early.emptied(V.tensor_tensor(
                        out=abd[:, par, ss], in0=g4, in1=dinv[:, par, ss].unsqueeze(2).broadcast_to([P, 4, P]),
                        op=ALU.mult), item)
                elif item[:2] == "sc":
                    s = int(item[2:])
                    gb = early.filled_bank(dve, n, item)
                    V.tensor_reduce(out=nmax[:, s:s + 1], in_=gb[:], axis=AX.X, op=ALU.max,
                                    negate=True).then_inc(s_cmax, 1)
                elif item[0] == "w":
                    s = int(item[1:])
                    gb = early.filled_bank(dve, n, item)
                    V.reciprocal(esum[:, 1, s:s + 1], esum[:, 0, s:s + 1]).then_inc(s_rinv, 1)
                    dve.wait_ge(s_rinv, n * NS + (s + 1))
                    early.emptied(V.tensor_scalar(aw[:, par, s, M:AW], gb[:, 0:HD], esum[:, 1, s:s + 1], None,
                                                  ALU.mult), item)
                elif item[:2] == "sa":
                    u = int(item[2:])
                    gb = late.filled_bank(dve, n, item)
                    V.tensor_reduce(out=amax[:, u % RING], in_=gb[:].rearrange("p (h m) -> p h m", m=M),
                                    axis=AX.X, op=ALU.max).then_inc(s_amax, 1)
                elif item[:2] == "na":
                    u = int(item[2:])
                    dve.wait_ge(s_aexp, n * NA + (u + 1))
                    V.tensor_reduce(out=asum[:, u % RING, 0], in_=pa[:, u % RING].rearrange("p (h m) -> p h m", m=M),
                                    axis=AX.X, op=ALU.add).then_inc(s_asum, 1)
                    dve.wait_ge(s_asum, n * (2 * NA) + (2 * u + 1))
                    V.reciprocal(asum[:, u % RING, 1], asum[:, u % RING, 0]).then_inc(s_asum, 1)
                elif item[0] == "R":
                    i, gr = int(item[1]), int(item[3])
                    a, b = GROUPS[gr]
                    k = slice(0, AW) if i < ITERS - 1 else slice(M, AW)
                    dve.wait_ge(s_rbd, step(n, i, gr))
                    square = I[gr][:, 0:(b - a) * AW].rearrange("p (s m) -> p s m", m=AW)[:, :, k]
                    V.scalar_tensor_tensor(out=uq[:, a:b, k], in0=aw[:, par, a:b, k], scalar=7.0,
                                           in1=square, op0=ALU.mult, op1=ALU.subtract)
                    V.scalar_tensor_tensor(out=tm[:, a:b, k], in0=square, scalar=-3.75,
                                           in1=aw3[:, a:b, k], op0=ALU.mult, op1=ALU.add).then_inc(s_tm, 1)
                elif item[0] == "N":
                    i, gr = int(item[1]), int(item[3])
                    a, b = GROUPS[gr]
                    k = slice(0, AW) if i < ITERS - 1 else slice(M, AW)
                    dve.wait_ge(s_tm, step(n, i, gr))
                    dve.wait_ge(s_pd, step(n, i, gr))
                    prod = I[gr][:, 0:(b - a) * AW].rearrange("p (s m) -> p s m", m=AW)
                    last = V.tensor_tensor(out=aw[:, par, a:b, k], in0=prod[:, :, k], in1=tm[:, a:b, k], op=ALU.add)
                    if i < ITERS - 1:
                        for e in range(2):
                            r = slice(64 * e, 64 * e + 64)
                            last = V.tensor_tensor(out=abd[r, par, a:b, r], in0=prod[r, :, 0:M],
                                                   in1=tm[r, a:b, 0:M], op=ALU.add)
                    last.then_inc(s_aw, 1)
                elif item == "Z":
                    gb = late.filled_bank(dve, n, item)
                    for e in range(2):
                        r = slice(64 * e, 64 * e + 64)
                        last = V.tensor_tensor(
                            out=zbd[r, :, HD * e:HD * e + HD],
                            in0=gb[r, 0:NS * HD].rearrange("p (s d) -> p s d", d=HD),
                            in1=dinv[r, par].unsqueeze(2).broadcast_to([64, NS, HD]), op=ALU.mult)
                    late.emptied(last, item)
                elif item[:2] == "pj":
                    t = int(item[2:])
                    gb = late.filled_bank(dve, n, item)
                    x = X[:, bass.ds(n * NT + t, 1), :]
                    late.emptied(V.tensor_tensor(out=x, in0=x, in1=gb[:, 0:C].unsqueeze(1), op=ALU.add), item)
                    late.brought_out(dve, n, [item])
                    dve.nop(nofuse=True)
                    V.bn_stats(stats[:, bass.ds(n * NT + t, 1), :], x)

            steps(dve, STEP, body)

        @block.scalar
        def _(act):
            ln_sqrt(nc, act, scr, s_var, s_sqrt)
            A = nc.scalar.activation

            def body(item, n, par):
                if item in ("xT0", "xT1"):
                    early.emptied(A(xT[:, int(item[2]), :], early.filled_bank(act, n, item)[:], ACT.Copy), item)
                elif item in ("q0", "q1"):
                    early.emptied(A(qT[:, par, int(item[1]), :], early.filled_bank(act, n, item)[:], ACT.Copy,
                                    scale=float(HD) ** -0.5), item)
                elif item in ("k0", "k1"):
                    early.emptied(A(kT[:, int(item[1]), :], early.filled_bank(act, n, item)[:], ACT.Copy), item)
                elif item in ("v0", "v1"):
                    j = 2 * int(item[1])
                    early.emptied(A(vv[:, j:j + 2, :], early.filled_bank(act, n, item)[:]
                                    .rearrange("p (t c) -> p t c", t=2), ACT.Copy), item)
                elif item == "e2":
                    early.brought_out(act, n, ["S20", "S21"])
                    A(k2[:], k2[:], ACT.Exp).then_inc(s_k2e, 1)
                elif item in ("kT0", "kT1"):
                    j = 4 * int(item[2])
                    early.emptied(A(k2T[:, j:j + 4, :], early.filled_bank(act, n, item)[:]
                                    .rearrange("p (s m) -> p s m", m=P), ACT.Copy), item)
                elif item[:2] == "ec":
                    s = int(item[2:])
                    gb = early.filled_bank(act, n, f"sc{s}")
                    act.wait_ge(s_cmax, n * NS + (s + 1))
                    if s < 2:
                        b, k = early.at(f"tc{NS - 2 + s}")
                        wait_later(act, early.full[b], (n - 1) * early.per[b] + (k + 1))
                    else:
                        early.filled_bank(act, n, f"tc{s - 2}")
                    early.emptied(A(pc[:, s % 2], gb[:], ACT.Exp, bias=nmax[:, s:s + 1],
                                    accum_out=esum[:, 0, s:s + 1]), f"sc{s}")
                elif item[:2] == "tc":
                    s = int(item[2:])
                    gb = early.filled_bank(act, n, item)
                    early.emptied(A(p3T[:, s % 2], gb[:].rearrange("p (j q) -> p j q", j=4), ACT.Copy), item)
                elif item[:2] == "sa":
                    u = int(item[2:])
                    gb = late.filled_bank(act, n, item)
                    act.wait_ge(s_amax, n * NA + (u + 1))
                    if u >= RING:
                        late.filled_bank(act, n, f"ta{u - RING}")
                    else:
                        b, k = late.at(f"ta{NA - RING + u}")
                        wait_later(act, late.full[b], (n - 1) * late.per[b] + (k + 1))
                    late.emptied(A(pa[:, u % RING], gb[:], ACT.Copy), item)
                elif item[:2] == "ea":
                    u = int(item[2:])
                    act.wait_ge(s_asub, n * NA + (u + 1))
                    A(pa[:, u % RING], pa[:, u % RING], ACT.Exp).then_inc(s_aexp, 1)
                elif item[:2] == "ta":
                    t, hh = int(item[2:]) // 2, int(item[2:]) % 2
                    gb = late.filled_bank(act, n, item)
                    late.emptied(A(p1T[:, 4 * hh:4 * hh + 4, t * P:(t + 1) * P],
                                   gb[:].rearrange("p (j q) -> p j q", j=4), ACT.Copy), item)
                elif item[0] == "R":
                    i, gr = int(item[1]), int(item[3])
                    a, b = GROUPS[gr]
                    if i == 0 and gr == 0:
                        early.brought_out(act, n, ["A0", "A1"] + [f"w{s}" for s in range(NS)])
                    k = slice(0, AW) if i < ITERS - 1 else slice(M, AW)
                    if i > 0:
                        act.wait_ge(s_aw, step(n, i - 1, gr))
                    A(aw3[:, a:b, k], aw[:, par, a:b, k], ACT.Copy, scale=3.25).then_inc(s_aw3, 1)
                    act.wait_ge(s_sq, step(n, i, gr))
                    square = I[gr][:, 0:(b - a) * AW].rearrange("p (s m) -> p s m", m=AW)
                    for e in range(2):
                        r = slice(64 * e, 64 * e + 64)
                        last = A(rbd[r, a:b, r], square[r, :, 0:M], ACT.Copy, scale=0.25)
                    last.then_inc(s_rbd, 1)
                elif item[:2] == "sv":
                    late.emptied(A(svT[:, int(item[2]), :], late.filled_bank(act, n, item)[:], ACT.Copy), item)

            steps(act, STEP, body)

        @block.tensor
        def _(pe):
            mm = nc.tensor.matmul
            for sm in (*early.empty, *late.empty):
                pe.sem_inc(sm, 1)
            pe.wait_ge(weights.loaded, weights.all)
            pe.wait_ge(s_zero, 4)

            def body(item, n, par):
                use = early if item in early.names else late if item in late.names else None
                gb = use.claim(pe, n, item) if use else None
                last = None
                if item[:2] == "xT":
                    kc = int(item[2])
                    for t in range(NT):
                        if kc == 0:
                            pe.wait_ge(s_xn, n * NT + (t + 1))
                        last = nc.tensor.transpose(gb[:, t * P:(t + 1) * P], xn[:, t, kc * P:(kc + 1) * P], ident[:])
                elif item in ("q0", "q1", "k0", "k1"):
                    blk = 2 * (item[0] == "k") + int(item[1])
                    early.brought_out(pe, n, ["xT0", "xT1"], item)
                    for kc in range(2):
                        last = mm(gb[:], wq[:, kc, blk * P:(blk + 1) * P], xT[:, kc, :],
                                  start=(kc == 0), stop=(kc == 1))
                elif item in ("v0", "v1"):
                    for j in range(2):
                        t = 2 * int(item[1]) + j
                        for kc in range(2):
                            last = mm(gb[:, j * C:(j + 1) * C], xT[:, kc, t * P:(t + 1) * P],
                                      wq[:, kc, 2 * C:3 * C], start=(kc == 0), stop=(kc == 1))
                elif item in ("S20", "S21"):
                    hh = int(item[2])
                    pe.wait_ge(s_lm, (n + 1) * 10)
                    for j in range(4):
                        last = mm(gb[:, j * P:(j + 1) * P], bdQ[:, hh, 2 * j:2 * j + 2, :], klm[:, hh, :],
                                  start=True, stop=True)
                elif item in ("d0", "d1"):
                    j = int(item[1])
                    last = mm(gb[:], bones[:], bdK2[:, par, 4 * j:4 * j + 4, :], start=True, stop=True)
                elif item in ("kT0", "kT1"):
                    pe.wait_ge(s_k2, (n + 1) * 6)
                    for j in range(4):
                        s = 4 * int(item[2]) + j
                        last = nc.tensor.transpose(gb[:, j * P:(j + 1) * P], bdK2[:, par, s, :], ident[:])
                elif item in ("A0", "A1"):
                    early.brought_out(pe, n, [f"kT{item[1]}"], item)
                    for j in range(4):
                        s = 4 * int(item[1]) + j
                        last = mm(gb[:, j * P:(j + 1) * P], k2T[:, s, :], k2T[:, s, :], start=True, stop=True)
                elif item[:2] == "sc":
                    s = int(item[2:])
                    if s == 0:
                        pe.wait_ge(s_lm, (n + 1) * 10)
                    last = mm(gb[:], bdQ[:, s // 4, 2 * (s % 4):2 * (s % 4) + 2, :], kT[:, s // 4, :],
                              start=True, stop=True)
                elif item[:2] == "tc":
                    s = int(item[2:])
                    early.brought_out(pe, n, [f"sc{s}"], item)
                    for j in range(4):
                        last = nc.tensor.transpose(gb[:, j * P:(j + 1) * P], pc[:, s % 2, j * P:(j + 1) * P], ident[:])
                elif item[0] == "w":
                    s = int(item[1:])
                    early.brought_out(pe, n, [f"tc{s}"], item)
                    for t in range(NT):
                        for j in range(4):
                            hd = 2 * s + j // 2
                            last = mm(gb[32 * j:32 * j + 32, 0:HD], p3T[:, s % 2, t, 32 * j:32 * j + 32],
                                      vv[:, t, hd * HD:(hd + 1) * HD], start=(t == 0), stop=(t == NT - 1))
                elif item[:2] == "sa":
                    t, hh = int(item[2:]) // 2, int(item[2:]) % 2
                    last = mm(gb[:], qT[:, par, hh, t * P:(t + 1) * P], bdKl[:, par, hh], start=True, stop=True)
                elif item[:2] == "ta":
                    u = int(item[2:])
                    pe.wait_ge(s_norm, n * NA + (u + 1))
                    for j in range(4):
                        last = nc.tensor.transpose(gb[:, j * P:(j + 1) * P], pa[:, u % RING, j * P:(j + 1) * P],
                                                   ident[:])
                elif item[0] == "R":
                    i, gr = int(item[1]), int(item[3])
                    if i == 0 and gr == 0:
                        early.brought_out(pe, n, ["A0", "A1"] + [f"w{s}" for s in range(NS)])
                    if i > 0:
                        pe.wait_ge(s_aw, step(n, i - 1, gr))
                    a, b = GROUPS[gr]
                    for s in range(a, b):
                        last = mm(I[gr][:, (s - a) * AW:(s - a + 1) * AW], abd[:, par, s, :], aw[:, par, s, :],
                                  start=True, stop=True)
                    last.then_inc(s_sq, 1)
                elif item[0] == "N":
                    i, gr = int(item[1]), int(item[3])
                    a, b = GROUPS[gr]
                    pe.wait_ge(s_tm, step(n, i, gr))
                    for s in range(a, b):
                        if i < ITERS - 1:
                            last = mm(I[gr][:, (s - a) * AW:(s - a + 1) * AW], rbd[:, s, :], uq[:, s, :],
                                      start=True, stop=True)
                        else:
                            for j in range(4):
                                r = slice(32 * j, 32 * j + 32)
                                last = mm(I[gr][r, (s - a) * AW + M:(s - a + 1) * AW], rbd[:, s, r],
                                          uq[:, s, M:AW], start=True, stop=True)
                    last.then_inc(s_pd, 1)
                elif item == "Z":
                    pe.wait_ge(s_aw, step(n, ITERS - 1, len(GROUPS) - 1))
                    for s in range(NS):
                        for j in range(4):
                            r = slice(32 * j, 32 * j + 32)
                            last = mm(gb[r, s * HD:(s + 1) * HD], bdK2[:, par, s, r], aw[:, par, s, M:AW],
                                      start=True, stop=True)
                elif item[:2] == "sv":
                    hh = int(item[2])
                    late.brought_out(pe, n, ["Z", f"ta{NA - 1}", f"ta{NA - 2}"], item)
                    for j in range(4):
                        last = mm(gb[32 * j:32 * j + 32, :], zbd[:, 4 * hh + j, :], p1T[:, 4 * hh + j, :],
                                  start=True, stop=True)
                elif item[:2] == "pj":
                    t = int(item[2:])
                    late.brought_out(pe, n, ["sv0", "sv1"], item)
                    for hh in range(HH):
                        last = mm(gb[:, 0:C], svT[:, hh, t * P:(t + 1) * P], wp[:, hh, :],
                                  start=(hh == 0), stop=(hh == 1))
                if use:
                    use.filled(last, item)

            steps(pe, STEP, body)


class Weights:

    def __init__(self, nc, ctx, label, parts):
        self.tensors = [ctx.enter_context(nc.sbuf_tensor(f"{label}_{name}", shape, fp32)) for name, shape, _ in parts]
        self.loaded = ctx.enter_context(nc.semaphore(f"{label}_loaded"))
        self.loads = []
        for dst, (_, _, src) in zip(self.tensors, parts):
            if isinstance(src, list):
                self.loads += [(dst[:, i], s) for i, s in enumerate(src)]
            else:
                self.loads.append((dst[:], src))
        self.all = 16 * len(self.loads)

    def load(self, sp):
        for dst, src in self.loads:
            sp.dma_start(dst, src).then_inc(self.loaded, 16)


def expert_weights(nc, ctx, w):
    return Weights(nc, ctx, "experts", [
        ("router", [P, 2, E], w["r_wT"].rearrange("(k p) e -> p k e", p=P)),
        ("router_bias", [P, E], w["r_b"].partition_broadcast(P)),
        ("w", [P, 2, E, C], [w["e_wT"][:, kc * P:(kc + 1) * P, :].rearrange("e p o -> p e o") for kc in range(2)]),
        ("bias", [E, C], w["e_b"]), ("rank", [P, E], w["rank"])])


def landmark_weights(nc, ctx, w):
    return Weights(nc, ctx, "landmarks", [
        ("qkv", [P, 2, 3 * C], w["b_w_qkv"].rearrange("(k p) n -> p k n", p=P)),
        ("proj", [P, 2, C], w["b_w_proj"].rearrange("(k p) n -> p k n", p=P)),
        ("head_mask", [P, 8], w["headmask"]), ("block_ones", [P, P], w["blockones"])])


def begin(nc, x, X, ident, s_x):
    with ExitStack() as ctx:
        s_id = ctx.enter_context(nc.semaphore("identity"))
        block = ctx.enter_context(nc.Block())

        @block.sync
        def _(sp):
            xv = x.rearrange("b (t p) c -> b p t c", p=P)
            for b in range(B):
                sp.dma_start(X[:, b * NT:(b + 1) * NT, :], xv[b]).then_inc(s_x[b], 16)

        @block.gpsimd
        def _(pool):
            nc.gpsimd.memset(ident[:], 0.0).then_inc(s_id, 1)
            pool.wait_ge(s_id, 1)
            nc.gpsimd.affine_select(out=ident[:], in_=ident[:], compare_op=ALU.not_equal, fill=1.0, base=0,
                                    pattern=[[-1, P]], channel_multiplier=1).then_inc(s_id, 1)
            pool.wait_ge(s_id, 2)


def build(nc, w, out):
    with ExitStack() as ctx:
        X = ctx.enter_context(nc.sbuf_tensor("X", [P, B * NT, C], fp32))
        stats = ctx.enter_context(nc.sbuf_tensor("stats", [P, B * NT, 6], fp32))
        ident = ctx.enter_context(nc.sbuf_tensor("ident", [P, P], fp32))
        s_x = [ctx.enter_context(nc.semaphore(f"x_loaded{b}")) for b in range(B)]
        begin(nc, w["x"], X, ident, s_x)
        experts = expert_weights(nc, ctx, w)
        cluster_attention(nc, X, stats, ident, w, s_x, experts.load)
        landmarks = landmark_weights(nc, ctx, w)
        moe_ffn(nc, X, stats, ident, experts, 1, landmarks.load, None)
        landmark_attention(nc, X, stats, ident, landmarks)
        moe_ffn(nc, X, stats, ident, experts, 2, lambda sp: None, out)


def _tables():
    import math
    import numpy as np
    gs, ncl, per = 64, 64, 8
    pos = np.arange(ncl + gs, dtype=np.float32)[:, None]
    div = np.exp(np.arange(0, HD, 2, dtype=np.float32) * np.float32(-math.log(10000.0) / HD))
    ang = (pos * div).astype(np.float32)
    S = np.stack([np.sin(ang), np.cos(ang)], axis=-1).reshape(ncl + gs, HD).astype(np.float32)
    order = np.array([d // 2 + (HD // 2) * (d % 2) for d in range(HD)])
    R = S[:, order]
    dims = np.arange(P) % HD
    tabq = R[:gs][:, dims].T
    posk = (np.arange(T) // gs) * per + np.arange(T) % gs
    tabk = R[posk][:, dims].T
    tabc = R[:ncl][:, dims].T[:, None, :] * (np.arange(P)[:, None] // HD == np.arange(8)[None])[:, :, None]
    own16 = (np.arange(P)[:, None] // per == np.arange(32)[None]).astype(np.float32)
    row = np.arange(P)
    g = 2 * np.arange(NT)[None, :] + (row // gs)[:, None]
    col = np.arange(2 * gs)
    local = (col // gs)[None, :] == (row // gs)[:, None]
    seen = np.where(local[:, None, :], (col % gs)[None, None, :] <= (row % gs)[:, None, None],
                    (col % gs)[None, None, :] < (g * per)[:, :, None])
    maska = np.where(seen, 0.0, -1e30)
    f = lambda a: np.ascontiguousarray(a, dtype=np.float32)
    rank = np.broadcast_to(E - np.arange(E), (P, E))
    return {"rank": f(rank), "tabq": f(tabq), "tabk": f(tabk), "tabc": f(tabc), "own16": f(own16), "maska": f(maska),
            "headmask": f(np.arange(P)[:, None] // HD == np.arange(8)[None]),
            "blockones": f(np.arange(P)[:, None] // 64 == (np.arange(P)[None] // 64))}


def _layout(i):
    import numpy as np
    c = np.ascontiguousarray
    i = {k: np.asarray(v) for k, v in i.items()}
    return {"x": c(i["L0_attn_a_x"]),
            "a_w_attnT": c(i["L0_attn_a_w_attn"].T), "a_w_projT": c(i["L0_attn_a_w_proj"].T),
            "a_b_attn": c(i["L0_attn_a_b_attn"]), "a_bqk": c(i["L0_attn_a_b_attn"][:2 * C].reshape(4, P).T),
            "a_b_proj": c(i["L0_attn_a_b_proj"]), "a_w_assign": c(i["L0_attn_a_w_assign"].repeat(8, axis=0)),
            "b_w_qkv": c(i["L0_attn_b_w_qkv"]), "b_w_proj": c(i["L0_attn_b_w_proj"]),
            "r_wT": c(i["L0_ffn_router_w"].T), "r_b": c(i["L0_ffn_router_b"]),
            "e_wT": c(i["L0_ffn_expert_w"].transpose(0, 2, 1)), "e_b": c(i["L0_ffn_expert_b"])}


def kernel(**inputs):
    import concourse.bacc as bacc
    from concourse.bass_utils import run_bass_kernel_spmd as run
    nc = bacc.Bacc("TRN2", target_bir_lowering=False, num_devices=1)
    arrays = {**_layout(inputs), **_tables()}
    w = {n: nc.dram_tensor(f"in_{n}", a.shape, mybir.dt.from_np(a.dtype), kind="ExternalInput").ap()
         for n, a in arrays.items()}
    out = nc.dram_tensor("out", (B, T, C), fp32, kind="ExternalOutput").ap()
    build(nc, w, out)
    r = run(nc, [{f"in_{n}": a for n, a in arrays.items()}], core_ids=[0])
    return r.results[0]["out"]
```
